# Optimizing a Trainium2 kernel written in Bass

```python
import numpy as np
import jax
import jax.numpy as jnp

def _softmax(x, axis=-1):
    return jax.nn.softmax(x, axis=axis)

def _gelu(x):
    return jax.nn.gelu(x, approximate=True)

def _silu(x):
    return jax.nn.silu(x)

def _sigmoid(x):
    return jax.nn.sigmoid(x)

def _layernorm(x, axis=-1, eps=1e-05):
    m = jnp.mean(x, axis=axis, keepdims=True)
    v = jnp.var(x, axis=axis, keepdims=True)
    return (x - m) / jnp.sqrt(v + eps)

def _scatter_add(tgt, idx, src, axis=0):
    return tgt.at[idx].add(src)

def _segment_sum(src, seg, n):
    return jax.ops.segment_sum(src, seg, n)
kernel_name = 'mk_gps_d1_gnn_r32_d39d21'

def setup_inputs(seed: int=0):
    np.random.seed(seed)
    _w = jnp.asarray

    def _rec_inputs():
        import jax
        import jax.numpy as jnp
        _gk = jax.random.key(seed)
        x = -0.0002117 + 1 * jax.random.normal(jax.random.fold_in(_gk, 1), (3125, 256), jnp.float32)
        src = jax.random.randint(jax.random.fold_in(_gk, 2), (50000,), 0, 3125, jnp.int32)
        dst = jnp.minimum((3125 * jax.random.uniform(jax.random.fold_in(_gk, 3), (50000,)) ** 2.0).astype(jnp.int32), 99999)
        _o = jnp.argsort(dst, stable=True)
        src = src[_o]
        dst = dst[_o]
        edge_weight = jax.random.uniform(jax.random.fold_in(_gk, 12), (50000,), jnp.float32, 0.0, 1)
        return (x, src, dst, edge_weight)
    x, src, dst, edge_weight = _rec_inputs()

    def _L0_gnn_setup():
        import jax, jax.numpy as jnp
        import numpy as np
        N = 3125
        E = 100000
        D_IN = 256
        D_OUT = 256
        key = jax.random.key(seed)
        k = jax.random.split(key, 8)
        stdv = 1.0 / np.sqrt(D_OUT)
        x = jax.random.normal(k[0], (N, D_IN), dtype=jnp.float32)
        edge_row = jax.random.randint(k[1], (E,), 0, N, dtype=jnp.int32)
        edge_col = jax.random.randint(k[2], (E,), 0, N, dtype=jnp.int32)
        edge_val = jax.random.uniform(k[3], (E,), dtype=jnp.float32)
        weight_l = jax.random.uniform(k[4], (D_IN, D_OUT), minval=-stdv, maxval=stdv, dtype=jnp.float32)
        bias_l = jax.random.uniform(k[5], (D_OUT,), minval=-stdv, maxval=stdv, dtype=jnp.float32)
        weight_r = jax.random.uniform(k[6], (D_IN, D_OUT), minval=-stdv, maxval=stdv, dtype=jnp.float32)
        bias_r = jax.random.uniform(k[7], (D_OUT,), minval=-stdv, maxval=stdv, dtype=jnp.float32)
        return {'x': x, 'edge_row': edge_row, 'edge_col': edge_col, 'edge_val': edge_val, 'weight_l': weight_l, 'bias_l': bias_l, 'weight_r': weight_r, 'bias_r': bias_r}
    _L0_gnn_all = _L0_gnn_setup()
    _L0_gnn_in = {k: v for k, v in _L0_gnn_all.items() if k in ('weight_l', 'bias_l', 'weight_r', 'bias_r')}
    del _L0_gnn_all

    def _L0_mix_setup():
        import jax, jax.numpy as jnp
        import numpy as np
        import math
        EMBED = 256
        HEADS = 4
        HEAD_DIM = EMBED // HEADS
        OUT_DIM = 256
        LN_EPS = 1e-05

        def _qkv_init(key):
            spread = math.sqrt(3.0 / EMBED)
            gain, delta = (0.01, 0.01)
            w = jax.random.uniform(key, (EMBED, EMBED), minval=-spread, maxval=spread) * gain
            return w + delta * jnp.eye(EMBED, dtype=w.dtype)

        def _layer_norm(x, g, b):
            mu = jnp.mean(x, axis=-1, keepdims=True)
            var = jnp.mean(jnp.square(x - mu), axis=-1, keepdims=True)
            return (x - mu) * jax.lax.rsqrt(var + LN_EPS) * g + b

        def _split_heads(x, B, S):
            return x.reshape(B, S, HEADS, HEAD_DIM).transpose(0, 2, 1, 3)
        key = jax.random.key(seed)
        ks = jax.random.split(key, 6)
        seq = jax.random.normal(ks[0], (4, 256, EMBED), dtype=jnp.float32)
        wq = _qkv_init(ks[1])
        wk = _qkv_init(ks[2])
        wv = _qkv_init(ks[3])
        bound = 1.0 / math.sqrt(EMBED)
        wo = jax.random.uniform(ks[4], (OUT_DIM, EMBED), minval=-bound, maxval=bound)
        bo = jax.random.uniform(ks[5], (OUT_DIM,), minval=-bound, maxval=bound)
        ln_k_g = jnp.ones((HEAD_DIM,), jnp.float32)
        ln_k_b = jnp.zeros((HEAD_DIM,), jnp.float32)
        ln_v_g = jnp.ones((HEAD_DIM,), jnp.float32)
        ln_v_b = jnp.zeros((HEAD_DIM,), jnp.float32)
        return {'seq': seq, 'wq': wq, 'wk': wk, 'wv': wv, 'wo': wo, 'bo': bo, 'ln_k_g': ln_k_g, 'ln_k_b': ln_k_b, 'ln_v_g': ln_v_g, 'ln_v_b': ln_v_b}
    _L0_mix_all = _L0_mix_setup()
    _L0_mix_in = {k: v for k, v in _L0_mix_all.items() if k in ('wq', 'wk', 'wv', 'wo', 'bo', 'ln_k_g', 'ln_k_b', 'ln_v_g', 'ln_v_b')}
    del _L0_mix_all

    def _L0_ffn_setup():
        import jax, jax.numpy as jnp
        import numpy as np
        B, S, H, F, E, K = (8, 128, 256, 512, 16, 2)
        EPS = 1e-05
        key = jax.random.key(seed)
        ks = jax.random.split(key, 9)
        sc = 0.02
        return {'x': jax.random.normal(ks[0], (B, S, H), dtype=jnp.float32), 'gate_w': jax.random.normal(ks[1], (H, E), dtype=jnp.float32) * sc, 'gate_b': jnp.zeros((E,), dtype=jnp.float32), 'w1': jax.random.normal(ks[2], (E, H, F), dtype=jnp.float32) * sc, 'b1': jnp.zeros((E, F), dtype=jnp.float32), 'w2': jax.random.normal(ks[3], (E, F, H), dtype=jnp.float32) * sc, 'b2': jnp.zeros((E, H), dtype=jnp.float32), 'gamma': jnp.ones((H,), dtype=jnp.float32), 'beta': jnp.zeros((H,), dtype=jnp.float32)}
    _L0_ffn_all = _L0_ffn_setup()
    _L0_ffn_in = {k: v for k, v in _L0_ffn_all.items() if k in ('gate_w', 'gate_b', 'w1', 'b1', 'w2', 'b2', 'gamma', 'beta')}
    del _L0_ffn_all
    return {'x': x, 'src': src, 'dst': dst, 'edge_weight': edge_weight, 'L0_gnn_weight_l': _L0_gnn_in['weight_l'], 'L0_gnn_bias_l': _L0_gnn_in['bias_l'], 'L0_gnn_weight_r': _L0_gnn_in['weight_r'], 'L0_gnn_bias_r': _L0_gnn_in['bias_r'], 'L0_mix_wq': _L0_mix_in['wq'], 'L0_mix_wk': _L0_mix_in['wk'], 'L0_mix_wv': _L0_mix_in['wv'], 'L0_mix_wo': _L0_mix_in['wo'], 'L0_mix_bo': _L0_mix_in['bo'], 'L0_mix_ln_k_g': _L0_mix_in['ln_k_g'], 'L0_mix_ln_k_b': _L0_mix_in['ln_k_b'], 'L0_mix_ln_v_g': _L0_mix_in['ln_v_g'], 'L0_mix_ln_v_b': _L0_mix_in['ln_v_b'], 'L0_ffn_gate_w': _L0_ffn_in['gate_w'], 'L0_ffn_gate_b': _L0_ffn_in['gate_b'], 'L0_ffn_w1': _L0_ffn_in['w1'], 'L0_ffn_b1': _L0_ffn_in['b1'], 'L0_ffn_w2': _L0_ffn_in['w2'], 'L0_ffn_b2': _L0_ffn_in['b2'], 'L0_ffn_gamma': _L0_ffn_in['gamma'], 'L0_ffn_beta': _L0_ffn_in['beta']}

def reference(x, src, dst, edge_weight, L0_gnn_weight_l, L0_gnn_bias_l, L0_gnn_weight_r, L0_gnn_bias_r, L0_mix_wq, L0_mix_wk, L0_mix_wv, L0_mix_wo, L0_mix_bo, L0_mix_ln_k_g, L0_mix_ln_k_b, L0_mix_ln_v_g, L0_mix_ln_v_b, L0_ffn_gate_w, L0_ffn_gate_b, L0_ffn_w1, L0_ffn_b1, L0_ffn_w2, L0_ffn_b2, L0_ffn_gamma, L0_ffn_beta):
    import jax
    import jax.numpy as jnp

    def _L0_gnn_ref(x, edge_row, edge_col, edge_val, weight_l, bias_l, weight_r, bias_r):
        import jax, jax.numpy as jnp
        import numpy as np
        N = 3125
        E = 100000
        D_IN = 256
        D_OUT = 256
        h = x @ weight_l
        msgs = edge_val[:, None] * h[edge_col]
        agg = jax.ops.segment_sum(msgs, edge_row, num_segments=N)
        out = agg + bias_l
        out = out + x @ weight_r + bias_r
        return out

    def _L0_mix_ref(seq, wq, wk, wv, wo, bo, ln_k_g, ln_k_b, ln_v_g, ln_v_b):
        import jax, jax.numpy as jnp
        import numpy as np
        import math
        EMBED = 256
        HEADS = 4
        HEAD_DIM = EMBED // HEADS
        OUT_DIM = 256
        LN_EPS = 1e-05

        def _qkv_init(key):
            spread = math.sqrt(3.0 / EMBED)
            gain, delta = (0.01, 0.01)
            w = jax.random.uniform(key, (EMBED, EMBED), minval=-spread, maxval=spread) * gain
            return w + delta * jnp.eye(EMBED, dtype=w.dtype)

        def _layer_norm(x, g, b):
            mu = jnp.mean(x, axis=-1, keepdims=True)
            var = jnp.mean(jnp.square(x - mu), axis=-1, keepdims=True)
            return (x - mu) * jax.lax.rsqrt(var + LN_EPS) * g + b

        def _split_heads(x, B, S):
            return x.reshape(B, S, HEADS, HEAD_DIM).transpose(0, 2, 1, 3)
        B, S, _ = seq.shape
        q = _split_heads(seq @ wq.T, B, S)
        k = _split_heads(seq @ wk.T, B, S)
        v = _split_heads(seq @ wv.T, B, S)
        k = _layer_norm(k, ln_k_g, ln_k_b)
        v = _layer_norm(v, ln_v_g, ln_v_b)
        kv = jnp.einsum('bhsd,bhse->bhde', k, v) / S
        ga = jnp.einsum('bhsd,bhde->bhse', q, kv)
        ga = ga.transpose(0, 2, 1, 3).reshape(B, S, EMBED)
        return ga @ wo.T + bo

    def _L0_ffn_ref(x, gate_w, gate_b, w1, b1, w2, b2, gamma, beta):
        import jax, jax.numpy as jnp
        import numpy as np
        B, S, H, F, E, K = (8, 128, 256, 512, 16, 2)
        EPS = 1e-05
        gate_logits = x @ gate_w + gate_b
        topk_vals, topk_idx = jax.lax.top_k(gate_logits, K)
        topk_w = jax.nn.softmax(topk_vals, axis=-1)
        h = jax.nn.relu(jnp.einsum('bsh,ehf->bsef', x, w1) + b1)
        expert_out = jnp.einsum('bsef,efh->bseh', h, w2) + b2
        sel = jnp.take_along_axis(expert_out, topk_idx[:, :, :, None], axis=2)
        moe = jnp.sum(topk_w[..., None] * sel, axis=2)
        y = x + moe
        mu = jnp.mean(y, axis=-1, keepdims=True)
        var = jnp.var(y, axis=-1, keepdims=True)
        return (y - mu) / jnp.sqrt(var + EPS) * gamma + beta
    xn = _layernorm(x, axis=-1)
    x = x + _L0_gnn_ref(xn, src, dst, edge_weight, L0_gnn_weight_l, L0_gnn_bias_l, L0_gnn_weight_r, L0_gnn_bias_r) + _L0_mix_ref(xn[None], L0_mix_wq, L0_mix_wk, L0_mix_wv, L0_mix_wo, L0_mix_bo, L0_mix_ln_k_g, L0_mix_ln_k_b, L0_mix_ln_v_g, L0_mix_ln_v_b)[0]
    x = x + _L0_ffn_ref(_layernorm(x, axis=-1)[None], L0_ffn_gate_w, L0_ffn_gate_b, L0_ffn_w1, L0_ffn_b1, L0_ffn_w2, L0_ffn_b2, L0_ffn_gamma, L0_ffn_beta)[0]
    return x

_drawn_inputs = setup_inputs


def setup_inputs(seed=0):
    import zlib

    import numpy as np

    out = dict(_drawn_inputs(seed))
    spreads = {'L0_mix_ln_k_g': (1.0, 0.6),
     'L0_mix_ln_k_b': (0.0, 0.8),
     'L0_mix_ln_v_g': (1.0, 0.6),
     'L0_mix_ln_v_b': (0.0, 0.8),
     'L0_ffn_gate_b': (0.0, 0.314),
     'L0_ffn_b1': (0.0, 0.8),
     'L0_ffn_b2': (0.0, 0.302),
     'L0_ffn_gamma': (1.0, 0.2),
     'L0_ffn_beta': (0.0, 0.348)}
    factors = {'L0_mix_wq': 8.0,
     'L0_mix_wk': 8.0,
     'L0_mix_wv': 8.0,
     'L0_mix_wo': 8.0,
     'L0_gnn_bias_l': 4.271,
     'L0_gnn_bias_r': 4.359,
     'L0_mix_bo': 4.271,
     'L0_ffn_w1': 3.538}
    for name, (base, spread) in spreads.items():
        noise = np.random.default_rng([zlib.crc32(name.encode()), seed]).standard_normal(out[name].shape)
        drawn = base * np.exp(spread * noise) if base else spread * noise
        out[name] = jnp.asarray(drawn.astype(out[name].dtype))
    for name, factor in factors.items():
        out[name] = (out[name] * factor).astype(out[name].dtype)
    return out
```

```python
from contextlib import ExitStack

import numpy as np

import concourse.bass as bass
from concourse import mybir

ALU = mybir.AluOpType
ACT = mybir.ActivationFunctionType
AX_X = mybir.AxisListType.X
F32 = mybir.dt.float32
I32 = mybir.dt.int32
U32 = mybir.dt.uint32
BF16 = mybir.dt.bfloat16
FP16 = mybir.dt.float16

P = 128
N = 3125
D = 256
DC = D // P
NT = -(-N // P)
TAIL = N - (NT - 1) * P
HEAD = 64
NE = 16
FF = 512
FC = FF // P
EPS = 1e-5

E = 50000
EP = 125
EC = E // EP
SUP = 2
TC = EC // SUP
NC = (EP * TC + NT * (P - 1)) // P
GB = 11
NI = NC // GB
SB = TC // NI
LAG = 2
WS = 4
assert EP * EC == E and NI * GB == NC and NI * SB == TC and SB % 2 == 0

TB = 5
TI = NT // TB
CAP = 3328
DUMMY = NE * CAP
TRASH = DUMMY + P
ZROWS = TRASH + 2 * P
MT = (2 * N + NE * (P - 1)) // P
MT += MT % 2

K_ID, K_TRI, K_ONE, K_CEN, K_MSK, K_IOTA = 0, 128, 256, 384, 512, 640
K_CAP, K_VAL, K_TR, K_END = 896, 912, 912 + NT, 912 + NT + 2 * NT


def constant_table():
    p = np.arange(P)[:, None]
    q = np.arange(P)[None, :]
    same = p // HEAD == q // HEAD
    c = np.zeros((P, K_END), np.float32)
    c[:, K_ID:K_ID + P] = p == q
    c[:, K_TRI:K_TRI + P] = p < q
    c[:, K_ONE:K_ONE + P] = 1
    c[:, K_CEN:K_CEN + P] = (p == q) - same / HEAD
    c[:, K_MSK:K_MSK + P] = same
    c[:, K_IOTA:K_IOTA + 256] = np.arange(256)
    c[:, K_CAP:K_CAP + NE] = np.arange(NE) * CAP
    real = p + P * np.arange(NT)[None, :] < N
    c[:, K_VAL:K_VAL + NT] = real
    c[:, K_TR:K_TR + 2 * NT] = np.stack([(1 - real) * (TRASH + p), (1 - real) * (TRASH + P + p)], 2).reshape(P, 2 * NT)
    return c


class Arena:

    def __init__(self, tensor, words):
        self.tensor, self.words, self.at = tensor, words, 0

    def cut(self, shape, dt=F32):
        size = 2 if dt in (BF16, FP16) else 4
        n = int(np.prod(shape))
        words = -(-n * size // 4)
        assert self.at + words <= self.words, (self.at, words, self.words)
        v = self.tensor[:, self.at:self.at + words]
        self.at += words
        if dt != F32:
            v = v.bitcast(dt)
        v = v[:, 0:n]
        if len(shape) == 2:
            v = v.rearrange("p (a b) -> p a b", a=shape[0])
        elif len(shape) == 3:
            v = v.rearrange("p (a b c) -> p a b c", a=shape[0], b=shape[1])
        return v


def rounds(eng, n, body):
    body(0)
    with eng.Fori(1, n) as i:
        body(i)


def wait(eng, sem, value):
    if isinstance(value, int) and value <= 0:
        return
    eng.wait_ge(sem, value)


class Chain:

    def __init__(self, eng, sem):
        self.eng, self.sem, self.n, self.base = eng, sem, 0, 0

    def link(self, ins, apart=False):
        self.n += 1
        ins.then_inc(self.sem, 1)
        self.eng.wait_ge(self.sem, self.base + self.n)
        if apart:
            self.eng.nop(nofuse=True)

    def rounds(self, n, per, body):
        body(0)
        first = self.n
        with self.eng.Fori(1, n) as i:
            self.base, self.n = (i - 1) * per + first, 0
            body(i)
            assert self.n == per, (self.n, per)
        self.base, self.n = 0, first + (n - 1) * per


def chunked(w):
    return w.rearrange("(c p) n -> p c n", p=P)


class Phase:

    def __init__(self, nc, ctx, tag):
        self.nc, self.ctx, self.tag, self.used = nc, ctx, tag, []
        ctx.callback(self.clear)

    def sb(self, name, shape, dt=F32):
        return self.ctx.enter_context(self.nc.sbuf_tensor(name, [P] + shape, dt))

    def sem(self, name):
        self.used.append(self.nc.alloc_semaphore(f"{self.tag}_{name}"))
        return self.used[-1]

    def clear(self):
        for used in self.used:
            self.nc.gpsimd.sem_clear(used)
            self.nc.release_semaphore(used)

    def sems(self, name, n):
        return [self.sem(f"{name}{k}") for k in range(n)]


def load_constants(nc, m):
    with ExitStack() as ctx:
        ph = Phase(nc, ctx, "load")
        loaded, copied = ph.sem("constants_loaded"), ph.sem("constants_copied")
        block = ctx.enter_context(nc.Block())

        @block.sync
        def _(sp):
            sp.dma_start(m.C[:, :], m.consts).then_inc(loaded, 16)

        @block.vector
        def _(dve):
            nc.vector.memset(m.zero_h[:, :], 0.0).then_inc(copied, 1)
            dve.wait_ge(loaded, 16)
            nc.vector.tensor_copy(m.iota_h[:, :], m.iota).then_inc(copied, 1)
            dve.wait_ge(copied, 2)


def rank_edges(nc, m):
    with ExitStack() as ctx:
        ph = Phase(nc, ctx, "rank")
        a = Arena(m.W2, NE * FC * D)
        onehot, running = a.cut([NT, TC], BF16), a.cut([NT, TC])
        a = Arena(m.W1, NE * DC * FF)
        src_i, dst_i, t_i, u_i = (a.cut([EC], I32) for _ in range(4))
        ew_f, bucket = a.cut([EC]), a.cut([EC])
        ends, count, columns, base = a.cut([NT + 1]), a.cut([NT]), a.cut([NT]), a.cut([NT])
        cols_end = a.cut([SUP, NT])
        total_i, total_j = a.cut([NT], I32), a.cut([NT], I32)
        slot, slot_i, slot_j = a.cut([TC]), a.cut([TC], I32), a.cut([TC], I32)
        over, over_n = a.cut([NC, NT]), a.cut([NC])
        loaded, counted, summed, link = (ph.sem(n) for n in ("edges_loaded", "counted", "summed", "rank_link"))
        prefix, total = m.bank[0][:, 0:NT], m.bank[1][:, 0:NT]
        block = ctx.enter_context(nc.Block())

        @block.sync
        def _(sp):
            for to, of in ((src_i, m.src), (dst_i, m.dst), (ew_f, m.ew)):
                sp.dma_start(to[0:EP, :], of.rearrange("(p t) -> p t", p=EP)).then_inc(loaded, 16)

        @block.tensor
        def _(pe):
            for s in range(SUP):
                pe.wait_ge(counted, s + 1)
                nc.tensor.matmul(prefix[0:P, :], m.tri[0:EP, :], count[0:EP, :], start=True, stop=True)
                nc.tensor.matmul(total, m.ones[0:EP, :], count[0:EP, :], start=True, stop=True).then_inc(summed, 1)

        @block.vector
        def _(dve):
            c = Chain(dve, link)
            V = nc.vector
            e = slice(0, EP)
            dve.wait_ge(loaded, 48)
            c.link(V.tensor_scalar(t_i[e, :], dst_i[e, :], 2047, None, ALU.bitwise_and))
            c.link(V.tensor_copy(m.val[e, 0, :], t_i[e, :]))
            c.link(V.tensor_scalar(t_i[e, :], dst_i[e, :], 4, P, ALU.logical_shift_right, ALU.bitwise_and))
            c.link(V.tensor_scalar(u_i[e, :], src_i[e, :], P - 1, None, ALU.bitwise_and))
            c.link(V.tensor_tensor(t_i[e, :], t_i[e, :], u_i[e, :], ALU.bitwise_or))
            c.link(V.tensor_copy(m.val[e, 1, :], t_i[e, :]))
            c.link(V.tensor_copy(m.part_h[e, :], ew_f[e, :]))
            c.link(V.tensor_copy(m.val[e, 2, :], m.part_h[e, :]))
            c.link(V.tensor_tensor(ew_f[e, :], ew_f[e, :], m.val[e, 2, :], ALU.subtract))
            c.link(V.tensor_copy(m.part_h[e, :], ew_f[e, :]))
            c.link(V.tensor_copy(m.val[e, 3, :], m.part_h[e, :]))
            c.link(V.tensor_tensor(m.val[e, 4, :], ew_f[e, :], m.val[e, 3, :], ALU.subtract))
            c.link(V.tensor_scalar(t_i[e, :], src_i[e, :], 7, None, ALU.logical_shift_right))
            c.link(V.tensor_copy(bucket[e, :], t_i[e, :]))
            c.link(V.memset(ends[:, :], 0.0))
            for s in range(SUP):
                t = slice(s * TC, (s + 1) * TC)
                c.link(V.tensor_tensor(onehot[e, :, :], bucket[e, t].unsqueeze(1).to_broadcast([EP, NT, TC]),
                                       m.iota[e, 0:NT].unsqueeze(2).to_broadcast([EP, NT, TC]), ALU.is_equal))
                flat = onehot[e, :, :].rearrange("p b t -> p (b t)")
                c.link(V.tensor_tensor_scan(running[e, :, :].rearrange("p b t -> p (b t)"), flat, flat, 0.0,
                                            ALU.add, ALU.max))
                c.link(V.tensor_copy(ends[e, 1:NT + 1], running[e, :, TC - 1]))
                V.tensor_tensor(count[e, :], ends[e, 1:NT + 1], ends[e, 0:NT], ALU.subtract).then_inc(counted, 1)
                dve.wait_ge(summed, s + 1)
                c.link(V.tensor_scalar(total_i[:, :], total, float(P - 1), None, ALU.add))
                c.link(V.tensor_scalar(total_j[:, :], total_i[:, :], 7, None, ALU.logical_shift_right))
                c.link(V.tensor_copy(columns[:, :], total_j[:, :]))
                c.link(V.tensor_tensor_scan(cols_end[:, s, :], columns[:, :], columns[:, :], 0.0, ALU.add, ALU.max))
                c.link(V.tensor_tensor(base[e, :], cols_end[e, s, :], columns[e, :], ALU.subtract))
                c.link(V.scalar_tensor_tensor(base[e, :], base[e, :], float(P), prefix[e, :], ALU.mult, ALU.add))
                c.link(V.scalar_tensor_tensor(base[e, :], base[e, :], 1.0, ends[e, 0:NT], ALU.subtract, ALU.subtract))
                c.link(V.tensor_tensor(running[e, :, :], running[e, :, :],
                                       base[e, :].unsqueeze(2).to_broadcast([EP, NT, TC]), ALU.add))
                c.link(V.tensor_tensor(running[e, :, :], running[e, :, :], onehot[e, :, :], ALU.mult))
                c.link(V.tensor_reduce(slot[e, :], running[e, :, :].rearrange("p b t -> p t b"), AX_X, ALU.add))
                c.link(V.tensor_copy(slot_i[e, :], slot[e, :]))
                c.link(V.tensor_scalar(slot_j[e, :], slot_i[e, :], P - 1, None, ALU.bitwise_and))
                c.link(V.tensor_copy(m.row_of[e, t], slot_j[e, :]))
                c.link(V.tensor_scalar(slot_j[e, :], slot_i[e, :], 7, None, ALU.logical_shift_right))
                c.link(V.tensor_copy(m.col_of[e, t], slot_j[e, :]))
                c.link(V.tensor_tensor(over[0:1, :, :], cols_end[0:1, s, :].unsqueeze(1).to_broadcast([1, NC, NT]),
                                       m.iota[0:1, 0:NC].unsqueeze(2).to_broadcast([1, NC, NT]), ALU.is_le))
                c.link(V.tensor_reduce(over_n[0:1, :], over[0:1, :, :], AX_X, ALU.add))
                c.link(V.tensor_scalar(m.bucket_i[0:1, s, :], over_n[0:1, :], float(NT - 1), None, ALU.min))


def earlier(i, k, lag):
    k -= lag
    if k >= 0:
        return i, k
    return None if isinstance(i, int) and i == 0 else (i - 1, k + TB)


def since(k, slots):
    if k >= slots:
        return slots
    return TB - max(v for v in range(TB) if v % slots == k) + k


def node_stage(nc, m):
    with ExitStack() as ctx:
        ph = Phase(nc, ctx, "node")
        a = Arena(m.W1, NE * DC * FF)
        wl, wr = a.cut([DC, D]), a.cut([DC, D])
        wq, wk, wv, wo = (a.cut([DC, D]) for _ in range(4))
        wkv, woT, mixed, weff = a.cut([DC, 2 * D]), a.cut([DC, D]), a.cut([DC, D]), a.cut([DC, D])
        kvT, t1, t2 = a.cut([DC, P]), a.cut([DC, P]), a.cut([DC, P])
        kg, kb, vg, vb, vsum = a.cut([HEAD]), a.cut([HEAD]), a.cut([1]), a.cut([1]), a.cut([DC])
        biases, bias = a.cut([3, D]), a.cut([D])
        st6, mv, rstd = a.cut([NT, 6]), a.cut([NT, 2]), a.cut([NT])
        eps_x, eps_kv = a.cut([1]), a.cut([1])
        xn, xt, hs = a.cut([TB, D]), a.cut([TB, D]), a.cut([TB, D])
        squares, kv = a.cut([3, 2 * D]), a.cut([3, 2 * D])
        ssum, root, rs = a.cut([TB, 8]), a.cut([TB, 8]), a.cut([TB, 8])
        a = Arena(m.W2, NE * FC * D)
        xnT = a.cut([NT, D])
        b_t, b_h = (m.bank[0], m.bank[7]), (m.bank[1], m.bank[6])
        b_kv, b_acc, b_ks = m.bank[2:4], m.bank[4], m.bank[5]
        names = ("stats x_loaded w_loaded p_loaded cleared link prepared prep_read xn_ready xt_psum xt_ready xt_kept "
                 "var_ready rooted reduced kv_rooted h_psum h_ready kv_psum squared kv_ready kv_used kv_folded mixed_psum mixed_ready weff_psum "
                 "weff_ready bias_added bias_link again add_psum added")
        s = {n: ph.sem(n) for n in names.split()}
        h_stored = ph.sems("h_stored", TB)
        block = ctx.enter_context(nc.Block())

        @block.sync
        def _(sp):
            sp.wait_ge(s["cleared"], 1)
            per = TB * P
            for g in range(TI):
                rows = min(per, (N - g * per) // P * P)
                sp.dma_start(m.Y[:, g * TB:g * TB + rows // P, :],
                             m.x[g * per:g * per + rows, :].rearrange("(t p) d -> p t d", p=P)).then_inc(s["x_loaded"], 16)
            sp.dma_start(m.Y[0:TAIL, NT - 1, :], m.x[N - TAIL:N, :]).then_inc(s["x_loaded"], 16)
            for t in range(3):
                of = (m.bl, m.br, m.bo)[t]
                sp.dma_start(biases[:, t, :], of.unsqueeze(0).to_broadcast([P, D])).then_inc(s["p_loaded"], 16)

            def store(i, k):
                sp.wait_ge(s["h_ready"], i * TB + k + 1)
                sp.dma_start(m.h_table[bass.ds((i * TB + k) * P, P), :], hs[:, k, :]).then_inc(h_stored[k], 16)

            rounds(sp, TI, lambda i: [store(i, k) for k in range(TB)])
            for k in range(TB):
                sp.wait_ge(h_stored[k], 16 * TI)

        @block.gpsimd
        def _(pool):
            def keep(i, k):
                t = i * TB + k
                pool.wait_ge(s["xt_ready"], t + 1)
                nc.gpsimd.tensor_copy(xnT[:, bass.ds(t, 1), :], xt[:, k:k + 1, :]).then_inc(s["xt_kept"], 1)

            rounds(pool, TI, lambda i: [keep(i, k) for k in range(TB)])
            pool.wait_ge(s["p_loaded"], 16 * 9)
            nc.gpsimd.tensor_tensor(bias[:, :], biases[:, 0, :], biases[:, 1, :], ALU.add).then_inc(s["bias_link"], 1)
            pool.wait_ge(s["bias_link"], 1)
            nc.gpsimd.tensor_tensor(bias[:, :], bias[:, :], biases[:, 2, :], ALU.add).then_inc(s["bias_link"], 1)
            pool.wait_ge(s["bias_link"], 2)
            pool.wait_ge(s["xn_ready"], NT)
            nc.gpsimd.tensor_tensor(m.Y[:, :, :], m.Y[:, :, :], bias[:, :].unsqueeze(1).to_broadcast([P, NT, D]),
                                    ALU.add).then_inc(s["bias_added"], 1)

        @block.scalar
        def _(act):
            A = nc.scalar
            for to, of in ((wk, m.wk), (wv, m.wv), (wo, m.wo), (wl, m.wl), (wq, m.wq), (wr, m.wr)):
                act.dma_start(to[:, :, :], chunked(of)).then_inc(s["w_loaded"], 16)
            for to, of in ((kg, m.kg), (kb, m.kb)):
                act.dma_start(to[:, :], of.unsqueeze(0).to_broadcast([P, HEAD])).then_inc(s["p_loaded"], 16)
            for to, of in ((vg, m.vg), (vb, m.vb)):
                for half in range(2):
                    act.dma_start(to[half * HEAD:(half + 1) * HEAD, :], of.unsqueeze(1)).then_inc(s["p_loaded"], 16)
            act.wait_ge(s["var_ready"], 3)
            A.activation(rstd[:, :], mv[:, :, 1], ACT.Sqrt, bias=eps_x[:, :]).then_inc(s["rooted"], 1)
            act.wait_ge(s["prepared"], 1)
            A.copy(wkv[:, 0, :], m.bank[6][:, :]).then_inc(s["prep_read"], 1)
            A.copy(wkv[:, 1, :], m.bank[7][:, :]).then_inc(s["prep_read"], 1)
            A.copy(woT[:, :, :], m.bank[5][:, :].rearrange("p (c d) -> p c d", c=DC)).then_inc(s["prep_read"], 1)

            def copy_t(i, k):
                t = i * TB + k
                act.wait_ge(s["xt_psum"], t + 1)
                wait(act, s["kv_psum"], t - TB + 1)
                wait(act, s["xt_kept"], t - TB + 1)
                A.copy(xt[:, k, :], b_t[k % 2][:, 0:D]).then_inc(s["xt_ready"], 1)

            def copy_h(i, k):
                t = i * TB + k
                act.wait_ge(s["h_psum"], t + 1)
                wait(act, h_stored[k], i * 16)
                A.copy(hs[:, k, :], b_h[k % 2][:, 0:D]).then_inc(s["h_ready"], 1)
                act.wait_ge(s["kv_psum"], t + 1)
                wait(act, s["reduced"], t - since(k, 3) + 1)
                A.activation(squares[:, k % 3, :], b_kv[k % 2][:, :], ACT.Square).then_inc(s["squared"], 1)

            def root_kv(i, k):
                act.wait_ge(s["reduced"], i * TB + k + 1)
                A.activation(root[:, k, :], ssum[:, k, :], ACT.Sqrt, bias=eps_kv[:, :]).then_inc(s["kv_rooted"], 1)

            def body(i):
                for k in range(TB):
                    if before := earlier(i, k, 2):
                        root_kv(*before)
                    copy_t(i, k)
                    if before := earlier(i, k, 1):
                        copy_h(*before)

            rounds(act, TI, body)
            root_kv(TI - 1, TB - 2)
            copy_h(TI - 1, TB - 1)
            root_kv(TI - 1, TB - 1)

            act.wait_ge(s["mixed_psum"], 1)
            A.activation(mixed[:, :, :], m.bank[6][:, :].rearrange("p (c d) -> p c d", c=DC), ACT.Copy,
                         scale=1.0 / N).then_inc(s["mixed_ready"], 1)

            def again(i, k):
                t = i * TB + k
                act.wait_ge(s["kv_psum"], NT)
                wait(act, s["add_psum"], t - TB + 1)
                A.copy(xt[:, k:k + 1, :], xnT[:, bass.ds(t, 1), :]).then_inc(s["again"], 1)

            act.wait_ge(s["xt_kept"], NT)
            rounds(act, TI, lambda i: [again(i, k) for k in range(TB)])

        @block.tensor
        def _(pe):
            T = nc.tensor
            pe.wait_ge(s["w_loaded"], 16 * 6)
            for c in range(DC):
                for half, w in enumerate((wk, wv)):
                    for h in range(DC):
                        T.matmul(m.bank[6 + c][:, half * D + h * P:half * D + (h + 1) * P],
                                 w[:, h, c * P:(c + 1) * P], m.center, start=True, stop=True)
            for o in range(DC):
                for c in range(DC):
                    last = T.transpose(m.bank[5][:, c * D + o * P:c * D + (o + 1) * P], wo[:, o, c * P:(c + 1) * P], m.ident)
            last.then_inc(s["prepared"], 1)
            pe.wait_ge(s["prep_read"], 3)
            for b in (b_acc, b_ks):
                T.matmul(b[:, :], m.zero_h[:, 0:P], m.zero_h[:, :], start=True, stop=False)

            def turn(i, k):
                t = i * TB + k
                pe.wait_ge(s["xn_ready"], t + 1)
                wait(pe, s["xt_ready"], t - since(k, 2) + 1)
                for c in range(DC):
                    last = T.transpose(b_t[k % 2][:, c * P:(c + 1) * P], xn[:, k, c * P:(c + 1) * P], m.ident)
                last.then_inc(s["xt_psum"], 1)

            def project(i, k):
                t = i * TB + k
                pe.wait_ge(s["xt_ready"], t + 1)
                wait(pe, s["h_ready"], t - since(k, 2) + 1)
                for c in range(DC):
                    last = T.matmul(b_h[k % 2][:, 0:D], xt[:, k, c * P:(c + 1) * P], wl[:, c, :],
                                    start=(c == 0), stop=(c == DC - 1))
                last.then_inc(s["h_psum"], 1)
                wait(pe, s["kv_ready"], t - since(k, 2) + 1)
                for c in range(DC):
                    last = T.matmul(b_kv[k % 2][:, :], xt[:, k, c * P:(c + 1) * P], wkv[:, c, :],
                                    start=(c == 0), stop=(c == DC - 1))
                last.then_inc(s["kv_psum"], 1)

            def accumulate(i, k, rows=P):
                pe.wait_ge(s["kv_ready"], i * TB + k + 1)
                done = rows != P
                slot = kv[0:rows, k % 3, :]
                for c in range(DC):
                    v = slot[:, D + c * P:D + (c + 1) * P]
                    T.matmul(b_acc[:, c * P:(c + 1) * P], v, slot[:, c * P:(c + 1) * P], start=False, stop=False)
                    T.matmul(b_acc[:, D + c:D + c + 1], v, m.ones[0:rows, 0:1], start=False,
                             stop=done and c == DC - 1)
                T.matmul(b_ks[:, 0:D], m.ones[0:rows, :], slot[:, 0:D], start=False, stop=done).then_inc(s["kv_used"], 1)

            def body(i):
                for k in range(TB):
                    turn(i, k)
                    if before := earlier(i, k, 1):
                        project(*before)
                    if before := earlier(i, k, 2):
                        accumulate(*before)

            rounds(pe, TI, body)
            project(TI - 1, TB - 1)
            accumulate(TI - 1, TB - 2)
            accumulate(TI - 1, TB - 1, TAIL)
            pe.wait_ge(s["kv_folded"], 1)
            for c in range(DC):
                last = T.matmul(m.bank[6][:, c * D:(c + 1) * D], kvT[:, c, :], woT[:, c, :], start=True, stop=True)
            last.then_inc(s["mixed_psum"], 1)
            pe.wait_ge(s["mixed_ready"], 1)
            for o in range(DC):
                for c in range(DC):
                    last = T.matmul(m.bank[7][:, o * D:(o + 1) * D], wq[:, c, o * P:(o + 1) * P], mixed[:, c, :],
                                    start=(c == 0), stop=(c == DC - 1))
            last.then_inc(s["weff_psum"], 1)
            pe.wait_ge(s["weff_ready"], 1)

            def apply(i, k):
                t = i * TB + k
                pe.wait_ge(s["again"], t + 1)
                wait(pe, s["added"], t - since(k, 4) + 1)
                for c in range(DC):
                    last = T.matmul(m.bank[k % 4][:, 0:D], xt[:, k, c * P:(c + 1) * P], weff[:, c, :],
                                    start=(c == 0), stop=(c == DC - 1))
                last.then_inc(s["add_psum"], 1)

            rounds(pe, TI, lambda i: [apply(i, k) for k in range(TB)])

        @block.vector
        def _(dve):
            V = nc.vector
            c = Chain(dve, s["link"])
            V.memset(m.Y[:, NT - 1, :], 0.0).then_inc(s["cleared"], 1)
            dve.wait_ge(s["x_loaded"], 16 * (TI + 1))

            V.memset(eps_x[:, :], EPS).then_inc(s["var_ready"], 1)
            V.memset(eps_kv[:, :], HEAD * EPS).then_inc(s["var_ready"], 1)

            def stats(i, k):
                t = i * TB + k
                V.bn_stats(st6[:, bass.ds(t, 1), :].rearrange("p a d -> p (a d)"),
                           m.Y[:, bass.ds(t, 1), :].rearrange("p a d -> p (a d)")).then_inc(s["stats"], 1)

            rounds(dve, TI, lambda i: [stats(i, k) for k in range(TB)])
            dve.wait_ge(s["stats"], NT)
            for t in range(NT):
                last = V.bn_aggr(mv[:, t, :], st6[:, t, :])
            last.then_inc(s["var_ready"], 1)
            dve.wait_ge(s["rooted"], 1)
            c.link(V.reciprocal(rstd[:, :], rstd[:, :]))

            def normalise(i, k):
                t = i * TB + k
                wait(dve, s["xt_psum"], t - TB + 1)
                V.tensor_scalar(xn[:, k:k + 1, :], m.Y[:, bass.ds(t, 1), :], mv[:, bass.ds(t, 1), 0:1].rearrange("p a b -> p (a b)"),
                                rstd[:, bass.ds(t, 1)], ALU.subtract, ALU.mult).then_inc(s["xn_ready"], 1)

            def reduce_kv(i, k):
                dve.wait_ge(s["squared"], i * TB + k + 1)
                V.tensor_reduce(ssum[:, k, :], squares[:, k % 3, :].rearrange("p (h d) -> p h d", d=HEAD), AX_X,
                                ALU.add).then_inc(s["reduced"], 1)

            def scale_kv(i, k):
                t = i * TB + k
                dve.wait_ge(s["kv_rooted"], t + 1)
                c.link(V.reciprocal(rs[:, k, :], root[:, k, :]))
                wait(dve, s["kv_used"], t - since(k, 3) + 1)
                V.scalar_tensor_tensor(kv[:, k % 3, :].rearrange("p (h d) -> p h d", d=HEAD),
                                       b_kv[k % 2][:, :].rearrange("p (h d) -> p h d", d=HEAD), float(HEAD) ** 0.5,
                                       rs[:, k, :].unsqueeze(2).to_broadcast([P, 8, HEAD]),
                                       ALU.mult, ALU.mult).then_inc(s["kv_ready"], 1)

            def body(i):
                for k in range(TB):
                    normalise(i, k)
                    if before := earlier(i, k, 2):
                        scale_kv(*before)
                    if before := earlier(i, k, 1):
                        reduce_kv(*before)

            c.rounds(TI, TB, body)
            scale_kv(TI - 1, TB - 2)
            reduce_kv(TI - 1, TB - 1)
            scale_kv(TI - 1, TB - 1)

            dve.wait_ge(s["kv_used"], NT)
            dve.wait_ge(s["p_loaded"], 16 * 9)
            pair = lambda v: v.rearrange("p (h d) -> p h d", d=HEAD)
            kg2, kb2 = (v[:, :].unsqueeze(1).to_broadcast([P, 2, HEAD]) for v in (kg, kb))
            c.link(V.tensor_copy(vsum[:, :], b_acc[:, D:D + DC]))
            for h in range(DC):
                c.link(V.tensor_tensor(pair(t1[:, h, :]), pair(b_acc[:, h * P:(h + 1) * P]), kg2, ALU.mult))
                c.link(V.scalar_tensor_tensor(pair(t1[:, h, :]), kb2, vsum[:, h:h + 1], pair(t1[:, h, :]), ALU.mult, ALU.add))
                c.link(V.tensor_tensor(pair(t2[:, h, :]), pair(b_ks[:, h * P:(h + 1) * P]), kg2, ALU.mult))
                c.link(V.scalar_tensor_tensor(pair(t2[:, h, :]), kb2, float(N), pair(t2[:, h, :]), ALU.mult, ALU.add))
                c.link(V.tensor_scalar(t2[:, h, :], t2[:, h, :], vb[:, :], None, ALU.mult))
                c.link(V.scalar_tensor_tensor(t1[:, h, :], t1[:, h, :], vg[:, :], t2[:, h, :], ALU.mult, ALU.add))
                last = V.tensor_tensor(kvT[:, h, :], t1[:, h, :], m.mask, ALU.mult)
            last.then_inc(s["kv_folded"], 1)
            dve.wait_ge(s["weff_psum"], 1)
            V.tensor_tensor(weff[:, :, :], m.bank[7][:, :].rearrange("p (c d) -> p c d", c=DC), wr[:, :, :],
                            ALU.add).then_inc(s["weff_ready"], 1)
            dve.wait_ge(s["bias_added"], 1)

            def add(i, k):
                t = i * TB + k
                dve.wait_ge(s["add_psum"], t + 1)
                tile = m.Y[:, bass.ds(t, 1), :]
                V.tensor_tensor(tile, tile, m.bank[k % 4][:, 0:D].unsqueeze(1), ALU.add).then_inc(s["added"], 1)

            rounds(dve, TI, lambda i: [add(i, k) for k in range(TB)])
            dve.wait_ge(s["added"], NT)


def last_use(u, slots, per_round):
    if u >= slots:
        return slots
    return per_round - max(v for v in range(per_round) if v % slots == u) + u


def edge_stage(nc, m):
    with ExitStack() as ctx:
        ph = Phase(nc, ctx, "edge")
        target, place, weight = ph.sb("slot_target", [SUP, NC], I32), ph.sb("slot_place", [SUP, NC]), ph.sb("slot_weight", [SUP, NC])
        code, high = ph.sb("slot_code", [2, NC], I32), ph.sb("slot_high", [NC], I32)
        columns, rows = ph.sb("onehot_col", [2, NC], BF16), ph.sb("onehot_row_value", [2, 5, P], FP16)
        rows_b = ph.sb("onehot_row_part", [2, 3, P], BF16)
        spread, fetched = ph.sb("spread", [WS, P]), ph.sb("fetched", [GB, D])
        index = ph.sb("fetch_index", [GB], I32)
        names = "opened placed shown closed table link spread_ready added w1_in w2_in"
        s = {n: ph.sem(n) for n in names.split()}
        staged, landed, used = ph.sems("staged", GB), ph.sems("landed", GB), ph.sems("used", GB)
        place_of = [m.bank[j // 2][:, (j % 2) * 256:(j % 2) * 256 + NC] for j in range(5)]
        b_add = m.bank[4:8]
        block = ctx.enter_context(nc.Block())

        @block.sync
        def _(sp):
            for e in range(NE):
                sp.dma_start(m.w1_sb[:, e, :, :], m.w1[e].rearrange("(c p) f -> p c f", p=P)).then_inc(s["w1_in"], 16)
            for e in range(NE):
                sp.dma_start(m.w2_sb[:, e, :, :], m.w2[e].rearrange("(c p) d -> p c d", p=P)).then_inc(s["w2_in"], 16)
            sp.wait_ge(s["w1_in"], 16 * NE)
            sp.wait_ge(s["w2_in"], 16 * NE)

        @block.gpsimd
        def _(pool):
            with pool.Fori(1, SUP * NI + 1) as v:
                for u in range(GB):
                    pool.wait_ge(s["table"], 1)
                    pool.wait_ge(staged[u], v)
                    nc.gpsimd.indirect_dma_start(fetched[:, u, :], None, m.h_table,
                                                 bass.IndirectOffsetOnAxis(ap=index[:, u:u + 1], axis=0)).then_inc(landed[u], 16)

        @block.scalar
        def _(act):
            for part in range(SUP):
                act.wait_ge(s["table"], part + 1)

                def stage(i, part=part):
                    for u in range(GB):
                        wait(act, used[u], part * NI + i)
                        nc.scalar.copy(index[:, u:u + 1], target[:, part, bass.ds(i * GB + u, 1)]).then_inc(staged[u], 1)

                rounds(act, NI, stage)

        @block.tensor
        def _(pe):
            T = nc.tensor

            def zero(start, stop):
                for b, width in ((0, 512), (1, 512), (2, NC)):
                    last = T.matmul(m.bank[b][:, 0:width], m.zero_h[:, 0:P], m.zero_h[:, 0:width], start=start, stop=stop)
                return last

            def place_column(part, i, n):
                t = part * TC + i * SB + n
                pe.wait_ge(s["shown"], t + 1)
                for j in range(5):
                    row = rows[0:EP, n % 2, j, :] if j < 2 else rows_b[0:EP, n % 2, j - 2, :]
                    last = T.matmul(place_of[j], row, columns[0:EP, n % 2, :], start=False, stop=False)
                last.then_inc(s["placed"], 1)

            def spread_column(part, i, u):
                g = part * NC + i * GB + u
                pe.wait_ge(landed[u], (part * NI + i + 1) * 16)
                pe.wait_ge(s["spread_ready"], g + 1)
                wait(pe, s["added"], g - last_use(u, 4, GB) + 1)
                T.matmul(b_add[u % 4][:, 0:D], spread[:, u % WS, :], fetched[:, u, :], start=True,
                         stop=True).then_inc(used[u], 1)

            zero(True, False)
            rounds(pe, NI, lambda i: [place_column(0, i, n) for n in range(SB)])
            zero(False, True).then_inc(s["closed"], 1)
            for part in range(SUP):
                more = part + 1 < SUP
                if more:
                    pe.wait_ge(s["table"], part + 1)
                    zero(True, False)

                def body(i, part=part, more=more):
                    for u in range(GB):
                        if more and u < SB:
                            place_column(part + 1, i, u)
                        spread_column(part, i, u)

                rounds(pe, NI, body)
                if more:
                    zero(False, True).then_inc(s["closed"], 1)

        @block.vector
        def _(dve):
            V = nc.vector
            c = Chain(dve, s["link"])
            e = slice(0, EP)

            def show_column(part, i, n):
                t = part * TC + i * SB + n
                b = n % 2
                wait(dve, s["placed"], t - 1)
                at = bass.ds(part * TC + i * SB + n, 1)
                V.tensor_scalar(columns[e, b, :], m.iota_h[e, 0:NC], m.col_of[e, at], None, ALU.is_equal)
                for j in range(5):
                    to = rows[e, b, j, :] if j < 2 else rows_b[e, b, j - 2, :]
                    last = V.tensor_scalar(to, m.iota_h[e, 0:P], m.row_of[e, at],
                                           m.val[e, j, at], ALU.is_equal, ALU.mult)
                last.then_inc(s["shown"], 1)

            def read_table(part):
                dve.wait_ge(s["closed"], part + 1)
                for j in range(2):
                    c.link(V.tensor_copy(code[:, j, :], place_of[j]))
                c.link(V.tensor_scalar(high[:, :], code[:, 1, :], P, 4, ALU.bitwise_and, ALU.logical_shift_left))
                c.link(V.tensor_tensor(target[:, part, :], code[:, 0, :], high[:, :], ALU.bitwise_or))
                c.link(V.tensor_scalar(high[:, :], code[:, 1, :], P - 1, None, ALU.bitwise_and))
                c.link(V.tensor_copy(place[:, part, :], high[:, :]))
                c.link(V.tensor_copy(weight[:, part, :], place_of[2]))
                for j in (3, 4):
                    last = V.tensor_tensor(weight[:, part, :], weight[:, part, :], place_of[j], ALU.add)
                    if j == 3:
                        c.link(last)
                last.then_inc(s["table"], 1)
                dve.wait_ge(s["table"], part + 1)

            def spread_weights(part, i, u):
                back = last_use(u, WS, GB)
                v, r = (u - back, i) if u >= back else (u - back + GB, i - 1)
                wait(dve, used[v], part * NI + r + 1 if part or not (isinstance(i, int) and r < 0) else 0)
                at = bass.ds(i * GB + u, 1)
                V.tensor_scalar(spread[:, u % WS, :], m.iota[:, 0:P], place[:, part, at], weight[:, part, at],
                                ALU.is_equal, ALU.mult).then_inc(s["spread_ready"], 1)

            def add(part, i, u):
                g = part * NC + i * GB + u
                bucket = dve.value_load(m.bucket_i[0:1, part, bass.ds(i * GB + u, 1)], min_val=0, max_val=NT - 1)
                dve.wait_ge(used[u], part * NI + i + 1)
                wait(dve, s["added"], g)
                tile = m.Y[:, bass.ds(bucket, 1), :]
                V.tensor_tensor(tile, tile, b_add[u % 4][:, 0:D].unsqueeze(1), ALU.add).then_inc(s["added"], 1)

            rounds(dve, NI, lambda i: [show_column(0, i, n) for n in range(SB)])
            read_table(0)
            for part in range(SUP):

                def body(i, part=part):
                    for u in range(GB):
                        if part + 1 < SUP and u < SB:
                            show_column(part + 1, i, u)
                        spread_weights(part, i, u)
                        if u >= LAG:
                            add(part, i, u - LAG)
                    for u in range(GB - LAG, GB):
                        add(part, i, u)

                rounds(dve, NI, body)
                if part + 1 < SUP:
                    read_table(part + 1)
            dve.wait_ge(s["added"], SUP * NC)


def route_stage(nc, m):
    with ExitStack() as ctx:
        ph = Phase(nc, ctx, "route")
        gate, gate_b = ph.sb("gate_w", [DC, NE]), ph.sb("gate_b", [NE])
        st6, mv, rstd, eps = ph.sb("rt_stats", [NT, 6]), ph.sb("rt_mean_var", [NT, 2]), ph.sb("rt_rstd", [NT]), ph.sb("rt_eps", [1])
        zs, zT = ph.sb("z_slots", [TB, D]), ph.sb("zT_slots", [2, D])
        logit, top, top_at, top_f = ph.sb("logits", [NE]), ph.sb("top8", [8]), ph.sb("top8_at", [8], U32), ph.sb("top_f", [2])
        both, seen = ph.sb("both_onehots", [TB, NE]), ph.sb("seen", [NE])
        pos, pick, row_i = ph.sb("positions", [NE]), ph.sb("picked", [2, NE]), ph.sb("scatter_row", [TB, 2], I32)
        b1_rows, zeros = ph.sb("b1_rows", [P]), ph.sb("zeros", [D])
        n_i, n_j, n_f, tiles = ph.sb("n_i", [NE], I32), ph.sb("n_j", [NE], I32), ph.sb("n_f", [NE]), ph.sb("tiles", [NE])
        tile_end, shift = ph.sb("tile_end", [NE]), ph.sb("region_shift", [NE])
        over, ex_f, row_f, valid = ph.sb("over", [MT, NE]), ph.sb("expert_f", [MT]), ph.sb("row_f", [MT]), ph.sb("valid", [MT])
        pad_i = ph.sb("pad_row", [NE], I32)
        fid, ex2 = ph.sb("fetch_f", [NT, 2]), ph.sb("exp_gap", [NT])
        picked2 = over[:, 0:2 * NT, :]
        names = ("params stats var_ready rooted link cleared z_ready zT_psum zT_ready z_kept logit_psum both_ready "
                 "rank_psum seen_ready b1_psum counts_ready counts pads_ready pads gap_ready gap_exp")
        s = {n: ph.sem(n) for n in names.split()}
        row_ready, scattered = ph.sems("row_ready", TB), ph.sems("scattered", TB)
        b_t, b_l, b_r, b_b, b_n = m.bank[0:2], m.bank[2:4], m.bank[4:6], m.bank[6], m.bank[7]
        block = ctx.enter_context(nc.Block())

        @block.sync
        def _(sp):
            sp.dma_start(gate[:, :, :], m.gate_w.rearrange("(c p) e -> p c e", p=P)).then_inc(s["params"], 16)
            sp.dma_start(gate_b[:, :], m.gate_b.unsqueeze(0).to_broadcast([P, NE])).then_inc(s["params"], 16)
            sp.dma_start(b1_rows[0:NE * FC, :], m.b1.rearrange("e (c f) -> (e c) f", f=P)).then_inc(s["params"], 16)
            sp.dma_start(m.b2_rows[0:NE, :], m.b2).then_inc(s["params"], 16)
            sp.dma_start(m.gamma_b[:, :], m.gamma.unsqueeze(0).to_broadcast([P, D])).then_inc(s["params"], 16)
            sp.dma_start(m.beta_b[:, :], m.beta.unsqueeze(0).to_broadcast([P, D])).then_inc(s["params"], 16)
            sp.wait_ge(s["cleared"], 1)
            sp.dma_start(m.routed[DUMMY:DUMMY + P, :], zeros[:, :]).then_inc(s["pads"], 16)
            sp.wait_ge(s["pads_ready"], 1)
            for e in range(NE):
                row = sp.value_load(pad_i[0:1, e:e + 1], min_val=0, max_val=DUMMY - P)
                sp.dma_start(m.routed[bass.ds(row, P), :], zeros[:, :]).then_inc(s["pads"], 16)
            sp.wait_ge(s["pads"], 16 * (NE + 1))
            sp.wait_ge(s["params"], 16 * 6)

        @block.gpsimd
        def _(pool):
            with pool.Fori(1, TI + 1) as v:
                for k in range(TB):
                    for r in range(2):
                        pool.wait_ge(s["cleared"], 1)
                        pool.wait_ge(row_ready[k], v)
                        nc.gpsimd.indirect_dma_start(m.routed, bass.IndirectOffsetOnAxis(ap=row_i[:, k, r:r + 1], axis=0),
                                                     zs[:, k, :], None).then_inc(scattered[k], 16)
            for k in range(TB):
                pool.wait_ge(scattered[k], 32 * TI)

        @block.scalar
        def _(act):
            A = nc.scalar
            act.wait_ge(s["var_ready"], 2)
            A.activation(rstd[:, :], mv[:, :, 1], ACT.Sqrt, bias=eps[:, :]).then_inc(s["rooted"], 1)

            def copies(i, k):
                t = i * TB + k
                act.wait_ge(s["zT_psum"], t + 1)
                wait(act, s["logit_psum"], t - last_use(k, 2, TB) + 1)
                A.copy(zT[:, k % 2, :], b_t[k % 2][:, 0:D]).then_inc(s["zT_ready"], 1)
                A.copy(m.Z[:, bass.ds(t, 1), :], zs[:, k:k + 1, :]).then_inc(s["z_kept"], 1)

            rounds(act, TI, lambda i: [copies(i, k) for k in range(TB)])
            act.wait_ge(s["b1_psum"], 1)
            A.copy(m.b1_cols[:, :], b_b[:, 0:NE * FC]).then_inc(s["z_kept"], 1)
            act.wait_ge(s["gap_ready"], 1)
            A.activation(ex2[:, :], m.share[:, :, 1], ACT.Exp).then_inc(s["gap_exp"], 1)

        @block.tensor
        def _(pe):
            T = nc.tensor
            pe.wait_ge(s["params"], 16 * 6)
            T.transpose(b_b[:, 0:NE * FC], b1_rows[0:NE * FC, :], m.ident[0:NE * FC, 0:NE * FC]).then_inc(s["b1_psum"], 1)

            def turn(i, k):
                t = i * TB + k
                pe.wait_ge(s["z_ready"], t + 1)
                wait(pe, s["zT_ready"], t - last_use(k, 2, TB) + 1)
                for c in range(DC):
                    last = T.transpose(b_t[k % 2][:, c * P:(c + 1) * P], zs[:, k, c * P:(c + 1) * P], m.ident)
                last.then_inc(s["zT_psum"], 1)

            def logits(i, k):
                t = i * TB + k
                pe.wait_ge(s["zT_ready"], t + 1)
                wait(pe, s["both_ready"], t - last_use(k, 2, TB) + 1)
                for c in range(DC):
                    last = T.matmul(b_l[k % 2][:, 0:NE], zT[:, k % 2, c * P:(c + 1) * P], gate[:, c, :],
                                    start=(c == 0), stop=(c == DC - 1))
                last.then_inc(s["logit_psum"], 1)

            def rank(i, k):
                t = i * TB + k
                pe.wait_ge(s["both_ready"], t + 1)
                pe.wait_ge(s["seen_ready"], t + 1)
                T.matmul(b_r[k % 2][:, 0:NE], m.tri, both[:, k, :], start=True, stop=False)
                T.matmul(b_r[k % 2][:, 0:NE], m.ones, seen[:, :], start=False, stop=True).then_inc(s["rank_psum"], 1)

            def body(i):
                for k in range(TB):
                    turn(i, k)
                    if before := earlier(i, k, 1):
                        logits(*before)
                    if before := earlier(i, k, 2):
                        rank(*before)

            rounds(pe, TI, body)
            logits(TI - 1, TB - 1)
            rank(TI - 1, TB - 2)
            rank(TI - 1, TB - 1)
            pe.wait_ge(s["seen_ready"], NT + 1)
            T.matmul(b_n[:, 0:NE], m.ones, seen[:, :], start=True, stop=True).then_inc(s["counts"], 1)

        @block.vector
        def _(dve):
            V = nc.vector
            c = Chain(dve, s["link"])
            V.memset(zeros[:, :], 0.0).then_inc(s["cleared"], 1)
            V.memset(eps[:, :], EPS).then_inc(s["var_ready"], 1)
            V.memset(seen[:, :], 0.0).then_inc(s["seen_ready"], 1)

            def stats(i, k):
                at = bass.ds(i * TB + k, 1)
                V.bn_stats(st6[:, at, :].rearrange("p a d -> p (a d)"),
                           m.Y[:, at, :].rearrange("p a d -> p (a d)")).then_inc(s["stats"], 1)

            rounds(dve, TI, lambda i: [stats(i, k) for k in range(TB)])
            dve.wait_ge(s["stats"], NT)
            for t in range(NT):
                last = V.bn_aggr(mv[:, t, :], st6[:, t, :])
            last.then_inc(s["var_ready"], 1)
            dve.wait_ge(s["rooted"], 1)
            c.link(V.reciprocal(rstd[:, :], rstd[:, :]))
            dve.wait_ge(s["params"], 16 * 6)

            def normalise(i, k):
                t = i * TB + k
                at = bass.ds(t, 1)
                wait(dve, s["zT_psum"], t - TB + 1)
                wait(dve, s["z_kept"], t - TB + 1)
                wait(dve, scattered[k], i * 32)
                V.tensor_scalar(zs[:, k:k + 1, :], m.Y[:, at, :], mv[:, at, 0:1].rearrange("p a b -> p (a b)"),
                                rstd[:, at], ALU.subtract, ALU.mult).then_inc(s["z_ready"], 1)

            def choose(i, k):
                t = i * TB + k
                dve.wait_ge(s["logit_psum"], t + 1)
                c.link(V.tensor_tensor(logit[:, :], b_l[k % 2][:, 0:NE], gate_b[:, :], ALU.add), apart=True)
                c.link(V.max(top[:, :], logit[:, :]), apart=True)
                V.tensor_copy(m.share[:, bass.ds(t, 1), :], top[:, 0:2].unsqueeze(1))
                c.link(V.max_index(top_at[:, :], top[:, :], logit[:, :]))
                c.link(V.tensor_copy(top_f[:, :], top_at[:, 0:2]))
                real = m.C[:, bass.ds(t + K_VAL, 1)]
                for r in range(2):
                    last = V.tensor_scalar(m.chosen[:, bass.ds(t, 1), r:r + 1, :].rearrange("p a b e -> p (a b) e"),
                                           m.iota[:, 0:NE].unsqueeze(1), top_f[:, r:r + 1], real, ALU.is_equal, ALU.mult)
                c.link(last)
                pair = m.chosen[:, bass.ds(t, 1), :, :]
                V.tensor_tensor(both[:, k:k + 1, :], pair[:, :, 0, :], pair[:, :, 1, :], ALU.add).then_inc(s["both_ready"], 1)

            def place(i, k):
                t = i * TB + k
                dve.wait_ge(s["rank_psum"], t + 1)
                dve.wait_ge(s["both_ready"], t + 1)
                c.link(V.tensor_tensor(pos[:, :], b_r[k % 2][:, 0:NE], m.C[:, K_CAP:K_CAP + NE], ALU.add))
                V.tensor_tensor(seen[:, :], seen[:, :], both[:, k, :], ALU.add).then_inc(s["seen_ready"], 1)
                pair = m.chosen[:, bass.ds(t, 1), :, :].rearrange("p a r e -> p (a r) e")
                c.link(V.tensor_tensor(pick[:, :, :], pair, pos[:, :].unsqueeze(1).to_broadcast([P, 2, NE]), ALU.mult))
                row = m.row_f[:, bass.ds(t, 1), :].rearrange("p a r -> p (a r)")
                c.link(V.tensor_reduce(row, pick[:, :, :], AX_X, ALU.add))
                wait(dve, scattered[k], i * 32)
                V.tensor_tensor(row_i[:, k, :], row, m.C[:, bass.ds(t * 2 + K_TR, 2)], ALU.add).then_inc(row_ready[k], 1)

            def body(i):
                for k in range(TB):
                    normalise(i, k)
                    if before := earlier(i, k, 2):
                        choose(*before)
                    if before := earlier(i, k, 3):
                        place(*before)

            c.rounds(TI, 8 * TB, body)
            place(TI - 1, TB - 3)
            choose(TI - 1, TB - 2)
            place(TI - 1, TB - 2)
            choose(TI - 1, TB - 1)
            place(TI - 1, TB - 1)

            dve.wait_ge(s["counts"], 1)
            c.link(V.tensor_tensor(n_f[:, :], b_n[:, 0:NE], m.C[:, K_CAP:K_CAP + NE], ALU.add))
            V.tensor_copy(pad_i[:, :], n_f[:, :]).then_inc(s["pads_ready"], 1)
            c.link(V.tensor_scalar(n_i[:, :], b_n[:, 0:NE], float(P - 1), None, ALU.add))
            c.link(V.tensor_scalar(n_j[:, :], n_i[:, :], 7, None, ALU.logical_shift_right))
            c.link(V.tensor_copy(tiles[:, :], n_j[:, :]))
            c.link(V.tensor_tensor_scan(tile_end[:, :], tiles[:, :], tiles[:, :], 0.0, ALU.add, ALU.max))
            c.link(V.tensor_tensor(shift[:, :], tile_end[:, :], tiles[:, :], ALU.subtract))
            c.link(V.scalar_tensor_tensor(shift[:, :], shift[:, :], -float(P), m.C[:, K_CAP:K_CAP + NE], ALU.mult, ALU.add))
            o = slice(0, 1)
            tile_no = m.iota[o, 0:MT]
            c.link(V.tensor_tensor(over[o, :, :], tile_end[o, :].unsqueeze(1).to_broadcast([1, MT, NE]),
                                   tile_no.unsqueeze(2).to_broadcast([1, MT, NE]), ALU.is_le))
            c.link(V.tensor_reduce(ex_f[o, :], over[o, :, :], AX_X, ALU.add))
            c.link(V.tensor_scalar(valid[o, :], ex_f[o, :], float(NE), None, ALU.is_lt))
            c.link(V.tensor_scalar(ex_f[o, :], ex_f[o, :], float(NE - 1), None, ALU.min))
            c.link(V.tensor_copy(m.expert_i[o, :], ex_f[o, :]))
            c.link(V.tensor_tensor(over[o, :, :], ex_f[o, :].unsqueeze(2).to_broadcast([1, MT, NE]),
                                   m.iota[o, 0:NE].unsqueeze(1).to_broadcast([1, MT, NE]), ALU.is_equal))
            c.link(V.tensor_tensor(over[o, :, :], over[o, :, :], shift[o, :].unsqueeze(1).to_broadcast([1, MT, NE]), ALU.mult))
            c.link(V.tensor_reduce(row_f[o, :], over[o, :, :], AX_X, ALU.add))
            c.link(V.scalar_tensor_tensor(row_f[o, :], tile_no, float(P), row_f[o, :], ALU.mult, ALU.add))
            c.link(V.scalar_tensor_tensor(row_f[o, :], row_f[o, :], float(DUMMY), valid[o, :], ALU.subtract, ALU.mult))
            c.link(V.tensor_scalar(m.tile_row_i[o, :], row_f[o, :], float(DUMMY), None, ALU.add))
            c.link(V.tensor_tensor(picked2,
                                   m.chosen[:, :, :, :].rearrange("p t r e -> p (t r) e"),
                                   shift[:, :].unsqueeze(1).to_broadcast([P, 2 * NT, NE]), ALU.mult))
            c.link(V.tensor_reduce(fid[:, :, :].rearrange("p t r -> p (t r)"),
                                   picked2, AX_X, ALU.add))
            c.link(V.tensor_tensor(fid[:, :, :], m.row_f[:, :, :], fid[:, :, :], ALU.subtract))
            c.link(V.tensor_tensor(m.fetch_i[:, :, :], fid[:, :, :],
                                   m.C[:, K_VAL:K_VAL + NT].unsqueeze(2).to_broadcast([P, NT, 2]), ALU.mult))
            V.tensor_tensor(m.share[:, :, 1], m.share[:, :, 1], m.share[:, :, 0], ALU.subtract).then_inc(s["gap_ready"], 1)
            dve.wait_ge(s["gap_exp"], 1)
            c.link(V.tensor_scalar(m.share[:, :, 0], ex2[:, :], 1.0, None, ALU.add))
            c.link(V.reciprocal(m.share[:, :, 0], m.share[:, :, 0]))
            c.link(V.tensor_tensor(m.share[:, :, 1], ex2[:, :], m.share[:, :, 0], ALU.mult))


def expert_stage(nc, m):
    UN = 4
    with ExitStack() as ctx:
        ph = Phase(nc, ctx, "expert")
        z, zT = ph.sb("tile_z", [UN, D]), ph.sb("tile_zT", [2, D])
        h, hT, y = ph.sb("tile_h", [FF]), ph.sb("tile_hT", [2, FF]), ph.sb("tile_y", [UN, D])
        mix, mixT = ph.sb("b2_share", [NE]), ph.sb("b2_shareT", [P])
        names = "link mix_ready mixT_psum mixT_ready b2_psum b2_added zT_psum zT_ready h_psum h_ready hT_psum hT_ready y_psum y_ready beta_added"
        s = {n: ph.sem(n) for n in names.split()}
        loaded, stored = ph.sems("z_loaded", UN), ph.sems("y_stored", UN)
        b_zT, b_h, b_hT, b_y = m.bank[0:2], m.bank[2:4], m.bank[4:6], m.bank[6:8]
        block = ctx.enter_context(nc.Block())
        turns = MT // UN

        def step(body):
            def run(eng):
                for k in range(UN):
                    body(0, k)
                with eng.Fori(1, turns - 1) as i:
                    for k in range(UN):
                        body(i, k)
                for k in range(UN):
                    body(turns - 1, k)
            return run

        def following(i, k):
            if k + 1 < UN:
                return i, k + 1
            return None if isinstance(i, int) and i == turns - 1 else (i + 1, 0)

        @block.sync
        def _(sp):
            def load(i, k):
                j = i * UN + k
                row = sp.value_load(m.tile_row_i[0:1, bass.ds(j, 1)], min_val=0, max_val=DUMMY)
                wait(sp, s["zT_psum"], j - UN + 1)
                sp.dma_start(z[:, k, :], m.routed[bass.ds(row, P), :]).then_inc(loaded[k], 16)

            step(load)(sp)

        @block.scalar
        def _(act):
            def node(i, k):
                act.wait_ge(s["mixT_psum"], i * TB + k + 1)
                nc.scalar.copy(mixT[0:NE, :], b_h[0][0:NE, 0:P]).then_inc(s["mixT_ready"], 1)

            rounds(act, TI, lambda i: [node(i, k) for k in range(TB)])

            def relu(i, k):
                j = i * UN + k
                expert = act.value_load(m.expert_i[0:1, bass.ds(j, 1)], min_val=0, max_val=NE - 1)
                act.wait_ge(s["hT_psum"], j + 1)
                wait(act, s["y_psum"], j - 1)
                for f in range(FC):
                    last = nc.scalar.activation(hT[:, k % 2, f * P:(f + 1) * P], b_hT[k % 2][:, f * P:(f + 1) * P],
                                                ACT.Relu, bias=m.b1_cols[:, bass.ds(expert * FC + f, 1)])
                last.then_inc(s["hT_ready"], 1)

            def store(i, k):
                j = i * UN + k
                act.wait_ge(s["y_ready"], j + 1)
                act.dma_start(m.expert_out[bass.ds(j * P, P), :], y[:, k, :]).then_inc(stored[k], 16)

            def body(i, k):
                relu(i, k)
                if k:
                    store(i, k - 1)
                elif not (isinstance(i, int) and i == 0):
                    store(i - 1, UN - 1)

            step(body)(act)
            store(turns - 1, UN - 1)
            for k in range(UN):
                act.wait_ge(stored[k], 16 * turns)

        @block.gpsimd
        def _(pool):
            nc.gpsimd.tensor_tensor(m.Y[:, :, :], m.Y[:, :, :], m.beta_b[:, :].unsqueeze(1).to_broadcast([P, NT, D]),
                                    ALU.add).then_inc(s["beta_added"], 1)
            pool.wait_ge(s["beta_added"], 1)

        @block.tensor
        def _(pe):
            T = nc.tensor

            def node(i, k):
                t = i * TB + k
                pe.wait_ge(s["mix_ready"], t + 1)
                T.transpose(b_h[0][0:NE, 0:P], mix[:, :], m.ident).then_inc(s["mixT_psum"], 1)
                pe.wait_ge(s["mixT_ready"], t + 1)
                wait(pe, s["b2_added"], t - last_use(k, 2, TB) + 1)
                T.matmul(b_y[k % 2][:, 0:D], mixT[0:NE, :], m.b2_rows[0:NE, :], start=True, stop=True).then_inc(s["b2_psum"], 1)

            rounds(pe, TI, lambda i: [node(i, k) for k in range(TB)])
            pe.wait_ge(s["b2_added"], NT)

            def enter(i, k):
                j = i * UN + k
                b = k % 2
                expert = pe.value_load(m.expert_i[0:1, bass.ds(j, 1)], min_val=0, max_val=NE - 1)
                pe.wait_ge(loaded[k], i * 16 + 16)
                wait(pe, s["zT_ready"], j - 1)
                for c in range(DC):
                    last = T.transpose(b_zT[b][:, c * P:(c + 1) * P], z[:, k, c * P:(c + 1) * P], m.ident)
                last.then_inc(s["zT_psum"], 1)
                pe.wait_ge(s["zT_ready"], j + 1)
                wait(pe, s["h_ready"], j - 1)
                for c in range(DC):
                    last = T.matmul(b_h[b][:, :], zT[:, b, c * P:(c + 1) * P],
                                    m.w1_sb[:, bass.ds(expert, 1), c, :].rearrange("p a f -> p (a f)"),
                                    start=(c == 0), stop=(c == DC - 1))
                last.then_inc(s["h_psum"], 1)

            def body(i, k):
                j = i * UN + k
                b = k % 2
                pe.wait_ge(s["h_ready"], j + 1)
                wait(pe, s["hT_ready"], j - 1)
                for f in range(FC):
                    last = T.transpose(b_hT[b][:, f * P:(f + 1) * P], h[:, f * P:(f + 1) * P], m.ident)
                last.then_inc(s["hT_psum"], 1)
                if after := following(i, k):
                    enter(*after)
                expert = pe.value_load(m.expert_i[0:1, bass.ds(j, 1)], min_val=0, max_val=NE - 1)
                pe.wait_ge(s["hT_ready"], j + 1)
                wait(pe, s["y_ready"], j - 1)
                for f in range(FC):
                    last = T.matmul(b_y[b][:, 0:D], hT[:, b, f * P:(f + 1) * P],
                                    m.w2_sb[:, bass.ds(expert, 1), f, :].rearrange("p a f -> p (a f)"),
                                    start=(f == 0), stop=(f == FC - 1))
                last.then_inc(s["y_psum"], 1)

            enter(0, 0)
            step(body)(pe)

        @block.vector
        def _(dve):
            V = nc.vector
            c = Chain(dve, s["link"])

            def node(i, k):
                t = i * TB + k
                at = bass.ds(t, 1)
                pair, share = m.chosen[:, at, :, :], m.share[:, at, :]
                wait(dve, s["mixT_psum"], t)
                c.link(V.tensor_scalar(mix[:, :].unsqueeze(1), pair[:, :, 0, :], share[:, :, 0], None, ALU.mult))
                V.scalar_tensor_tensor(mix[:, :].unsqueeze(1), pair[:, :, 1, :], share[:, :, 1], mix[:, :].unsqueeze(1),
                                       ALU.mult, ALU.add).then_inc(s["mix_ready"], 1)

            def add_b2(i, k):
                t = i * TB + k
                dve.wait_ge(s["b2_psum"], t + 1)
                tile = m.Z[:, bass.ds(t, 1), :]
                V.tensor_tensor(tile, tile, b_y[k % 2][:, 0:D].unsqueeze(1), ALU.add).then_inc(s["b2_added"], 1)

            def nodes(i):
                for k in range(TB):
                    node(i, k)
                    if before := earlier(i, k, 1):
                        add_b2(*before)

            c.rounds(TI, TB, nodes)
            add_b2(TI - 1, TB - 1)

            def enter(i, k):
                j = i * UN + k
                b = k % 2
                dve.wait_ge(s["zT_psum"], j + 1)
                wait(dve, s["h_psum"], j - 1)
                V.tensor_copy(zT[:, b, :], b_zT[b][:, 0:D]).then_inc(s["zT_ready"], 1)
                dve.wait_ge(s["h_psum"], j + 1)
                wait(dve, s["hT_psum"], j)
                V.tensor_copy(h[:, :], b_h[b][:, :]).then_inc(s["h_ready"], 1)

            def body(i, k):
                j = i * UN + k
                if after := following(i, k):
                    enter(*after)
                dve.wait_ge(s["y_psum"], j + 1)
                wait(dve, stored[k], i * 16)
                V.tensor_copy(y[:, k, :], b_y[k % 2][:, 0:D]).then_inc(s["y_ready"], 1)

            enter(0, 0)
            step(body)(dve)


def combine_stage(nc, m):
    with ExitStack() as ctx:
        ph = Phase(nc, ctx, "combine")
        a = Arena(m.W1, NE * DC * FF)
        got, index = a.cut([TB, 2, D]), ph.sb("got_index", [TB, 2], I32)
        y, o = a.cut([TB, D]), a.cut([TB, D])
        st6, mv, root, eps = ph.sb("cb_stats", [TB, 6]), ph.sb("cb_mean_var", [TB, 2]), ph.sb("cb_root", [TB, 1]), ph.sb("cb_eps", [1])
        s = {n: ph.sem(n) for n in "link eps_ready var_ready rooted weighed result tail_out".split()}
        staged, landed, stored = ph.sems("cb_staged", TB), ph.sems("cb_landed", TB), ph.sems("cb_stored", TB)
        block = ctx.enter_context(nc.Block())

        @block.sync
        def _(sp):
            def store(i, k):
                t = i * TB + k
                sp.wait_ge(s["result"], t + 1)
                sp.dma_start(m.out[bass.ds(t * P, P), :], o[:, k, :]).then_inc(stored[k], 16)

            for k in range(TB):
                store(0, k)
            with sp.Fori(1, TI - 1) as i:
                for k in range(TB):
                    store(i, k)
            for k in range(TB - 1):
                store(TI - 1, k)
            sp.wait_ge(s["result"], NT)
            sp.dma_start(m.out[N - TAIL:N, :], o[0:TAIL, TB - 1, :]).then_inc(s["tail_out"], 16)
            for k in range(TB):
                sp.wait_ge(stored[k], 16 * (TI - (k == TB - 1)))
            sp.wait_ge(s["tail_out"], 16)

        @block.gpsimd
        def _(pool):
            with pool.Fori(1, TI + 1) as v:
                for k in range(TB):
                    for r in range(2):
                        pool.wait_ge(s["eps_ready"], 1)
                        pool.wait_ge(staged[k], v)
                        nc.gpsimd.indirect_dma_start(got[:, k, r, :], None, m.expert_out,
                                                     bass.IndirectOffsetOnAxis(ap=index[:, k, r:r + 1], axis=0)).then_inc(landed[k], 16)

        @block.scalar
        def _(act):
            A = nc.scalar

            def stage(i, k):
                wait(act, s["weighed"], (i - 1) * TB + k + 1)
                A.copy(index[:, k:k + 1, :], m.fetch_i[:, bass.ds(i * TB + k, 1), :]).then_inc(staged[k], 1)

            def take_root(i, k):
                act.wait_ge(s["var_ready"], i * TB + k + 1)
                A.activation(root[:, k, :], mv[:, k, 1:2], ACT.Sqrt, bias=eps[:, :]).then_inc(s["rooted"], 1)

            for k in range(TB):
                stage(0, k)
            act.wait_ge(s["eps_ready"], 1)
            with act.Fori(1, TI) as i:
                for k in range(TB):
                    take_root(i - 1, k)
                    stage(i, k)
            for k in range(TB):
                take_root(TI - 1, k)

        @block.vector
        def _(dve):
            V = nc.vector
            c = Chain(dve, s["link"])
            V.memset(eps[:, :], EPS).then_inc(s["eps_ready"], 1)

            def weigh(i, k):
                t = i * TB + k
                at = bass.ds(t, 1)
                share = m.share[:, at, :]
                dve.wait_ge(landed[k], i * 32 + 32)
                c.link(V.scalar_tensor_tensor(y[:, k:k + 1, :], got[:, k, 0:1, :], share[:, :, 0], m.Z[:, at, :], ALU.mult, ALU.add))
                V.scalar_tensor_tensor(y[:, k:k + 1, :], got[:, k, 1:2, :], share[:, :, 1], y[:, k:k + 1, :], ALU.mult,
                                       ALU.add).then_inc(s["weighed"], 1)
                dve.wait_ge(s["weighed"], t + 1)
                c.link(V.bn_stats(st6[:, k, :], y[:, k, :]), apart=True)
                V.bn_aggr(mv[:, k, :], st6[:, k, :]).then_inc(s["var_ready"], 1)

            def finish(i, k):
                t = i * TB + k
                dve.wait_ge(s["rooted"], t + 1)
                dve.wait_ge(s["var_ready"], t + 1)
                c.link(V.reciprocal(root[:, k, :], root[:, k, :]))
                c.link(V.tensor_scalar(y[:, k, :], y[:, k, :], mv[:, k, 0:1], root[:, k, :], ALU.subtract, ALU.mult))
                c.link(V.tensor_tensor(y[:, k, :], y[:, k, :], m.gamma_b[:, :], ALU.mult))
                wait(dve, stored[k], i * 16)
                V.tensor_tensor(o[:, k:k + 1, :], y[:, k:k + 1, :], m.Y[:, bass.ds(t, 1), :], ALU.add).then_inc(s["result"], 1)

            def body(i):
                for k in range(TB):
                    weigh(i, k)
                    if before := earlier(i, k, 1):
                        finish(*before)

            c.rounds(TI, 5 * TB, body)
            finish(TI - 1, TB - 1)


class Memory:
    pass


def build(nc, x, src, dst, ew, wl, bl, wr, br, wq, wk, wv, wo, bo, kg, kb, vg, vb,
          gate_w, gate_b, w1, b1, w2, b2, gamma, beta, consts, out):
    m = Memory()
    m.x, m.src, m.dst, m.ew, m.consts, m.out = x, src, dst, ew, consts, out
    m.wl, m.bl, m.wr, m.br = wl, bl, wr, br
    m.wq, m.wk, m.wv, m.wo, m.bo = wq, wk, wv, wo, bo
    m.kg, m.kb, m.vg, m.vb = kg, kb, vg, vb
    m.gate_w, m.gate_b, m.w1, m.b1, m.w2, m.b2, m.gamma, m.beta = gate_w, gate_b, w1, b1, w2, b2, gamma, beta
    m.h_table = nc.dram_tensor("h_table", (NT * P, D), F32, kind="Internal").ap()
    m.routed = nc.dram_tensor("routed_z", (ZROWS, D), F32, kind="Internal").ap()
    m.expert_out = nc.dram_tensor("expert_out", (MT * P, D), F32, kind="Internal").ap()
    with ExitStack() as ctx:
        ph = Phase(nc, ctx, "whole")
        m.bank = [ctx.enter_context(nc.psum_tensor(f"bank{i}", [P, 512], F32)) for i in range(8)]
        m.C = ph.sb("constants", [K_END])
        m.ident, m.tri, m.ones = m.C[:, K_ID:K_ID + P], m.C[:, K_TRI:K_TRI + P], m.C[:, K_ONE:K_ONE + P]
        m.center, m.mask, m.iota = m.C[:, K_CEN:K_CEN + P], m.C[:, K_MSK:K_MSK + P], m.C[:, K_IOTA:K_IOTA + 256]
        m.iota_h = ph.sb("iota_bf16", [256], BF16)
        m.zero_h = ph.sb("zero_bf16", [512], BF16)
        m.Y = ph.sb("nodes", [NT, D])
        m.W1 = ph.sb("w1_all", [NE * DC * FF])
        m.W2 = ph.sb("w2_all", [NE * FC * D])
        m.w1_sb = m.W1[:, :].rearrange("p (e c f) -> p e c f", e=NE, c=DC)
        m.w2_sb = m.W2[:, :].rearrange("p (e c d) -> p e c d", e=NE, c=FC)
        load_constants(nc, m)
        with ExitStack() as edge_ctx:
            pe = Phase(nc, edge_ctx, "edges")
            m.row_of, m.col_of = pe.sb("edge_slot_row", [EC]), pe.sb("edge_slot_col", [EC])
            m.val = pe.sb("edge_values", [5, EC])
            m.part_h = pe.sb("edge_part_bf16", [EC], BF16)
            m.bucket_i = pe.sb("column_bucket", [SUP, NC], I32)
            rank_edges(nc, m)
            node_stage(nc, m)
            edge_stage(nc, m)
        late = Phase(nc, ctx, "late")
        m.Z = late.sb("normed_nodes", [NT, D])
        m.chosen, m.share = late.sb("chosen", [NT, 2, NE]), late.sb("share", [NT, 2])
        m.row_f, m.fetch_i = late.sb("routed_row", [NT, 2]), late.sb("fetch_row", [NT, 2], I32)
        m.expert_i, m.tile_row_i = late.sb("tile_expert", [MT], I32), late.sb("tile_row", [MT], I32)
        m.b1_cols, m.b2_rows = late.sb("b1_columns", [NE * FC]), late.sb("b2_rows", [D])
        m.gamma_b, m.beta_b = late.sb("gamma", [D]), late.sb("beta", [D])
        route_stage(nc, m)
        expert_stage(nc, m)
        combine_stage(nc, m)


_INS = ["x", "src", "dst", "edge_weight", "L0_gnn_weight_l", "L0_gnn_bias_l", "L0_gnn_weight_r", "L0_gnn_bias_r",
        "L0_mix_wq", "L0_mix_wk", "L0_mix_wv", "L0_mix_wo", "L0_mix_bo", "L0_mix_ln_k_g", "L0_mix_ln_k_b",
        "L0_mix_ln_v_g", "L0_mix_ln_v_b", "L0_ffn_gate_w", "L0_ffn_gate_b", "L0_ffn_w1", "L0_ffn_b1", "L0_ffn_w2",
        "L0_ffn_b2", "L0_ffn_gamma", "L0_ffn_beta"]


def kernel(**inputs):
    import concourse.bacc as _bacc
    from concourse.bass_utils import run_bass_kernel_spmd as _run

    nc = _bacc.Bacc("TRN2", target_bir_lowering=False, num_devices=1)
    arrays, args = {}, []
    feed = [(name, np.ascontiguousarray(inputs[name])) for name in _INS] + [("consts", constant_table())]
    for name, a in feed:
        arrays[f"in_{name}_dram"] = a
        args.append(nc.dram_tensor(f"in_{name}_dram", a.shape, mybir.dt.from_np(a.dtype), kind="ExternalInput").ap())
    args.append(nc.dram_tensor("out_0_dram", (N, D), F32, kind="ExternalOutput").ap())
    build(nc, *args)
    r = _run(nc, [arrays], core_ids=[0])
    return r.results[0]["out_0_dram"]
```

```python
from contextlib import ExitStack

import numpy as np

import concourse.bass as bass
from concourse import mybir

ALU = mybir.AluOpType
ACT = mybir.ActivationFunctionType
AX_X = mybir.AxisListType.X
F32 = mybir.dt.float32
I32 = mybir.dt.int32
U32 = mybir.dt.uint32
BF16 = mybir.dt.bfloat16
FP16 = mybir.dt.float16

P = 128
N = 3125
D = 256
DC = D // P
NT = -(-N // P)
TAIL = N - (NT - 1) * P
HEAD = 64
NE = 16
FF = 512
FC = FF // P
EPS = 1e-5

E = 50000
EP = 125
EC = E // EP
SUP = 2
TC = EC // SUP
NI = NT
SB = TC // NI
HB = SB // 2
NC = (EP * TC + NT * (P - 1)) // P
NC += -NC % NI
GB = NC // NI
LAG = 3
GBP = GB + -GB % 4
SHOW = (1, 5)
assert EP * EC == E and NI * SB == TC and 2 * HB == SB and NC <= 2 * P and GB >= SB and SUP == 2

TB = 5
TI = NT // TB
CAP = 3328
DUMMY = NE * CAP
TRASH = DUMMY + P
ZROWS = TRASH + 2 * P
MT = (2 * N + NE * (P - 1)) // P
MT += MT % 2

K_ID, K_TRI, K_ONE, K_CEN, K_MSK, K_IOTA = 0, 128, 256, 384, 512, 640
K_CAP, K_VAL, K_TR, K_COL, K_END = 896, 912, 912 + NT, 912 + 3 * NT, 914 + 3 * NT


def constant_table():
    p = np.arange(P)[:, None]
    q = np.arange(P)[None, :]
    same = p // HEAD == q // HEAD
    c = np.zeros((P, K_END), np.float32)
    c[:, K_ID:K_ID + P] = p == q
    c[:, K_TRI:K_TRI + P] = p < q
    c[:, K_ONE:K_ONE + P] = 1
    c[:, K_CEN:K_CEN + P] = (p == q) - same / HEAD
    c[:, K_MSK:K_MSK + P] = same
    c[:, K_IOTA:K_IOTA + 256] = np.arange(256)
    c[:, K_CAP:K_CAP + NE] = np.arange(NE) * CAP
    real = p + P * np.arange(NT)[None, :] < N
    c[:, K_VAL:K_VAL + NT] = real
    c[:, K_TR:K_TR + 2 * NT] = np.stack([(1 - real) * (TRASH + p), (1 - real) * (TRASH + P + p)], 2).reshape(P, 2 * NT)
    c[:, K_COL:K_COL + 2] = p + P * np.arange(2)
    return c


class Arena:

    def __init__(self, tensor, words, at=0):
        self.tensor, self.words, self.at = tensor, words, at

    def cut(self, shape, dt=F32):
        size = 2 if dt in (BF16, FP16) else 4
        n = int(np.prod(shape))
        words = -(-n * size // 4)
        assert self.at + words <= self.words, (self.at, words, self.words)
        v = self.tensor[:, self.at:self.at + words]
        self.at += words
        if dt != F32:
            v = v.bitcast(dt)
        v = v[:, 0:n]
        if len(shape) == 2:
            v = v.rearrange("p (a b) -> p a b", a=shape[0])
        elif len(shape) == 3:
            v = v.rearrange("p (a b c) -> p a b c", a=shape[0], b=shape[1])
        return v


def rounds(eng, n, body):
    body(0)
    with eng.Fori(1, n) as i:
        body(i)


def wait(eng, sem, value):
    if isinstance(value, int) and value <= 0:
        return
    eng.wait_ge(sem, value)


class Chain:

    def __init__(self, eng, sem):
        self.eng, self.sem, self.n, self.base = eng, sem, 0, 0

    def link(self, ins, apart=False):
        self.n += 1
        ins.then_inc(self.sem, 1)
        self.eng.wait_ge(self.sem, self.base + self.n)
        if apart:
            self.eng.nop(nofuse=True)

    def rounds(self, n, per, body):
        body(0)
        first = self.n
        with self.eng.Fori(1, n) as i:
            self.base, self.n = (i - 1) * per + first, 0
            body(i)
            assert self.n == per, (self.n, per)
        self.base, self.n = 0, first + (n - 1) * per


def chunked(w):
    return w.rearrange("(c p) n -> p c n", p=P)


class Phase:

    def __init__(self, nc, ctx, tag):
        self.nc, self.ctx, self.tag, self.used = nc, ctx, tag, []
        ctx.callback(self.clear)

    def sb(self, name, shape, dt=F32):
        return self.ctx.enter_context(self.nc.sbuf_tensor(name, [P] + shape, dt))

    def sem(self, name):
        self.used.append(self.nc.alloc_semaphore(f"{self.tag}_{name}"))
        return self.used[-1]

    def clear(self):
        for used in self.used:
            self.nc.gpsimd.sem_clear(used)
            self.nc.release_semaphore(used)

    def sems(self, name, n):
        return [self.sem(f"{name}{k}") for k in range(n)]


def earlier(i, k, lag):
    k -= lag
    if k >= 0:
        return i, k
    return None if isinstance(i, int) and i == 0 else (i - 1, k + TB)


def since(k, slots):
    if k >= slots:
        return slots
    return TB - max(v for v in range(TB) if v % slots == k) + k


def last_use(u, slots, per_round):
    if u >= slots:
        return slots
    return per_round - max(v for v in range(per_round) if v % slots == u) + u


def prepare_stage(nc, m):
    with ExitStack() as ctx:
        ph = Phase(nc, ctx, "prepare")
        a = Arena(m.W2, NE * FC * D, m.xnT_words)
        onehot, running = a.cut([NT, TC], BF16), a.cut([NT, TC])
        a = Arena(m.W1, NE * DC * FF, m.small_words)
        wl = a.cut([DC, D])
        src_i, dst_i, t_i, u_i = (a.cut([EC], I32) for _ in range(4))
        ew_f, bucket = a.cut([EC]), a.cut([EC])
        ends, count, columns, base = a.cut([NT + 1]), a.cut([NT]), a.cut([NT]), a.cut([NT])
        cols_end = a.cut([SUP, NT])
        total_i, total_j = a.cut([NT], I32), a.cut([NT], I32)
        slot, slot_i, slot_j = a.cut([TC]), a.cut([TC], I32), a.cut([TC], I32)
        over, over_n = a.cut([2, NT]), a.cut([SUP, 2])
        st6, mv, rstd, shift, eps_x = a.cut([NT, 6]), a.cut([NT, 2]), a.cut([NT]), a.cut([NT]), a.cut([1])
        xn, xt, hs = a.cut([TB, D]), a.cut([TB, D]), a.cut([TB, D])
        names = ("consts edges x_loaded wl_loaded cleared stats var_ready rooted norm_ready xn_ready xt_psum xt_ready xt_kept "
                 "h_psum h_ready counted summed bucket_ready bucket_psum link")
        s = {n: ph.sem(n) for n in names.split()}
        h_stored = ph.sems("h_stored", TB)
        prefix, total, b_bucket = m.bank[0][:, 0:NT], m.bank[1][:, 0:NT], m.bank[2:4]
        b_t, b_h = m.bank[4:6], m.bank[6:8]
        block = ctx.enter_context(nc.Block())

        @block.sync
        def _(sp):
            for to, of in ((src_i, m.src), (dst_i, m.dst), (ew_f, m.ew)):
                sp.dma_start(to[0:EP, :], of.rearrange("(p t) -> p t", p=EP)).then_inc(s["edges"], 16)
            sp.dma_start(m.C[:, :], m.consts).then_inc(s["consts"], 16)
            sp.wait_ge(s["cleared"], 1)
            per = TB * P
            for g in range(TI):
                rows = min(per, (N - g * per) // P * P)
                sp.dma_start(m.Y[:, g * TB:g * TB + rows // P, :],
                             m.x[g * per:g * per + rows, :].rearrange("(t p) d -> p t d", p=P)).then_inc(s["x_loaded"], 16)
            sp.dma_start(m.Y[0:TAIL, NT - 1, :], m.x[N - TAIL:N, :]).then_inc(s["x_loaded"], 16)

            def store(i, k):
                sp.wait_ge(s["h_ready"], i * TB + k + 1)
                sp.dma_start(m.h_table[bass.ds((i * TB + k) * P, P), :], hs[:, k, :]).then_inc(h_stored[k], 16)

            rounds(sp, TI, lambda i: [store(i, k) for k in range(TB)])
            for k in range(TB):
                sp.wait_ge(h_stored[k], 16 * TI)

        @block.gpsimd
        def _(pool):
            def keep(i, k):
                t = i * TB + k
                pool.wait_ge(s["xt_ready"], t + 1)
                nc.gpsimd.tensor_copy(m.xnT[:, bass.ds(t, 1), :], xt[:, k:k + 1, :]).then_inc(s["xt_kept"], 1)

            rounds(pool, TI, lambda i: [keep(i, k) for k in range(TB)])
            pool.wait_ge(s["xt_kept"], NT)

        @block.scalar
        def _(act):
            A = nc.scalar
            act.dma_start(wl[:, :, :], chunked(m.wl)).then_inc(s["wl_loaded"], 16)
            for to, of in ((m.wk_sb, m.wk), (m.wv_sb, m.wv), (m.wo_sb, m.wo), (m.wq_sb, m.wq), (m.wr_sb, m.wr)):
                act.dma_start(to[:, :, :], chunked(of)).then_inc(m.w_loaded, 16)
            for to, of in ((m.kg_sb, m.kg), (m.kb_sb, m.kb)):
                act.dma_start(to[:, :], of.unsqueeze(0).to_broadcast([P, HEAD])).then_inc(m.w_loaded, 16)
            for to, of in ((m.vg_sb, m.vg), (m.vb_sb, m.vb)):
                for half in range(2):
                    act.dma_start(to[half * HEAD:(half + 1) * HEAD, :], of.unsqueeze(1)).then_inc(m.w_loaded, 16)
            for t, of in enumerate((m.bl, m.br, m.bo)):
                act.dma_start(m.biases[:, t, :], of.unsqueeze(0).to_broadcast([P, D])).then_inc(m.w_loaded, 16)
            act.wait_ge(s["var_ready"], 2)
            A.activation(rstd[:, :], mv[:, :, 1], ACT.Sqrt, bias=eps_x[:, :]).then_inc(s["rooted"], 1)

            def normalise(i, k):
                t = i * TB + k
                wait(act, s["xt_psum"], t - TB + 1)
                A.activation(xn[:, k:k + 1, :], m.Y[:, bass.ds(t, 1), :], ACT.Identity, bias=shift[:, bass.ds(t, 1)],
                             scale=rstd[:, bass.ds(t, 1)]).then_inc(s["xn_ready"], 1)

            def copy_t(i, k):
                t = i * TB + k
                act.wait_ge(s["xt_psum"], t + 1)
                wait(act, s["h_psum"], t - TB + 1)
                wait(act, s["xt_kept"], t - TB + 1)
                A.copy(xt[:, k, :], b_t[k % 2][:, 0:D]).then_inc(s["xt_ready"], 1)

            def copy_h(i, k):
                t = i * TB + k
                act.wait_ge(s["h_psum"], t + 1)
                wait(act, h_stored[k], i * 16)
                A.copy(hs[:, k, :], b_h[k % 2][:, 0:D]).then_inc(s["h_ready"], 1)

            def body(i):
                for k in range(TB):
                    normalise(i, k)
                    if before := earlier(i, k, 1):
                        copy_t(*before)
                    if before := earlier(i, k, 2):
                        copy_h(*before)

            act.wait_ge(s["norm_ready"], 1)
            rounds(act, TI, body)
            copy_t(TI - 1, TB - 1)
            copy_h(TI - 1, TB - 2)
            copy_h(TI - 1, TB - 1)

        @block.tensor
        def _(pe):
            T = nc.tensor

            def sum_counts(part):
                pe.wait_ge(s["counted"], part + 1)
                T.matmul(prefix, m.tri[0:EP, :], count[0:EP, :], start=True, stop=True)
                T.matmul(total, m.ones[0:EP, :], count[0:EP, :], start=True, stop=True).then_inc(s["summed"], 1)

            def turn_buckets(part):
                pe.wait_ge(s["bucket_ready"], part + 1)
                for half in range(2):
                    last = T.transpose(b_bucket[part][0:1, half * P:(half + 1) * P], over_n[:, part, half:half + 1], m.ident)
                last.then_inc(s["bucket_psum"], 1)

            def turn(i, k):
                t = i * TB + k
                pe.wait_ge(s["xn_ready"], t + 1)
                wait(pe, s["xt_ready"], t - since(k, 2) + 1)
                for c in range(DC):
                    last = T.transpose(b_t[k % 2][:, c * P:(c + 1) * P], xn[:, k, c * P:(c + 1) * P], m.ident)
                last.then_inc(s["xt_psum"], 1)

            def project(i, k):
                t = i * TB + k
                pe.wait_ge(s["xt_ready"], t + 1)
                wait(pe, s["h_ready"], t - since(k, 2) + 1)
                for c in range(DC):
                    last = T.matmul(b_h[k % 2][:, 0:D], xt[:, k, c * P:(c + 1) * P], wl[:, c, :],
                                    start=(c == 0), stop=(c == DC - 1))
                last.then_inc(s["h_psum"], 1)

            def body(i):
                for k in range(TB):
                    turn(i, k)
                    if before := earlier(i, k, 1):
                        project(*before)

            pe.wait_ge(s["consts"], 16)
            sum_counts(0)
            pe.wait_ge(s["wl_loaded"], 16)
            rounds(pe, TI, body)
            project(TI - 1, TB - 1)
            turn_buckets(0)
            sum_counts(1)
            turn_buckets(1)

        @block.vector
        def _(dve):
            c = Chain(dve, s["link"])
            V = nc.vector
            e = slice(0, EP)
            V.memset(m.Y[:, NT - 1, :], 0.0).then_inc(s["cleared"], 1)
            V.memset(m.zero_h[:, :], 0.0)
            V.memset(eps_x[:, :], EPS).then_inc(s["var_ready"], 1)
            dve.wait_ge(s["edges"], 48)
            c.link(V.tensor_scalar(u_i[e, :], src_i[e, :], 7, None, ALU.logical_shift_right))
            c.link(V.tensor_copy(bucket[e, :], u_i[e, :]))
            c.link(V.memset(ends[:, :], 0.0))
            dve.wait_ge(s["consts"], 16)

            def count_part(part):
                t = slice(part * TC, (part + 1) * TC)
                c.link(V.tensor_tensor(onehot[e, :, :], bucket[e, t].unsqueeze(1).to_broadcast([EP, NT, TC]),
                                       m.iota[e, 0:NT].unsqueeze(2).to_broadcast([EP, NT, TC]), ALU.is_equal))
                flat = onehot[e, :, :].rearrange("p b t -> p (b t)")
                c.link(V.tensor_tensor_scan(running[e, :, :].rearrange("p b t -> p (b t)"), flat, flat, 0.0,
                                            ALU.add, ALU.max))
                c.link(V.tensor_copy(ends[e, 1:NT + 1], running[e, :, TC - 1]))
                V.tensor_tensor(count[e, :], ends[e, 1:NT + 1], ends[e, 0:NT], ALU.subtract).then_inc(s["counted"], 1)

            def place_part(part):
                t = slice(part * TC, (part + 1) * TC)
                dve.wait_ge(s["summed"], part + 1)
                c.link(V.tensor_scalar(total_i[:, :], total, float(P - 1), None, ALU.add))
                c.link(V.tensor_scalar(total_j[:, :], total_i[:, :], 7, None, ALU.logical_shift_right))
                c.link(V.tensor_copy(columns[:, :], total_j[:, :]))
                c.link(V.tensor_tensor_scan(cols_end[:, part, :], columns[:, :], columns[:, :], 0.0, ALU.add, ALU.max))
                c.link(V.tensor_tensor(base[e, :], cols_end[e, part, :], columns[e, :], ALU.subtract))
                c.link(V.scalar_tensor_tensor(base[e, :], base[e, :], float(P), prefix[e, :], ALU.mult, ALU.add))
                c.link(V.scalar_tensor_tensor(base[e, :], base[e, :], 1.0, ends[e, 0:NT], ALU.subtract, ALU.subtract))
                c.link(V.tensor_tensor(running[e, :, :], running[e, :, :],
                                       base[e, :].unsqueeze(2).to_broadcast([EP, NT, TC]), ALU.add))
                c.link(V.tensor_tensor(running[e, :, :], running[e, :, :], onehot[e, :, :], ALU.mult))
                c.link(V.tensor_reduce(slot[e, :], running[e, :, :].rearrange("p b t -> p t b"), AX_X, ALU.add))
                c.link(V.tensor_copy(slot_i[e, :], slot[e, :]))
                c.link(V.tensor_scalar(slot_j[e, :], slot_i[e, :], P - 1, None, ALU.bitwise_and))
                c.link(V.tensor_copy(m.row_of[e, t], slot_j[e, :]))
                c.link(V.tensor_scalar(slot_j[e, :], slot_i[e, :], 7, None, ALU.logical_shift_right))
                c.link(V.tensor_copy(m.col_of[e, t], slot_j[e, :]))
                c.link(V.tensor_tensor(over[:, :, :], cols_end[:, part, :].unsqueeze(1).to_broadcast([P, 2, NT]),
                                       m.C[:, K_COL:K_COL + 2].unsqueeze(2).to_broadcast([P, 2, NT]), ALU.is_le))
                c.link(V.tensor_reduce(over_n[:, part, :], over[:, :, :], AX_X, ALU.add))
                V.tensor_scalar(over_n[:, part, :], over_n[:, part, :], float(NT - 1), None,
                                ALU.min).then_inc(s["bucket_ready"], 1)

            def stats(i, k):
                t = i * TB + k
                V.bn_stats(st6[:, bass.ds(t, 1), :].rearrange("p a d -> p (a d)"),
                           m.Y[:, bass.ds(t, 1), :].rearrange("p a d -> p (a d)")).then_inc(s["stats"], 1)

            count_part(0)
            dve.wait_ge(s["x_loaded"], 16 * (TI + 1))
            rounds(dve, TI, lambda i: [stats(i, k) for k in range(TB)])
            dve.wait_ge(s["stats"], NT)
            for t in range(NT):
                last = V.bn_aggr(mv[:, t, :], st6[:, t, :])
            last.then_inc(s["var_ready"], 1)
            c.link(V.tensor_scalar(t_i[e, :], dst_i[e, :], 2047, None, ALU.bitwise_and))
            c.link(V.tensor_copy(m.code_h[e, 0, :], t_i[e, :]))
            dve.wait_ge(s["rooted"], 1)
            c.link(V.reciprocal(rstd[:, :], rstd[:, :]))
            V.scalar_tensor_tensor(shift[:, :], mv[:, :, 0], -1.0, rstd[:, :], ALU.mult, ALU.mult).then_inc(s["norm_ready"], 1)
            place_part(0)
            c.link(V.tensor_scalar(t_i[e, :], dst_i[e, :], 4, P, ALU.logical_shift_right, ALU.bitwise_and))
            c.link(V.tensor_scalar(u_i[e, :], src_i[e, :], P - 1, None, ALU.bitwise_and))
            c.link(V.tensor_tensor(t_i[e, :], t_i[e, :], u_i[e, :], ALU.bitwise_or))
            c.link(V.tensor_copy(m.code_h[e, 1, :], t_i[e, :]))
            for j in range(3):
                c.link(V.tensor_copy(m.part_h[e, j, :], ew_f[e, :]))
                if j < 2:
                    c.link(V.tensor_tensor(ew_f[e, :], ew_f[e, :], m.part_h[e, j, :], ALU.subtract))
            c.link(V.tensor_copy(m.iota_t[:, :, :], m.iota[:, 0:NC].unsqueeze(2).to_broadcast([P, NC, HB])))
            count_part(1)
            place_part(1)
            for part in range(SUP):
                dve.wait_ge(s["bucket_psum"], part + 1)
                c.link(V.tensor_copy(m.bucket_i[0:1, part, :, 0:GB],
                                     b_bucket[part][0:1, 0:NC].rearrange("p (i u) -> p i u", u=GB)))


def edge_stage(nc, m):
    with ExitStack() as ctx:
        ph = Phase(nc, ctx, "edge")
        a = Arena(m.W1, NE * DC * FF, m.small_words)
        wkv, woT, mixed = a.cut([DC, 2 * D]), a.cut([DC, D]), a.cut([DC, D])
        kvT, t1, t2, vsum = a.cut([DC, P]), a.cut([DC, P]), a.cut([DC, P]), a.cut([DC])
        eps_kv, bias = a.cut([1]), a.cut([D])
        squares, kv = a.cut([2 * D]), a.cut([2 * D])
        ssum, root, rs = a.cut([8]), a.cut([8]), a.cut([8])
        xt, weff = ph.sb("xn_tile", [D]), ph.sb("mixed_weight", [DC, D])
        target, pair = ph.sb("slot_target", [SUP, NC], I32), ph.sb("slot_place_weight", [SUP, NC, 2])
        code, high = ph.sb("slot_code", [2, NC], I32), ph.sb("slot_high", [NC], I32)
        columns, row_1 = ph.sb("onehot_col", [2, NC, HB], BF16), ph.sb("onehot_row", [P, HB], BF16)
        row_c, row_w = ph.sb("row_code", [2, 2, P, HB], FP16), ph.sb("row_weight", [2, 3, P, HB], BF16)
        spread, fetched = ph.sb("spread", [GB, P]), ph.sb("fetched", [GB, D])
        index, now = ph.sb("fetch_index", [GB], I32), ph.sb("now_place_weight", [GB, 2])
        names = ("placed shown closed table link mix_added w1_in w2_in prepared prep_read xt_ready kv_psum squared "
                 "reduced kv_rooted kv_ready kv_used kv_folded mixed_psum mixed_ready weff_psum weff_ready again mix_psum "
                 "eps_ready bias_link bias_added")
        s = {n: ph.sem(n) for n in names.split()}
        staged, paired, landed = ph.sems("staged", GB), ph.sems("paired", GB), ph.sems("landed", GB)
        spreads, used, added = ph.sems("spread_ready", GB), ph.sems("used", GB), ph.sems("added", GB)
        place_of = [m.bank[j // 2][:, (j % 2) * 256:(j % 2) * 256 + NC] for j in range(5)]
        b_kv, b_acc, b_ks, b_mix, b_add = m.bank[3], m.bank[4], m.bank[5], m.bank[3], m.bank[4:8]
        block = ctx.enter_context(nc.Block())

        @block.sync
        def _(sp):
            sp.wait_ge(s["weff_ready"], 1)
            sp.wait_ge(s["bias_added"], 1)
            for e in range(NE):
                sp.dma_start(m.w1_sb[:, e, :, :], m.w1[e].rearrange("(c p) f -> p c f", p=P)).then_inc(s["w1_in"], 16)
            sp.wait_ge(s["again"], NT)
            for e in range(NE):
                sp.dma_start(m.w2_sb[:, e, :, :], m.w2[e].rearrange("(c p) d -> p c d", p=P)).then_inc(s["w2_in"], 16)
            sp.wait_ge(s["w1_in"], 16 * NE)
            sp.wait_ge(s["w2_in"], 16 * NE)

        @block.gpsimd
        def _(pool):
            pool.wait_ge(m.w_loaded, m.w_total)
            nc.gpsimd.tensor_tensor(bias[:, :], m.biases[:, 0, :], m.biases[:, 1, :], ALU.add).then_inc(s["bias_link"], 1)
            pool.wait_ge(s["bias_link"], 1)
            nc.gpsimd.tensor_tensor(bias[:, :], bias[:, :], m.biases[:, 2, :], ALU.add).then_inc(s["bias_link"], 1)
            pool.wait_ge(s["bias_link"], 2)
            nc.gpsimd.tensor_tensor(m.Y[:, :, :], m.Y[:, :, :], bias[:, :].unsqueeze(1).to_broadcast([P, NT, D]),
                                    ALU.add).then_inc(s["bias_added"], 1)
            with pool.Fori(1, SUP * NI + 1) as v:
                for u in range(GB):
                    pool.wait_ge(s["table"], 1)
                    pool.wait_ge(staged[u], v)
                    nc.gpsimd.indirect_dma_start(fetched[:, u, :], None, m.h_table,
                                                 bass.IndirectOffsetOnAxis(ap=index[:, u:u + 1], axis=0)).then_inc(landed[u], 16)

        @block.scalar
        def _(act):
            A = nc.scalar
            act.wait_ge(s["prepared"], 1)
            A.copy(wkv[:, 0, :], m.bank[6][:, :]).then_inc(s["prep_read"], 1)
            A.copy(wkv[:, 1, :], m.bank[7][:, :]).then_inc(s["prep_read"], 1)
            A.copy(woT[:, :, :], m.bank[5][:, :].rearrange("p (c d) -> p c d", c=DC)).then_inc(s["prep_read"], 1)

            def take_root(i):
                act.wait_ge(s["reduced"], i + 1)
                A.activation(root[:, :], ssum[:, :], ACT.Sqrt, bias=eps_kv[:, :]).then_inc(s["kv_rooted"], 1)

            def keys(i):
                wait(act, s["kv_psum"], i)
                A.copy(xt[:, :].unsqueeze(1), m.xnT[:, bass.ds(i, 1), :]).then_inc(s["xt_ready"], 1)
                if not (isinstance(i, int) and i == 0):
                    take_root(i - 1)
                act.wait_ge(s["kv_psum"], i + 1)
                A.activation(squares[:, :], b_kv[:, :], ACT.Square).then_inc(s["squared"], 1)

            act.wait_ge(s["eps_ready"], 1)
            rounds(act, NT, keys)
            take_root(NT - 1)

            def stage(part, i):
                for u in range(GB):
                    wait(act, used[u], part * NI + i)
                    A.copy(index[:, u:u + 1], target[:, part, bass.ds(i * GB + u, 1)]).then_inc(staged[u], 1)
                    A.copy(now[:, u:u + 1, :], pair[:, part, bass.ds(i * GB + u, 1), :]).then_inc(paired[u], 1)

            def again(i):
                wait(act, s["mix_psum"], i)
                A.copy(xt[:, :].unsqueeze(1), m.xnT[:, bass.ds(i, 1), :]).then_inc(s["again"], 1)

            def first(i):
                stage(0, i)
                again(i)

            act.wait_ge(s["table"], 1)
            stage(0, 0)
            act.wait_ge(s["mixed_psum"], 1)
            A.activation(mixed[:, :, :], m.bank[6][:, :].rearrange("p (c d) -> p c d", c=DC), ACT.Copy,
                         scale=1.0 / N).then_inc(s["mixed_ready"], 1)
            again(0)
            with act.Fori(1, NI) as i:
                first(i)
            for part in range(1, SUP):
                act.wait_ge(s["table"], part + 1)
                rounds(act, NI, lambda i, part=part: stage(part, i))

        @block.tensor
        def _(pe):
            T = nc.tensor

            def zero(start, stop):
                for b, width in ((0, 512), (1, 512), (2, 256)):
                    last = T.matmul(m.bank[b][:, 0:width], m.zero_h[:, 0:P], m.zero_h[:, 0:width], start=start, stop=stop)
                return last

            def place_batch(part, i, h):
                pe.wait_ge(s["shown"], (part * NI + i) * 2 + h + 1)
                for n in range(HB):
                    for j in range(5):
                        row = row_c[0:EP, h, j, :, n] if j < 2 else row_w[0:EP, h, j - 2, :, n]
                        last = T.matmul(place_of[j], row, columns[0:EP, h, :, n], start=False, stop=False)
                last.then_inc(s["placed"], 1)

            def keys(i):
                pe.wait_ge(s["xt_ready"], i + 1)
                wait(pe, s["kv_ready"], i)
                for c in range(DC):
                    last = T.matmul(b_kv[:, :], xt[:, c * P:(c + 1) * P], wkv[:, c, :], start=(c == 0), stop=(c == DC - 1))
                last.then_inc(s["kv_psum"], 1)

            def accumulate(i, rows=P):
                pe.wait_ge(s["kv_ready"], i + 1)
                done = rows != P
                slot = kv[0:rows, :]
                for c in range(DC):
                    v = slot[:, D + c * P:D + (c + 1) * P]
                    T.matmul(b_acc[:, c * P:(c + 1) * P], v, slot[:, c * P:(c + 1) * P], start=False, stop=False)
                    T.matmul(b_acc[:, D + c:D + c + 1], v, m.ones[0:rows, 0:1], start=False,
                             stop=done and c == DC - 1)
                T.matmul(b_ks[:, 0:D], m.ones[0:rows, :], slot[:, 0:D], start=False, stop=done).then_inc(s["kv_used"], 1)

            def mix(i):
                pe.wait_ge(s["again"], i + 1)
                wait(pe, s["mix_added"], i)
                for c in range(DC):
                    last = T.matmul(b_mix[:, 0:D], xt[:, c * P:(c + 1) * P], weff[:, c, :], start=(c == 0), stop=(c == DC - 1))
                last.then_inc(s["mix_psum"], 1)

            def spread_column(part, i, u):
                v = part * NI + i + 1
                pe.wait_ge(landed[u], v * 16)
                pe.wait_ge(spreads[u], v)
                back = last_use(u, 4, GB)
                if u >= back:
                    pe.wait_ge(added[u - back], v)
                else:
                    wait(pe, added[u - back + GB], v - 1)
                T.matmul(b_add[u % 4][:, 0:D], spread[:, u, :], fetched[:, u, :], start=True,
                         stop=True).then_inc(used[u], 1)

            pe.wait_ge(m.w_loaded, m.w_total)
            for c in range(DC):
                for half, w in enumerate((m.wk_sb, m.wv_sb)):
                    for h in range(DC):
                        T.matmul(m.bank[6 + c][:, half * D + h * P:half * D + (h + 1) * P],
                                 w[:, h, c * P:(c + 1) * P], m.center, start=True, stop=True)
            for o in range(DC):
                for c in range(DC):
                    last = T.transpose(m.bank[5][:, c * D + o * P:c * D + (o + 1) * P],
                                       m.wo_sb[:, o, c * P:(c + 1) * P], m.ident)
            last.then_inc(s["prepared"], 1)
            zero(True, False)
            T.matmul(b_acc[:, :], m.zero_h[:, 0:P], m.zero_h[:, :], start=True, stop=False)
            pe.wait_ge(s["prep_read"], 3)
            T.matmul(b_ks[:, :], m.zero_h[:, 0:P], m.zero_h[:, :], start=True, stop=False)

            def first(i):
                place_batch(0, i, 0)
                place_batch(0, i, 1)
                keys(i)
                if not (isinstance(i, int) and i == 0):
                    accumulate(i - 1)

            rounds(pe, NI, first)
            zero(False, True).then_inc(s["closed"], 1)
            accumulate(NT - 1, TAIL)
            pe.wait_ge(s["kv_folded"], 1)
            for c in range(DC):
                last = T.matmul(m.bank[6][:, c * D:(c + 1) * D], kvT[:, c, :], woT[:, c, :], start=True, stop=True)
            last.then_inc(s["mixed_psum"], 1)
            pe.wait_ge(s["mixed_ready"], 1)
            for o in range(DC):
                for c in range(DC):
                    last = T.matmul(m.bank[7][:, o * D:(o + 1) * D], m.wq_sb[:, c, o * P:(o + 1) * P], mixed[:, c, :],
                                    start=(c == 0), stop=(c == DC - 1))
            last.then_inc(s["weff_psum"], 1)
            pe.wait_ge(s["table"], 1)
            zero(True, False)
            pe.wait_ge(s["weff_ready"], 1)

            def body(part, i):
                for u in range(GB):
                    spread_column(part, i, u)
                    if part == 0 and u - LAG in SHOW:
                        place_batch(1, i, SHOW.index(u - LAG))
                if part == 0:
                    mix(i)

            for part in range(SUP):
                rounds(pe, NI, lambda i, part=part: body(part, i))
                if part == 0:
                    zero(False, True).then_inc(s["closed"], 1)

        @block.vector
        def _(dve):
            V = nc.vector
            c = Chain(dve, s["link"])
            e = slice(0, EP)
            V.memset(eps_kv[:, :], HEAD * EPS).then_inc(s["eps_ready"], 1)

            def show_places(part, i, h):
                t = part * TC + i * SB + h * HB
                no = (part * NI + i) * 2 + h
                wait(dve, s["placed"], no - 1)
                V.tensor_tensor(columns[e, h, :, :], m.iota_t[e, :, :],
                                m.col_of[e, bass.ds(t, HB)].unsqueeze(1).to_broadcast([EP, NC, HB]), ALU.is_equal)
                wait(dve, s["shown"], no)
                c.link(V.tensor_tensor(row_1[e, :, :], m.iota_t[e, 0:P, :],
                                       m.row_of[e, bass.ds(t, HB)].unsqueeze(1).to_broadcast([EP, P, HB]), ALU.is_equal))

            def show_values(part, i, h):
                t = part * TC + i * SB + h * HB
                for to, of, n in ((row_c, m.code_h, 2), (row_w, m.part_h, 3)):
                    last = V.tensor_tensor(to[e, h, :, :, :], row_1[e, :, :].unsqueeze(1).to_broadcast([EP, n, P, HB]),
                                           of[e, :, bass.ds(t, HB)].unsqueeze(2).to_broadcast([EP, n, P, HB]), ALU.mult)
                last.then_inc(s["shown"], 1)

            def read_table(part):
                dve.wait_ge(s["closed"], part + 1)
                for j in range(2):
                    c.link(V.tensor_copy(code[:, j, :], place_of[j]))
                c.link(V.tensor_scalar(high[:, :], code[:, 1, :], P, 4, ALU.bitwise_and, ALU.logical_shift_left))
                c.link(V.tensor_tensor(target[:, part, :], code[:, 0, :], high[:, :], ALU.bitwise_or))
                c.link(V.tensor_scalar(high[:, :], code[:, 1, :], P - 1, None, ALU.bitwise_and))
                c.link(V.tensor_copy(pair[:, part, :, 0], high[:, :]))
                weight = pair[:, part, :, 1]
                c.link(V.tensor_copy(weight, place_of[2]))
                for j in (3, 4):
                    last = V.tensor_tensor(weight, weight, place_of[j], ALU.add)
                    if j == 3:
                        c.link(last)
                last.then_inc(s["table"], 1)
                dve.wait_ge(s["table"], part + 1)

            def reduce_kv(i):
                dve.wait_ge(s["squared"], i + 1)
                wait(dve, s["kv_rooted"], i)
                V.tensor_reduce(ssum[:, :], squares[:, :].rearrange("p (h d) -> p h d", d=HEAD), AX_X,
                                ALU.add).then_inc(s["reduced"], 1)

            def scale_kv(i):
                dve.wait_ge(s["kv_rooted"], i + 1)
                c.link(V.reciprocal(rs[:, :], root[:, :]))
                wait(dve, s["kv_used"], i)
                V.scalar_tensor_tensor(kv[:, :].rearrange("p (h d) -> p h d", d=HEAD),
                                       b_kv[:, :].rearrange("p (h d) -> p h d", d=HEAD), float(HEAD) ** 0.5,
                                       rs[:, :].unsqueeze(2).to_broadcast([P, 8, HEAD]),
                                       ALU.mult, ALU.mult).then_inc(s["kv_ready"], 1)

            def first(i):
                show_places(0, i, 0)
                show_values(0, i, 0)
                if not (isinstance(i, int) and i == 0):
                    reduce_kv(i - 1)
                show_places(0, i, 1)
                if not (isinstance(i, int) and i == 0):
                    scale_kv(i - 1)
                show_values(0, i, 1)

            c.rounds(NI, 3, first)
            reduce_kv(NT - 1)
            scale_kv(NT - 1)
            read_table(0)

            dve.wait_ge(s["kv_used"], NT)
            dve.wait_ge(m.w_loaded, m.w_total)
            heads = lambda v: v.rearrange("p (h d) -> p h d", d=HEAD)
            kg2, kb2 = (v[:, :].unsqueeze(1).to_broadcast([P, 2, HEAD]) for v in (m.kg_sb, m.kb_sb))
            vg, vb = m.vg_sb, m.vb_sb
            c.link(V.tensor_copy(vsum[:, :], b_acc[:, D:D + DC]))
            for h in range(DC):
                c.link(V.tensor_tensor(heads(t1[:, h, :]), heads(b_acc[:, h * P:(h + 1) * P]), kg2, ALU.mult))
                c.link(V.scalar_tensor_tensor(heads(t1[:, h, :]), kb2, vsum[:, h:h + 1], heads(t1[:, h, :]), ALU.mult, ALU.add))
                c.link(V.tensor_tensor(heads(t2[:, h, :]), heads(b_ks[:, h * P:(h + 1) * P]), kg2, ALU.mult))
                c.link(V.scalar_tensor_tensor(heads(t2[:, h, :]), kb2, float(N), heads(t2[:, h, :]), ALU.mult, ALU.add))
                c.link(V.tensor_scalar(t2[:, h, :], t2[:, h, :], vb[:, :], None, ALU.mult))
                c.link(V.scalar_tensor_tensor(t1[:, h, :], t1[:, h, :], vg[:, :], t2[:, h, :], ALU.mult, ALU.add))
                last = V.tensor_tensor(kvT[:, h, :], t1[:, h, :], m.mask, ALU.mult)
            last.then_inc(s["kv_folded"], 1)
            dve.wait_ge(s["weff_psum"], 1)
            V.tensor_tensor(weff[:, :, :], m.bank[7][:, :].rearrange("p (c d) -> p c d", c=DC), m.wr_sb[:, :, :],
                            ALU.add).then_inc(s["weff_ready"], 1)
            dve.wait_ge(s["bias_added"], 1)

            buckets = [dve.alloc_register(f"bucket{u}") for u in range(GB)]

            def spread_weights(part, i, u):
                dve.wait_ge(paired[u], part * NI + i + 1)
                V.tensor_scalar(spread[:, u, :], m.iota[:, 0:P], now[:, u, 0:1], now[:, u, 1:2],
                                ALU.is_equal, ALU.mult).then_inc(spreads[u], 1)

            def bucket_of(u):
                return dve.snap(buckets[u], min_val=0, max_val=NT - 1)

            def add(part, i, u, bucket):
                v = part * NI + i + 1
                dve.wait_ge(used[u], v)
                if u:
                    dve.wait_ge(added[u - 1], v)
                elif part == 0:
                    wait(dve, s["mix_added"], i)
                elif isinstance(i, int) and part == 1:
                    dve.wait_ge(s["mix_added"], NI)
                else:
                    dve.wait_ge(added[GB - 1], v - 1)
                tile = m.Y[:, bass.ds(bucket, 1), :]
                V.tensor_tensor(tile, tile, b_add[u % 4][:, 0:D].unsqueeze(1), ALU.add).then_inc(added[u], 1)

            def add_mix(i):
                dve.wait_ge(s["mix_psum"], i + 1)
                dve.wait_ge(added[GB - 1], i + 1)
                tile = m.Y[:, bass.ds(i, 1), :]
                V.tensor_tensor(tile, tile, b_mix[:, 0:D].unsqueeze(1), ALU.add).then_inc(s["mix_added"], 1)

            def body(part, i):
                for u in range(GB):
                    if u == LAG:
                        dve.load(buckets, m.bucket_i[0:1, part, bass.ds(i, 1), 0:GB].rearrange("p a u -> p (a u)"))
                    bucket = bucket_of((u - LAG) % GB)
                    spread_weights(part, i, u)
                    if part == 0 and u in SHOW:
                        show_places(1, i, SHOW.index(u))
                    if u >= LAG:
                        add(part, i, u - LAG, bucket)
                    elif not (isinstance(i, int) and i == 0):
                        add(part, i - 1, u - LAG + GB, bucket)
                        if part == 0 and u == LAG - 1:
                            add_mix(i - 1)
                    if part == 0 and u in SHOW:
                        show_values(1, i, SHOW.index(u))

            for part in range(SUP):
                c.rounds(NI, 2 if part == 0 else 0, lambda i, part=part: body(part, i))
                for u in range(GB - LAG, GB):
                    add(part, NI - 1, u, bucket_of(u))
                if part == 0:
                    add_mix(NI - 1)
                if part == 0:
                    read_table(1)
            dve.wait_ge(added[GB - 1], SUP * NI)


def route_stage(nc, m):
    with ExitStack() as ctx:
        ph = Phase(nc, ctx, "route")
        gate, gate_b = ph.sb("gate_w", [DC, NE]), ph.sb("gate_b", [NE])
        st6, mv, rstd, eps = ph.sb("rt_stats", [NT, 6]), ph.sb("rt_mean_var", [NT, 2]), ph.sb("rt_rstd", [NT]), ph.sb("rt_eps", [1])
        zs, zT = ph.sb("z_slots", [TB, D]), ph.sb("zT_slots", [2, D])
        logit, top, top_at, top_f = ph.sb("logits", [NE]), ph.sb("top8", [8]), ph.sb("top8_at", [8], U32), ph.sb("top_f", [2])
        both, seen = ph.sb("both_onehots", [TB, NE]), ph.sb("seen", [NE])
        pos, pick, row_i = ph.sb("positions", [NE]), ph.sb("picked", [2, NE]), ph.sb("scatter_row", [TB, 2], I32)
        b1_rows, zeros = ph.sb("b1_rows", [P]), ph.sb("zeros", [D])
        n_i, n_j, n_f, tiles = ph.sb("n_i", [NE], I32), ph.sb("n_j", [NE], I32), ph.sb("n_f", [NE]), ph.sb("tiles", [NE])
        tile_end, shift = ph.sb("tile_end", [NE]), ph.sb("region_shift", [NE])
        over, ex_f, row_f, valid = ph.sb("over", [MT, NE]), ph.sb("expert_f", [MT]), ph.sb("row_f", [MT]), ph.sb("valid", [MT])
        pad_i = ph.sb("pad_row", [NE], I32)
        fid, ex2 = ph.sb("fetch_f", [NT, 2]), ph.sb("exp_gap", [NT])
        picked2 = over[:, 0:2 * NT, :]
        names = ("params stats var_ready rooted link cleared z_ready zT_psum zT_ready z_kept logit_psum both_ready "
                 "rank_psum seen_ready b1_psum counts_ready counts pads_ready pads gap_ready gap_exp")
        s = {n: ph.sem(n) for n in names.split()}
        row_ready, scattered = ph.sems("row_ready", TB), ph.sems("scattered", TB)
        b_t, b_l, b_r, b_b, b_n = m.bank[0:2], m.bank[2:4], m.bank[4:6], m.bank[6], m.bank[7]
        block = ctx.enter_context(nc.Block())

        @block.sync
        def _(sp):
            sp.dma_start(gate[:, :, :], m.gate_w.rearrange("(c p) e -> p c e", p=P)).then_inc(s["params"], 16)
            sp.dma_start(gate_b[:, :], m.gate_b.unsqueeze(0).to_broadcast([P, NE])).then_inc(s["params"], 16)
            sp.dma_start(b1_rows[0:NE * FC, :], m.b1.rearrange("e (c f) -> (e c) f", f=P)).then_inc(s["params"], 16)
            sp.dma_start(m.b2_rows[0:NE, :], m.b2).then_inc(s["params"], 16)
            sp.dma_start(m.gamma_b[:, :], m.gamma.unsqueeze(0).to_broadcast([P, D])).then_inc(s["params"], 16)
            sp.dma_start(m.beta_b[:, :], m.beta.unsqueeze(0).to_broadcast([P, D])).then_inc(s["params"], 16)
            sp.wait_ge(s["cleared"], 1)
            sp.dma_start(m.routed[DUMMY:DUMMY + P, :], zeros[:, :]).then_inc(s["pads"], 16)
            sp.wait_ge(s["pads_ready"], 1)
            for e in range(NE):
                row = sp.value_load(pad_i[0:1, e:e + 1], min_val=0, max_val=DUMMY - P)
                sp.dma_start(m.routed[bass.ds(row, P), :], zeros[:, :]).then_inc(s["pads"], 16)
            sp.wait_ge(s["pads"], 16 * (NE + 1))
            sp.wait_ge(s["params"], 16 * 6)

        @block.gpsimd
        def _(pool):
            with pool.Fori(1, TI + 1) as v:
                for k in range(TB):
                    for r in range(2):
                        pool.wait_ge(s["cleared"], 1)
                        pool.wait_ge(row_ready[k], v)
                        nc.gpsimd.indirect_dma_start(m.routed, bass.IndirectOffsetOnAxis(ap=row_i[:, k, r:r + 1], axis=0),
                                                     zs[:, k, :], None).then_inc(scattered[k], 16)
            for k in range(TB):
                pool.wait_ge(scattered[k], 32 * TI)

        @block.scalar
        def _(act):
            A = nc.scalar
            act.wait_ge(s["var_ready"], 2)
            A.activation(rstd[:, :], mv[:, :, 1], ACT.Sqrt, bias=eps[:, :]).then_inc(s["rooted"], 1)

            def copies(i, k):
                t = i * TB + k
                act.wait_ge(s["zT_psum"], t + 1)
                wait(act, s["logit_psum"], t - last_use(k, 2, TB) + 1)
                A.copy(zT[:, k % 2, :], b_t[k % 2][:, 0:D]).then_inc(s["zT_ready"], 1)
                A.copy(m.Z[:, bass.ds(t, 1), :], zs[:, k:k + 1, :]).then_inc(s["z_kept"], 1)

            rounds(act, TI, lambda i: [copies(i, k) for k in range(TB)])
            act.wait_ge(s["b1_psum"], 1)
            A.copy(m.b1_cols[:, :], b_b[:, 0:NE * FC]).then_inc(s["z_kept"], 1)
            act.wait_ge(s["gap_ready"], 1)
            A.activation(ex2[:, :], m.share[:, :, 1], ACT.Exp).then_inc(s["gap_exp"], 1)

        @block.tensor
        def _(pe):
            T = nc.tensor
            pe.wait_ge(s["params"], 16 * 6)
            T.transpose(b_b[:, 0:NE * FC], b1_rows[0:NE * FC, :], m.ident[0:NE * FC, 0:NE * FC]).then_inc(s["b1_psum"], 1)

            def turn(i, k):
                t = i * TB + k
                pe.wait_ge(s["z_ready"], t + 1)
                wait(pe, s["zT_ready"], t - last_use(k, 2, TB) + 1)
                for c in range(DC):
                    last = T.transpose(b_t[k % 2][:, c * P:(c + 1) * P], zs[:, k, c * P:(c + 1) * P], m.ident)
                last.then_inc(s["zT_psum"], 1)

            def logits(i, k):
                t = i * TB + k
                pe.wait_ge(s["zT_ready"], t + 1)
                wait(pe, s["both_ready"], t - last_use(k, 2, TB) + 1)
                for c in range(DC):
                    last = T.matmul(b_l[k % 2][:, 0:NE], zT[:, k % 2, c * P:(c + 1) * P], gate[:, c, :],
                                    start=(c == 0), stop=(c == DC - 1))
                last.then_inc(s["logit_psum"], 1)

            def rank(i, k):
                t = i * TB + k
                pe.wait_ge(s["both_ready"], t + 1)
                pe.wait_ge(s["seen_ready"], t + 1)
                T.matmul(b_r[k % 2][:, 0:NE], m.tri, both[:, k, :], start=True, stop=False)
                T.matmul(b_r[k % 2][:, 0:NE], m.ones, seen[:, :], start=False, stop=True).then_inc(s["rank_psum"], 1)

            def body(i):
                for k in range(TB):
                    turn(i, k)
                    if before := earlier(i, k, 1):
                        logits(*before)
                    if before := earlier(i, k, 2):
                        rank(*before)

            rounds(pe, TI, body)
            logits(TI - 1, TB - 1)
            rank(TI - 1, TB - 2)
            rank(TI - 1, TB - 1)
            pe.wait_ge(s["seen_ready"], NT + 1)
            T.matmul(b_n[:, 0:NE], m.ones, seen[:, :], start=True, stop=True).then_inc(s["counts"], 1)

        @block.vector
        def _(dve):
            V = nc.vector
            c = Chain(dve, s["link"])
            V.memset(zeros[:, :], 0.0).then_inc(s["cleared"], 1)
            V.memset(eps[:, :], EPS).then_inc(s["var_ready"], 1)
            V.memset(seen[:, :], 0.0).then_inc(s["seen_ready"], 1)

            def stats(i, k):
                at = bass.ds(i * TB + k, 1)
                V.bn_stats(st6[:, at, :].rearrange("p a d -> p (a d)"),
                           m.Y[:, at, :].rearrange("p a d -> p (a d)")).then_inc(s["stats"], 1)

            rounds(dve, TI, lambda i: [stats(i, k) for k in range(TB)])
            dve.wait_ge(s["stats"], NT)
            for t in range(NT):
                last = V.bn_aggr(mv[:, t, :], st6[:, t, :])
            last.then_inc(s["var_ready"], 1)
            dve.wait_ge(s["rooted"], 1)
            c.link(V.reciprocal(rstd[:, :], rstd[:, :]))
            dve.wait_ge(s["params"], 16 * 6)

            def normalise(i, k):
                t = i * TB + k
                at = bass.ds(t, 1)
                wait(dve, s["zT_psum"], t - TB + 1)
                wait(dve, s["z_kept"], t - TB + 1)
                wait(dve, scattered[k], i * 32)
                V.tensor_scalar(zs[:, k:k + 1, :], m.Y[:, at, :], mv[:, at, 0:1].rearrange("p a b -> p (a b)"),
                                rstd[:, at], ALU.subtract, ALU.mult).then_inc(s["z_ready"], 1)

            def choose(i, k):
                t = i * TB + k
                dve.wait_ge(s["logit_psum"], t + 1)
                c.link(V.tensor_tensor(logit[:, :], b_l[k % 2][:, 0:NE], gate_b[:, :], ALU.add), apart=True)
                c.link(V.max(top[:, :], logit[:, :]), apart=True)
                V.tensor_copy(m.share[:, bass.ds(t, 1), :], top[:, 0:2].unsqueeze(1))
                c.link(V.max_index(top_at[:, :], top[:, :], logit[:, :]))
                c.link(V.tensor_copy(top_f[:, :], top_at[:, 0:2]))
                real = m.C[:, bass.ds(t + K_VAL, 1)]
                for r in range(2):
                    last = V.tensor_scalar(m.chosen[:, bass.ds(t, 1), r:r + 1, :].rearrange("p a b e -> p (a b) e"),
                                           m.iota[:, 0:NE].unsqueeze(1), top_f[:, r:r + 1], real, ALU.is_equal, ALU.mult)
                c.link(last)
                pair = m.chosen[:, bass.ds(t, 1), :, :]
                V.tensor_tensor(both[:, k:k + 1, :], pair[:, :, 0, :], pair[:, :, 1, :], ALU.add).then_inc(s["both_ready"], 1)

            def place(i, k):
                t = i * TB + k
                dve.wait_ge(s["rank_psum"], t + 1)
                dve.wait_ge(s["both_ready"], t + 1)
                c.link(V.tensor_tensor(pos[:, :], b_r[k % 2][:, 0:NE], m.C[:, K_CAP:K_CAP + NE], ALU.add))
                V.tensor_tensor(seen[:, :], seen[:, :], both[:, k, :], ALU.add).then_inc(s["seen_ready"], 1)
                pair = m.chosen[:, bass.ds(t, 1), :, :].rearrange("p a r e -> p (a r) e")
                c.link(V.tensor_tensor(pick[:, :, :], pair, pos[:, :].unsqueeze(1).to_broadcast([P, 2, NE]), ALU.mult))
                row = m.row_f[:, bass.ds(t, 1), :].rearrange("p a r -> p (a r)")
                c.link(V.tensor_reduce(row, pick[:, :, :], AX_X, ALU.add))
                wait(dve, scattered[k], i * 32)
                V.tensor_tensor(row_i[:, k, :], row, m.C[:, bass.ds(t * 2 + K_TR, 2)], ALU.add).then_inc(row_ready[k], 1)

            def body(i):
                for k in range(TB):
                    normalise(i, k)
                    if before := earlier(i, k, 2):
                        choose(*before)
                    if before := earlier(i, k, 3):
                        place(*before)

            c.rounds(TI, 8 * TB, body)
            place(TI - 1, TB - 3)
            choose(TI - 1, TB - 2)
            place(TI - 1, TB - 2)
            choose(TI - 1, TB - 1)
            place(TI - 1, TB - 1)

            dve.wait_ge(s["counts"], 1)
            c.link(V.tensor_tensor(n_f[:, :], b_n[:, 0:NE], m.C[:, K_CAP:K_CAP + NE], ALU.add))
            V.tensor_copy(pad_i[:, :], n_f[:, :]).then_inc(s["pads_ready"], 1)
            c.link(V.tensor_scalar(n_i[:, :], b_n[:, 0:NE], float(P - 1), None, ALU.add))
            c.link(V.tensor_scalar(n_j[:, :], n_i[:, :], 7, None, ALU.logical_shift_right))
            c.link(V.tensor_copy(tiles[:, :], n_j[:, :]))
            c.link(V.tensor_tensor_scan(tile_end[:, :], tiles[:, :], tiles[:, :], 0.0, ALU.add, ALU.max))
            c.link(V.tensor_tensor(shift[:, :], tile_end[:, :], tiles[:, :], ALU.subtract))
            c.link(V.scalar_tensor_tensor(shift[:, :], shift[:, :], -float(P), m.C[:, K_CAP:K_CAP + NE], ALU.mult, ALU.add))
            o = slice(0, 1)
            tile_no = m.iota[o, 0:MT]
            c.link(V.tensor_tensor(over[o, :, :], tile_end[o, :].unsqueeze(1).to_broadcast([1, MT, NE]),
                                   tile_no.unsqueeze(2).to_broadcast([1, MT, NE]), ALU.is_le))
            c.link(V.tensor_reduce(ex_f[o, :], over[o, :, :], AX_X, ALU.add))
            c.link(V.tensor_scalar(valid[o, :], ex_f[o, :], float(NE), None, ALU.is_lt))
            c.link(V.tensor_scalar(ex_f[o, :], ex_f[o, :], float(NE - 1), None, ALU.min))
            c.link(V.tensor_copy(m.expert_i[o, :], ex_f[o, :]))
            c.link(V.tensor_tensor(over[o, :, :], ex_f[o, :].unsqueeze(2).to_broadcast([1, MT, NE]),
                                   m.iota[o, 0:NE].unsqueeze(1).to_broadcast([1, MT, NE]), ALU.is_equal))
            c.link(V.tensor_tensor(over[o, :, :], over[o, :, :], shift[o, :].unsqueeze(1).to_broadcast([1, MT, NE]), ALU.mult))
            c.link(V.tensor_reduce(row_f[o, :], over[o, :, :], AX_X, ALU.add))
            c.link(V.scalar_tensor_tensor(row_f[o, :], tile_no, float(P), row_f[o, :], ALU.mult, ALU.add))
            c.link(V.scalar_tensor_tensor(row_f[o, :], row_f[o, :], float(DUMMY), valid[o, :], ALU.subtract, ALU.mult))
            c.link(V.tensor_scalar(m.tile_row_i[o, :], row_f[o, :], float(DUMMY), None, ALU.add))
            c.link(V.tensor_tensor(picked2,
                                   m.chosen[:, :, :, :].rearrange("p t r e -> p (t r) e"),
                                   shift[:, :].unsqueeze(1).to_broadcast([P, 2 * NT, NE]), ALU.mult))
            c.link(V.tensor_reduce(fid[:, :, :].rearrange("p t r -> p (t r)"),
                                   picked2, AX_X, ALU.add))
            c.link(V.tensor_tensor(fid[:, :, :], m.row_f[:, :, :], fid[:, :, :], ALU.subtract))
            c.link(V.tensor_tensor(m.fetch_i[:, :, :], fid[:, :, :],
                                   m.C[:, K_VAL:K_VAL + NT].unsqueeze(2).to_broadcast([P, NT, 2]), ALU.mult))
            V.tensor_tensor(m.share[:, :, 1], m.share[:, :, 1], m.share[:, :, 0], ALU.subtract).then_inc(s["gap_ready"], 1)
            dve.wait_ge(s["gap_exp"], 1)
            c.link(V.tensor_scalar(m.share[:, :, 0], ex2[:, :], 1.0, None, ALU.add))
            c.link(V.reciprocal(m.share[:, :, 0], m.share[:, :, 0]))
            c.link(V.tensor_tensor(m.share[:, :, 1], ex2[:, :], m.share[:, :, 0], ALU.mult))


def expert_stage(nc, m):
    UN = 4
    with ExitStack() as ctx:
        ph = Phase(nc, ctx, "expert")
        z, zT = ph.sb("tile_z", [UN, D]), ph.sb("tile_zT", [2, D])
        h, hT, y = ph.sb("tile_h", [FF]), ph.sb("tile_hT", [2, FF]), ph.sb("tile_y", [UN, D])
        mix, mixT = ph.sb("b2_share", [NE]), ph.sb("b2_shareT", [P])
        names = "link mix_ready mixT_psum mixT_ready b2_psum b2_added zT_psum zT_ready h_psum h_ready hT_psum hT_ready y_psum y_ready beta_added"
        s = {n: ph.sem(n) for n in names.split()}
        loaded, stored = ph.sems("z_loaded", UN), ph.sems("y_stored", UN)
        b_zT, b_h, b_hT, b_y = m.bank[0:2], m.bank[2:4], m.bank[4:6], m.bank[6:8]
        block = ctx.enter_context(nc.Block())
        turns = MT // UN

        def step(body):
            def run(eng):
                for k in range(UN):
                    body(0, k)
                with eng.Fori(1, turns - 1) as i:
                    for k in range(UN):
                        body(i, k)
                for k in range(UN):
                    body(turns - 1, k)
            return run

        def following(i, k):
            if k + 1 < UN:
                return i, k + 1
            return None if isinstance(i, int) and i == turns - 1 else (i + 1, 0)

        @block.sync
        def _(sp):
            def load(i, k):
                j = i * UN + k
                row = sp.value_load(m.tile_row_i[0:1, bass.ds(j, 1)], min_val=0, max_val=DUMMY)
                wait(sp, s["zT_psum"], j - UN + 1)
                sp.dma_start(z[:, k, :], m.routed[bass.ds(row, P), :]).then_inc(loaded[k], 16)

            step(load)(sp)

        @block.scalar
        def _(act):
            def node(i, k):
                act.wait_ge(s["mixT_psum"], i * TB + k + 1)
                nc.scalar.copy(mixT[0:NE, :], b_h[0][0:NE, 0:P]).then_inc(s["mixT_ready"], 1)

            rounds(act, TI, lambda i: [node(i, k) for k in range(TB)])

            def relu(i, k):
                j = i * UN + k
                expert = act.value_load(m.expert_i[0:1, bass.ds(j, 1)], min_val=0, max_val=NE - 1)
                act.wait_ge(s["hT_psum"], j + 1)
                wait(act, s["y_psum"], j - 1)
                for f in range(FC):
                    last = nc.scalar.activation(hT[:, k % 2, f * P:(f + 1) * P], b_hT[k % 2][:, f * P:(f + 1) * P],
                                                ACT.Relu, bias=m.b1_cols[:, bass.ds(expert * FC + f, 1)])
                last.then_inc(s["hT_ready"], 1)

            def store(i, k):
                j = i * UN + k
                act.wait_ge(s["y_ready"], j + 1)
                act.dma_start(m.expert_out[bass.ds(j * P, P), :], y[:, k, :]).then_inc(stored[k], 16)

            def body(i, k):
                relu(i, k)
                if k:
                    store(i, k - 1)
                elif not (isinstance(i, int) and i == 0):
                    store(i - 1, UN - 1)

            step(body)(act)
            store(turns - 1, UN - 1)
            for k in range(UN):
                act.wait_ge(stored[k], 16 * turns)

        @block.gpsimd
        def _(pool):
            nc.gpsimd.tensor_tensor(m.Y[:, :, :], m.Y[:, :, :], m.beta_b[:, :].unsqueeze(1).to_broadcast([P, NT, D]),
                                    ALU.add).then_inc(s["beta_added"], 1)
            pool.wait_ge(s["beta_added"], 1)

        @block.tensor
        def _(pe):
            T = nc.tensor

            def node(i, k):
                t = i * TB + k
                pe.wait_ge(s["mix_ready"], t + 1)
                T.transpose(b_h[0][0:NE, 0:P], mix[:, :], m.ident).then_inc(s["mixT_psum"], 1)
                pe.wait_ge(s["mixT_ready"], t + 1)
                wait(pe, s["b2_added"], t - last_use(k, 2, TB) + 1)
                T.matmul(b_y[k % 2][:, 0:D], mixT[0:NE, :], m.b2_rows[0:NE, :], start=True, stop=True).then_inc(s["b2_psum"], 1)

            rounds(pe, TI, lambda i: [node(i, k) for k in range(TB)])
            pe.wait_ge(s["b2_added"], NT)

            def enter(i, k):
                j = i * UN + k
                b = k % 2
                expert = pe.value_load(m.expert_i[0:1, bass.ds(j, 1)], min_val=0, max_val=NE - 1)
                pe.wait_ge(loaded[k], i * 16 + 16)
                wait(pe, s["zT_ready"], j - 1)
                for c in range(DC):
                    last = T.transpose(b_zT[b][:, c * P:(c + 1) * P], z[:, k, c * P:(c + 1) * P], m.ident)
                last.then_inc(s["zT_psum"], 1)
                pe.wait_ge(s["zT_ready"], j + 1)
                wait(pe, s["h_ready"], j - 1)
                for c in range(DC):
                    last = T.matmul(b_h[b][:, :], zT[:, b, c * P:(c + 1) * P],
                                    m.w1_sb[:, bass.ds(expert, 1), c, :].rearrange("p a f -> p (a f)"),
                                    start=(c == 0), stop=(c == DC - 1))
                last.then_inc(s["h_psum"], 1)

            def body(i, k):
                j = i * UN + k
                b = k % 2
                pe.wait_ge(s["h_ready"], j + 1)
                wait(pe, s["hT_ready"], j - 1)
                for f in range(FC):
                    last = T.transpose(b_hT[b][:, f * P:(f + 1) * P], h[:, f * P:(f + 1) * P], m.ident)
                last.then_inc(s["hT_psum"], 1)
                if after := following(i, k):
                    enter(*after)
                expert = pe.value_load(m.expert_i[0:1, bass.ds(j, 1)], min_val=0, max_val=NE - 1)
                pe.wait_ge(s["hT_ready"], j + 1)
                wait(pe, s["y_ready"], j - 1)
                for f in range(FC):
                    last = T.matmul(b_y[b][:, 0:D], hT[:, b, f * P:(f + 1) * P],
                                    m.w2_sb[:, bass.ds(expert, 1), f, :].rearrange("p a f -> p (a f)"),
                                    start=(f == 0), stop=(f == FC - 1))
                last.then_inc(s["y_psum"], 1)

            enter(0, 0)
            step(body)(pe)

        @block.vector
        def _(dve):
            V = nc.vector
            c = Chain(dve, s["link"])

            def node(i, k):
                t = i * TB + k
                at = bass.ds(t, 1)
                pair, share = m.chosen[:, at, :, :], m.share[:, at, :]
                wait(dve, s["mixT_psum"], t)
                c.link(V.tensor_scalar(mix[:, :].unsqueeze(1), pair[:, :, 0, :], share[:, :, 0], None, ALU.mult))
                V.scalar_tensor_tensor(mix[:, :].unsqueeze(1), pair[:, :, 1, :], share[:, :, 1], mix[:, :].unsqueeze(1),
                                       ALU.mult, ALU.add).then_inc(s["mix_ready"], 1)

            def add_b2(i, k):
                t = i * TB + k
                dve.wait_ge(s["b2_psum"], t + 1)
                tile = m.Z[:, bass.ds(t, 1), :]
                V.tensor_tensor(tile, tile, b_y[k % 2][:, 0:D].unsqueeze(1), ALU.add).then_inc(s["b2_added"], 1)

            def nodes(i):
                for k in range(TB):
                    node(i, k)
                    if before := earlier(i, k, 1):
                        add_b2(*before)

            c.rounds(TI, TB, nodes)
            add_b2(TI - 1, TB - 1)

            def enter(i, k):
                j = i * UN + k
                b = k % 2
                dve.wait_ge(s["zT_psum"], j + 1)
                wait(dve, s["h_psum"], j - 1)
                V.tensor_copy(zT[:, b, :], b_zT[b][:, 0:D]).then_inc(s["zT_ready"], 1)
                dve.wait_ge(s["h_psum"], j + 1)
                wait(dve, s["hT_psum"], j)
                V.tensor_copy(h[:, :], b_h[b][:, :]).then_inc(s["h_ready"], 1)

            def body(i, k):
                j = i * UN + k
                if after := following(i, k):
                    enter(*after)
                dve.wait_ge(s["y_psum"], j + 1)
                wait(dve, stored[k], i * 16)
                V.tensor_copy(y[:, k, :], b_y[k % 2][:, 0:D]).then_inc(s["y_ready"], 1)

            enter(0, 0)
            step(body)(dve)


def combine_stage(nc, m):
    with ExitStack() as ctx:
        ph = Phase(nc, ctx, "combine")
        a = Arena(m.W1, NE * DC * FF)
        got, index = a.cut([TB, 2, D]), ph.sb("got_index", [TB, 2], I32)
        y, o = a.cut([TB, D]), a.cut([TB, D])
        st6, mv, root, eps = ph.sb("cb_stats", [TB, 6]), ph.sb("cb_mean_var", [TB, 2]), ph.sb("cb_root", [TB, 1]), ph.sb("cb_eps", [1])
        s = {n: ph.sem(n) for n in "link eps_ready var_ready rooted weighed result tail_out".split()}
        staged, landed, stored = ph.sems("cb_staged", TB), ph.sems("cb_landed", TB), ph.sems("cb_stored", TB)
        block = ctx.enter_context(nc.Block())

        @block.sync
        def _(sp):
            def store(i, k):
                t = i * TB + k
                sp.wait_ge(s["result"], t + 1)
                sp.dma_start(m.out[bass.ds(t * P, P), :], o[:, k, :]).then_inc(stored[k], 16)

            for k in range(TB):
                store(0, k)
            with sp.Fori(1, TI - 1) as i:
                for k in range(TB):
                    store(i, k)
            for k in range(TB - 1):
                store(TI - 1, k)
            sp.wait_ge(s["result"], NT)
            sp.dma_start(m.out[N - TAIL:N, :], o[0:TAIL, TB - 1, :]).then_inc(s["tail_out"], 16)
            for k in range(TB):
                sp.wait_ge(stored[k], 16 * (TI - (k == TB - 1)))
            sp.wait_ge(s["tail_out"], 16)

        @block.gpsimd
        def _(pool):
            with pool.Fori(1, TI + 1) as v:
                for k in range(TB):
                    for r in range(2):
                        pool.wait_ge(s["eps_ready"], 1)
                        pool.wait_ge(staged[k], v)
                        nc.gpsimd.indirect_dma_start(got[:, k, r, :], None, m.expert_out,
                                                     bass.IndirectOffsetOnAxis(ap=index[:, k, r:r + 1], axis=0)).then_inc(landed[k], 16)

        @block.scalar
        def _(act):
            A = nc.scalar

            def stage(i, k):
                wait(act, s["weighed"], (i - 1) * TB + k + 1)
                A.copy(index[:, k:k + 1, :], m.fetch_i[:, bass.ds(i * TB + k, 1), :]).then_inc(staged[k], 1)

            def take_root(i, k):
                act.wait_ge(s["var_ready"], i * TB + k + 1)
                A.activation(root[:, k, :], mv[:, k, 1:2], ACT.Sqrt, bias=eps[:, :]).then_inc(s["rooted"], 1)

            for k in range(TB):
                stage(0, k)
            act.wait_ge(s["eps_ready"], 1)
            with act.Fori(1, TI) as i:
                for k in range(TB):
                    take_root(i - 1, k)
                    stage(i, k)
            for k in range(TB):
                take_root(TI - 1, k)

        @block.vector
        def _(dve):
            V = nc.vector
            c = Chain(dve, s["link"])
            V.memset(eps[:, :], EPS).then_inc(s["eps_ready"], 1)

            def weigh(i, k):
                t = i * TB + k
                at = bass.ds(t, 1)
                share = m.share[:, at, :]
                dve.wait_ge(landed[k], i * 32 + 32)
                c.link(V.scalar_tensor_tensor(y[:, k:k + 1, :], got[:, k, 0:1, :], share[:, :, 0], m.Z[:, at, :], ALU.mult, ALU.add))
                V.scalar_tensor_tensor(y[:, k:k + 1, :], got[:, k, 1:2, :], share[:, :, 1], y[:, k:k + 1, :], ALU.mult,
                                       ALU.add).then_inc(s["weighed"], 1)
                dve.wait_ge(s["weighed"], t + 1)
                c.link(V.bn_stats(st6[:, k, :], y[:, k, :]), apart=True)
                V.bn_aggr(mv[:, k, :], st6[:, k, :]).then_inc(s["var_ready"], 1)

            def finish(i, k):
                t = i * TB + k
                dve.wait_ge(s["rooted"], t + 1)
                dve.wait_ge(s["var_ready"], t + 1)
                c.link(V.reciprocal(root[:, k, :], root[:, k, :]))
                c.link(V.tensor_scalar(y[:, k, :], y[:, k, :], mv[:, k, 0:1], root[:, k, :], ALU.subtract, ALU.mult))
                c.link(V.tensor_tensor(y[:, k, :], y[:, k, :], m.gamma_b[:, :], ALU.mult))
                wait(dve, stored[k], i * 16)
                V.tensor_tensor(o[:, k:k + 1, :], y[:, k:k + 1, :], m.Y[:, bass.ds(t, 1), :], ALU.add).then_inc(s["result"], 1)

            def body(i):
                for k in range(TB):
                    weigh(i, k)
                    if before := earlier(i, k, 1):
                        finish(*before)

            c.rounds(TI, 5 * TB, body)
            finish(TI - 1, TB - 1)


class Memory:
    pass


def build(nc, x, src, dst, ew, wl, bl, wr, br, wq, wk, wv, wo, bo, kg, kb, vg, vb,
          gate_w, gate_b, w1, b1, w2, b2, gamma, beta, consts, out):
    m = Memory()
    m.x, m.src, m.dst, m.ew, m.consts, m.out = x, src, dst, ew, consts, out
    m.wl, m.bl, m.wr, m.br = wl, bl, wr, br
    m.wq, m.wk, m.wv, m.wo, m.bo = wq, wk, wv, wo, bo
    m.kg, m.kb, m.vg, m.vb = kg, kb, vg, vb
    m.gate_w, m.gate_b, m.w1, m.b1, m.w2, m.b2, m.gamma, m.beta = gate_w, gate_b, w1, b1, w2, b2, gamma, beta
    m.h_table = nc.dram_tensor("h_table", (NT * P, D), F32, kind="Internal").ap()
    m.routed = nc.dram_tensor("routed_z", (ZROWS, D), F32, kind="Internal").ap()
    m.expert_out = nc.dram_tensor("expert_out", (MT * P, D), F32, kind="Internal").ap()
    with ExitStack() as ctx:
        ph = Phase(nc, ctx, "whole")
        m.bank = [ctx.enter_context(nc.psum_tensor(f"bank{i}", [P, 512], F32)) for i in range(8)]
        m.C = ph.sb("constants", [K_END])
        m.ident, m.tri, m.ones = m.C[:, K_ID:K_ID + P], m.C[:, K_TRI:K_TRI + P], m.C[:, K_ONE:K_ONE + P]
        m.center, m.mask, m.iota = m.C[:, K_CEN:K_CEN + P], m.C[:, K_MSK:K_MSK + P], m.C[:, K_IOTA:K_IOTA + 256]
        m.zero_h = ph.sb("zero_bf16", [512], BF16)
        m.Y = ph.sb("nodes", [NT, D])
        m.W1 = ph.sb("w1_all", [NE * DC * FF])
        m.W2 = ph.sb("w2_all", [NE * FC * D])
        m.w1_sb = m.W1[:, :].rearrange("p (e c f) -> p e c f", e=NE, c=DC)
        m.w2_sb = m.W2[:, :].rearrange("p (e c d) -> p e c d", e=NE, c=FC)
        a = Arena(m.W2, NE * FC * D)
        m.xnT = a.cut([NT, D])
        m.xnT_words = a.at
        a = Arena(m.W1, NE * DC * FF)
        m.wq_sb, m.wk_sb, m.wv_sb, m.wo_sb, m.wr_sb = (a.cut([DC, D]) for _ in range(5))
        m.kg_sb, m.kb_sb, m.vg_sb, m.vb_sb = a.cut([HEAD]), a.cut([HEAD]), a.cut([1]), a.cut([1])
        m.biases = a.cut([3, D])
        m.small_words = a.at
        m.w_loaded, m.w_total = ph.sem("small_weights"), 16 * 14
        with ExitStack() as edge_ctx:
            edges = Phase(nc, edge_ctx, "edges")
            m.row_of, m.col_of = edges.sb("edge_slot_row", [EC], BF16), edges.sb("edge_slot_col", [EC], BF16)
            m.code_h, m.part_h = edges.sb("edge_code", [2, EC], FP16), edges.sb("edge_weight_parts", [3, EC], BF16)
            m.bucket_i = edges.sb("column_bucket", [SUP, NI, GBP], I32)
            m.iota_t = edges.sb("iota_batch", [NC, HB], BF16)
            prepare_stage(nc, m)
            edge_stage(nc, m)
        late = Phase(nc, ctx, "late")
        m.Z = late.sb("normed_nodes", [NT, D])
        m.chosen, m.share = late.sb("chosen", [NT, 2, NE]), late.sb("share", [NT, 2])
        m.row_f, m.fetch_i = late.sb("routed_row", [NT, 2]), late.sb("fetch_row", [NT, 2], I32)
        m.expert_i, m.tile_row_i = late.sb("tile_expert", [MT], I32), late.sb("tile_row", [MT], I32)
        m.b1_cols, m.b2_rows = late.sb("b1_columns", [NE * FC]), late.sb("b2_rows", [D])
        m.gamma_b, m.beta_b = late.sb("gamma", [D]), late.sb("beta", [D])
        route_stage(nc, m)
        expert_stage(nc, m)
        combine_stage(nc, m)


_INS = ["x", "src", "dst", "edge_weight", "L0_gnn_weight_l", "L0_gnn_bias_l", "L0_gnn_weight_r", "L0_gnn_bias_r",
        "L0_mix_wq", "L0_mix_wk", "L0_mix_wv", "L0_mix_wo", "L0_mix_bo", "L0_mix_ln_k_g", "L0_mix_ln_k_b",
        "L0_mix_ln_v_g", "L0_mix_ln_v_b", "L0_ffn_gate_w", "L0_ffn_gate_b", "L0_ffn_w1", "L0_ffn_b1", "L0_ffn_w2",
        "L0_ffn_b2", "L0_ffn_gamma", "L0_ffn_beta"]


def kernel(**inputs):
    import concourse.bacc as _bacc
    from concourse.bass_utils import run_bass_kernel_spmd as _run

    nc = _bacc.Bacc("TRN2", target_bir_lowering=False, num_devices=1)
    arrays, args = {}, []
    feed = [(name, np.ascontiguousarray(inputs[name])) for name in _INS] + [("consts", constant_table())]
    for name, a in feed:
        arrays[f"in_{name}_dram"] = a
        args.append(nc.dram_tensor(f"in_{name}_dram", a.shape, mybir.dt.from_np(a.dtype), kind="ExternalInput").ap())
    args.append(nc.dram_tensor("out_0_dram", (N, D), F32, kind="ExternalOutput").ap())
    build(nc, *args)
    r = _run(nc, [arrays], core_ids=[0])
    return r.results[0]["out_0_dram"]
```

```python
from contextlib import ExitStack

import numpy as np

import concourse.bass as bass
from concourse import mybir

ALU = mybir.AluOpType
ACT = mybir.ActivationFunctionType
AX_X = mybir.AxisListType.X
F32 = mybir.dt.float32
I32 = mybir.dt.int32
U32 = mybir.dt.uint32
BF16 = mybir.dt.bfloat16
FP16 = mybir.dt.float16

P = 128
N = 3125
D = 256
DC = D // P
NT = -(-N // P)
TAIL = N - (NT - 1) * P
HEAD = 64
NE = 16
FF = 512
FC = FF // P
EPS = 1e-5

E = 50000
EP = 125
EC = E // EP
SUP = 2
TC = EC // SUP
NI = NT
SB = TC // NI
HB = SB // 2
NC = (EP * TC + NT * (P - 1)) // P
GB = -(-NC // NI)
REST = NC - (NI - 1) * GB
LAG = 3
BY_ACT = (2, 4, 7)
HALF = 2048.0
GBP = GB + -GB % 4
SHOW = {GB - HB - 3 + n: (0, n) for n in range(3)} | {GB - 3 + n: (1, n) for n in range(3)}
assert EP * EC == E and NI * SB == TC and 2 * HB == SB and NC <= 2 * P and GB >= 2 * HB and HB >= 3 and SUP == 2
assert LAG < REST < GB

TB = 5
TI = NT // TB
CAP = 3328
DUMMY = NE * CAP
TRASH = DUMMY + P
ZROWS = TRASH + 2 * P
MT = (2 * N + NE * (P - 1)) // P
MT += MT % 2

K_ID, K_TRI, K_ONE, K_CEN, K_MSK, K_IOTA = 0, 128, 256, 384, 512, 640
K_CAP, K_VAL, K_TR, K_COL, K_END = 896, 912, 912 + NT, 912 + 3 * NT, 914 + 3 * NT


def constant_table():
    p = np.arange(P)[:, None]
    q = np.arange(P)[None, :]
    same = p // HEAD == q // HEAD
    c = np.zeros((P, K_END), np.float32)
    c[:, K_ID:K_ID + P] = p == q
    c[:, K_TRI:K_TRI + P] = p < q
    c[:, K_ONE:K_ONE + P] = 1
    c[:, K_CEN:K_CEN + P] = (p == q) - same / HEAD
    c[:, K_MSK:K_MSK + P] = same
    c[:, K_IOTA:K_IOTA + 256] = np.arange(256)
    c[:, K_CAP:K_CAP + NE] = np.arange(NE) * CAP
    real = p + P * np.arange(NT)[None, :] < N
    c[:, K_VAL:K_VAL + NT] = real
    c[:, K_TR:K_TR + 2 * NT] = np.stack([(1 - real) * (TRASH + p), (1 - real) * (TRASH + P + p)], 2).reshape(P, 2 * NT)
    c[:, K_COL:K_COL + 2] = p + P * np.arange(2)
    return c


class Arena:

    def __init__(self, tensor, words, at=0):
        self.tensor, self.words, self.at = tensor, words, at

    def cut(self, shape, dt=F32):
        size = 2 if dt in (BF16, FP16) else 4
        n = int(np.prod(shape))
        words = -(-n * size // 4)
        assert self.at + words <= self.words, (self.at, words, self.words)
        v = self.tensor[:, self.at:self.at + words]
        self.at += words
        if dt != F32:
            v = v.bitcast(dt)
        v = v[:, 0:n]
        if len(shape) == 2:
            v = v.rearrange("p (a b) -> p a b", a=shape[0])
        elif len(shape) == 3:
            v = v.rearrange("p (a b c) -> p a b c", a=shape[0], b=shape[1])
        return v


def rounds(eng, n, body):
    body(0)
    with eng.Fori(1, n) as i:
        body(i)


def wait(eng, sem, value):
    if isinstance(value, int) and value <= 0:
        return
    eng.wait_ge(sem, value)


class Chain:

    def __init__(self, eng, sem):
        self.eng, self.sem, self.n, self.base = eng, sem, 0, 0

    def link(self, ins, apart=False):
        self.n += 1
        ins.then_inc(self.sem, 1)
        self.eng.wait_ge(self.sem, self.base + self.n)
        if apart:
            self.eng.nop(nofuse=True)

    def loop(self, start, end, per, body):
        first = self.n
        with self.eng.Fori(start, end) as i:
            self.base, self.n = (i - start) * per + first, 0
            body(i)
            assert self.n == per, (self.n, per)
        self.base, self.n = 0, first + (end - start) * per

    def rounds(self, n, per, body):
        body(0)
        self.loop(1, n, per, body)


def chunked(w):
    return w.rearrange("(c p) n -> p c n", p=P)


class Phase:

    def __init__(self, nc, ctx, tag):
        self.nc, self.ctx, self.tag, self.used = nc, ctx, tag, []
        ctx.callback(self.clear)

    def sb(self, name, shape, dt=F32):
        return self.ctx.enter_context(self.nc.sbuf_tensor(name, [P] + shape, dt))

    def sem(self, name):
        self.used.append(self.nc.alloc_semaphore(f"{self.tag}_{name}"))
        return self.used[-1]

    def clear(self):
        for used in self.used:
            self.nc.gpsimd.sem_clear(used)
            self.nc.release_semaphore(used)

    def sems(self, name, n):
        return [self.sem(f"{name}{k}") for k in range(n)]


def earlier(i, k, lag):
    k -= lag
    if k >= 0:
        return i, k
    return None if isinstance(i, int) and i == 0 else (i - 1, k + TB)


def since(k, slots):
    if k >= slots:
        return slots
    return TB - max(v for v in range(TB) if v % slots == k) + k


def last_use(u, slots, per_round):
    if u >= slots:
        return slots
    return per_round - max(v for v in range(per_round) if v % slots == u) + u


def prepare_stage(nc, m):
    with ExitStack() as ctx:
        ph = Phase(nc, ctx, "prepare")
        a = Arena(m.W2, NE * FC * D, m.xnT_words)
        onehot, running = a.cut([NT, TC], BF16), a.cut([NT, TC])
        a = Arena(m.W1, NE * DC * FF, m.small_words)
        wl = a.cut([DC, D])
        src_i, dst_i, t_i, u_i = (a.cut([EC], I32) for _ in range(4))
        ew_f, bucket = a.cut([EC]), a.cut([EC])
        ends, count, columns, base = a.cut([NT + 1]), a.cut([NT]), a.cut([NT]), a.cut([NT])
        cols_end = a.cut([SUP, NT])
        total_i, total_j = a.cut([NT], I32), a.cut([NT], I32)
        slot, slot_i, slot_j = a.cut([TC]), a.cut([TC], I32), a.cut([TC], I32)
        over, over_n = a.cut([2, NT]), a.cut([SUP, 2])
        st6, mv, rstd, shift, eps_x = a.cut([NT, 6]), a.cut([NT, 2]), a.cut([NT]), a.cut([NT]), a.cut([1])
        xn, xt, hs = a.cut([TB, D]), a.cut([TB, D]), a.cut([TB, D])
        names = ("consts edges x_loaded wl_loaded cleared stats var_ready rooted norm_ready xn_ready xt_psum xt_ready xt_kept "
                 "h_psum h_ready counted summed bucket_ready bucket_psum link extras prepared prep_read")
        s = {n: ph.sem(n) for n in names.split()}
        h_stored = ph.sems("h_stored", TB)
        prefix, total, b_bucket = m.bank[0][:, 0:NT], m.bank[1][:, 0:NT], m.bank[2:4]
        b_t, b_h = m.bank[4:6], m.bank[6:8]
        block = ctx.enter_context(nc.Block())

        @block.sync
        def _(sp):
            for to, of in ((src_i, m.src), (dst_i, m.dst), (ew_f, m.ew)):
                sp.dma_start(to[0:EP, :], of.rearrange("(p t) -> p t", p=EP)).then_inc(s["edges"], 16)
            sp.dma_start(m.C[:, :], m.consts).then_inc(s["consts"], 16)
            sp.wait_ge(s["cleared"], 1)
            per = TB * P
            for g in range(TI):
                rows = min(per, (N - g * per) // P * P)
                sp.dma_start(m.Y[:, g * TB:g * TB + rows // P, :],
                             m.x[g * per:g * per + rows, :].rearrange("(t p) d -> p t d", p=P)).then_inc(s["x_loaded"], 16)
            sp.dma_start(m.Y[0:TAIL, NT - 1, :], m.x[N - TAIL:N, :]).then_inc(s["x_loaded"], 16)

            def store(i, k):
                sp.wait_ge(s["h_ready"], i * TB + k + 1)
                sp.dma_start(m.h_table[bass.ds((i * TB + k) * P, P), :], hs[:, k, :]).then_inc(h_stored[k], 16)

            rounds(sp, TI, lambda i: [store(i, k) for k in range(TB)])
            for k in range(TB):
                sp.wait_ge(h_stored[k], 16 * TI)

        @block.gpsimd
        def _(pool):
            pool.wait_ge(s["edges"], 48)
            nc.gpsimd.tensor_copy(m.top_h[0:EP, :], ew_f[0:EP, :].bitcast(BF16).rearrange(
                "p (t two) -> p t two", two=2)[:, :, 1]).then_inc(s["extras"], 1)
            pool.wait_ge(s["consts"], 16)
            nc.gpsimd.tensor_copy(m.iota_t[:, :, :], m.iota[:, 0:NC].unsqueeze(2).to_broadcast([P, NC, HB])).then_inc(s["extras"], 1)

            def keep(i, k):
                t = i * TB + k
                pool.wait_ge(s["xt_ready"], t + 1)
                nc.gpsimd.tensor_copy(m.xnT[:, bass.ds(t, 1), :], xt[:, k:k + 1, :]).then_inc(s["xt_kept"], 1)

            rounds(pool, TI, lambda i: [keep(i, k) for k in range(TB)])
            pool.wait_ge(s["xt_kept"], NT)
            pool.wait_ge(s["extras"], 2)

        @block.scalar
        def _(act):
            A = nc.scalar
            act.dma_start(wl[:, :, :], chunked(m.wl)).then_inc(s["wl_loaded"], 16)
            for to, of in ((m.wk_sb, m.wk), (m.wv_sb, m.wv), (m.wo_sb, m.wo), (m.wq_sb, m.wq), (m.wr_sb, m.wr)):
                act.dma_start(to[:, :, :], chunked(of)).then_inc(m.w_loaded, 16)
            for to, of in ((m.kg_sb, m.kg), (m.kb_sb, m.kb)):
                act.dma_start(to[:, :], of.unsqueeze(0).to_broadcast([P, HEAD])).then_inc(m.w_loaded, 16)
            for to, of in ((m.vg_sb, m.vg), (m.vb_sb, m.vb)):
                for half in range(2):
                    act.dma_start(to[half * HEAD:(half + 1) * HEAD, :], of.unsqueeze(1)).then_inc(m.w_loaded, 16)
            for t, of in enumerate((m.bl, m.br, m.bo)):
                act.dma_start(m.biases[:, t, :], of.unsqueeze(0).to_broadcast([P, D])).then_inc(m.w_loaded, 16)
            act.wait_ge(s["var_ready"], 2)
            A.activation(rstd[:, :], mv[:, :, 1], ACT.Sqrt, bias=eps_x[:, :]).then_inc(s["rooted"], 1)

            def normalise(i, k):
                t = i * TB + k
                wait(act, s["xt_psum"], t - TB + 1)
                A.activation(xn[:, k:k + 1, :], m.Y[:, bass.ds(t, 1), :], ACT.Identity, bias=shift[:, bass.ds(t, 1)],
                             scale=rstd[:, bass.ds(t, 1)]).then_inc(s["xn_ready"], 1)

            def copy_t(i, k):
                t = i * TB + k
                act.wait_ge(s["xt_psum"], t + 1)
                wait(act, s["h_psum"], t - TB + 1)
                wait(act, s["xt_kept"], t - TB + 1)
                A.copy(xt[:, k, :], b_t[k % 2][:, 0:D]).then_inc(s["xt_ready"], 1)

            def copy_h(i, k):
                t = i * TB + k
                act.wait_ge(s["h_psum"], t + 1)
                wait(act, h_stored[k], i * 16)
                A.copy(hs[:, k, :], b_h[k % 2][:, 0:D]).then_inc(s["h_ready"], 1)

            def body(i):
                for k in range(TB):
                    normalise(i, k)
                    if before := earlier(i, k, 1):
                        copy_t(*before)
                    if before := earlier(i, k, 2):
                        copy_h(*before)

            act.wait_ge(s["norm_ready"], 1)
            rounds(act, TI, body)
            copy_t(TI - 1, TB - 1)
            copy_h(TI - 1, TB - 2)
            copy_h(TI - 1, TB - 1)
            act.wait_ge(s["prepared"], 1)
            A.copy(m.wkv[:, 0, :], m.bank[6][:, :]).then_inc(s["prep_read"], 1)
            A.copy(m.wkv[:, 1, :], m.bank[7][:, :]).then_inc(s["prep_read"], 1)
            A.copy(m.woT[:, :, :], m.bank[5][:, :].rearrange("p (c d) -> p c d", c=DC)).then_inc(s["prep_read"], 1)
            act.wait_ge(s["prep_read"], 3)

        @block.tensor
        def _(pe):
            T = nc.tensor

            def sum_counts(part):
                pe.wait_ge(s["counted"], part + 1)
                T.matmul(prefix, m.tri[0:EP, :], count[0:EP, :], start=True, stop=True)
                T.matmul(total, m.ones[0:EP, :], count[0:EP, :], start=True, stop=True).then_inc(s["summed"], 1)

            def turn_buckets(part):
                pe.wait_ge(s["bucket_ready"], part + 1)
                for half in range(2):
                    last = T.transpose(b_bucket[part][0:1, half * P:(half + 1) * P], over_n[:, part, half:half + 1], m.ident)
                last.then_inc(s["bucket_psum"], 1)

            def turn(i, k):
                t = i * TB + k
                pe.wait_ge(s["xn_ready"], t + 1)
                wait(pe, s["xt_ready"], t - since(k, 2) + 1)
                for c in range(DC):
                    last = T.transpose(b_t[k % 2][:, c * P:(c + 1) * P], xn[:, k, c * P:(c + 1) * P], m.ident)
                last.then_inc(s["xt_psum"], 1)

            def project(i, k):
                t = i * TB + k
                pe.wait_ge(s["xt_ready"], t + 1)
                wait(pe, s["h_ready"], t - since(k, 2) + 1)
                for c in range(DC):
                    last = T.matmul(b_h[k % 2][:, 0:D], xt[:, k, c * P:(c + 1) * P], wl[:, c, :],
                                    start=(c == 0), stop=(c == DC - 1))
                last.then_inc(s["h_psum"], 1)

            def body(i):
                for k in range(TB):
                    turn(i, k)
                    if before := earlier(i, k, 1):
                        project(*before)

            pe.wait_ge(s["consts"], 16)
            sum_counts(0)
            pe.wait_ge(s["wl_loaded"], 16)
            body(0)
            with pe.Fori(1, TI - 1) as i:
                body(i)
            sum_counts(1)
            body(TI - 1)
            project(TI - 1, TB - 1)
            turn_buckets(0)
            pe.wait_ge(m.w_loaded, m.w_total)
            pe.wait_ge(s["xt_ready"], NT)
            pe.wait_ge(s["h_ready"], NT)
            for c in range(DC):
                for half, w in enumerate((m.wk_sb, m.wv_sb)):
                    for h in range(DC):
                        T.matmul(m.bank[6 + c][:, half * D + h * P:half * D + (h + 1) * P],
                                 w[:, h, c * P:(c + 1) * P], m.center, start=True, stop=True)
            for o in range(DC):
                for c in range(DC):
                    last = T.transpose(m.bank[5][:, c * D + o * P:c * D + (o + 1) * P],
                                       m.wo_sb[:, o, c * P:(c + 1) * P], m.ident)
            last.then_inc(s["prepared"], 1)
            turn_buckets(1)

        @block.vector
        def _(dve):
            c = Chain(dve, s["link"])
            V = nc.vector
            e = slice(0, EP)
            V.memset(m.Y[:, NT - 1, :], 0.0).then_inc(s["cleared"], 1)
            V.memset(m.zero_h[:, :], 0.0)
            V.memset(eps_x[:, :], EPS).then_inc(s["var_ready"], 1)
            dve.wait_ge(s["edges"], 48)
            c.link(V.tensor_scalar(u_i[e, :], src_i[e, :], 7, None, ALU.logical_shift_right))
            c.link(V.tensor_copy(bucket[e, :], u_i[e, :]))
            c.link(V.memset(ends[:, :], 0.0))
            dve.wait_ge(s["consts"], 16)

            def count_part(part):
                t = slice(part * TC, (part + 1) * TC)
                c.link(V.tensor_tensor(onehot[e, :, :], bucket[e, t].unsqueeze(1).to_broadcast([EP, NT, TC]),
                                       m.iota[e, 0:NT].unsqueeze(2).to_broadcast([EP, NT, TC]), ALU.is_equal))
                flat = onehot[e, :, :].rearrange("p b t -> p (b t)")
                c.link(V.tensor_tensor_scan(running[e, :, :].rearrange("p b t -> p (b t)"), flat, flat, 0.0,
                                            ALU.add, ALU.max))
                c.link(V.tensor_copy(ends[e, 1:NT + 1], running[e, :, TC - 1]))
                V.tensor_tensor(count[e, :], ends[e, 1:NT + 1], ends[e, 0:NT], ALU.subtract).then_inc(s["counted"], 1)

            def place_part(part):
                t = slice(part * TC, (part + 1) * TC)
                dve.wait_ge(s["summed"], part + 1)
                c.link(V.tensor_scalar(total_i[:, :], total, float(P - 1), None, ALU.add))
                c.link(V.tensor_scalar(total_j[:, :], total_i[:, :], 7, None, ALU.logical_shift_right))
                c.link(V.tensor_copy(columns[:, :], total_j[:, :]))
                c.link(V.tensor_tensor_scan(cols_end[:, part, :], columns[:, :], columns[:, :], 0.0, ALU.add, ALU.max))
                c.link(V.tensor_tensor(base[e, :], cols_end[e, part, :], columns[e, :], ALU.subtract))
                c.link(V.scalar_tensor_tensor(base[e, :], base[e, :], float(P), prefix[e, :], ALU.mult, ALU.add))
                c.link(V.scalar_tensor_tensor(base[e, :], base[e, :], 1.0, ends[e, 0:NT], ALU.subtract, ALU.subtract))
                c.link(V.tensor_tensor(running[e, :, :], running[e, :, :],
                                       base[e, :].unsqueeze(2).to_broadcast([EP, NT, TC]), ALU.add))
                c.link(V.tensor_tensor(running[e, :, :], running[e, :, :], onehot[e, :, :], ALU.mult))
                c.link(V.tensor_reduce(slot[e, :], running[e, :, :].rearrange("p b t -> p t b"), AX_X, ALU.add))
                c.link(V.tensor_copy(slot_i[e, :], slot[e, :]))
                c.link(V.tensor_scalar(slot_j[e, :], slot_i[e, :], P - 1, None, ALU.bitwise_and))
                c.link(V.tensor_copy(m.row_of[e, t], slot_j[e, :]))
                c.link(V.tensor_scalar(slot_j[e, :], slot_i[e, :], 7, None, ALU.logical_shift_right))
                c.link(V.tensor_copy(m.col_of[e, t], slot_j[e, :]))
                c.link(V.tensor_tensor(over[:, :, :], cols_end[:, part, :].unsqueeze(1).to_broadcast([P, 2, NT]),
                                       m.C[:, K_COL:K_COL + 2].unsqueeze(2).to_broadcast([P, 2, NT]), ALU.is_le))
                c.link(V.tensor_reduce(over_n[:, part, :], over[:, :, :], AX_X, ALU.add))
                V.tensor_scalar(over_n[:, part, :], over_n[:, part, :], float(NT - 1), None,
                                ALU.min).then_inc(s["bucket_ready"], 1)

            def stats(i, k):
                t = i * TB + k
                V.bn_stats(st6[:, bass.ds(t, 1), :].rearrange("p a d -> p (a d)"),
                           m.Y[:, bass.ds(t, 1), :].rearrange("p a d -> p (a d)")).then_inc(s["stats"], 1)

            count_part(0)
            dve.wait_ge(s["x_loaded"], 16 * (TI + 1))
            rounds(dve, TI, lambda i: [stats(i, k) for k in range(TB)])
            dve.wait_ge(s["stats"], NT)
            for t in range(NT):
                last = V.bn_aggr(mv[:, t, :], st6[:, t, :])
            last.then_inc(s["var_ready"], 1)
            c.link(V.tensor_scalar(m.code_h[e, 0, :], dst_i[e, :], HALF, None, ALU.subtract))
            ew_i = ew_f[e, :].bitcast(I32)
            dve.wait_ge(s["rooted"], 1)
            c.link(V.reciprocal(rstd[:, :], rstd[:, :]))
            V.scalar_tensor_tensor(shift[:, :], mv[:, :, 0], -1.0, rstd[:, :], ALU.mult, ALU.mult).then_inc(s["norm_ready"], 1)
            place_part(0)
            V.tensor_scalar(t_i[e, :], ew_i, 31, None, ALU.bitwise_and)
            c.link(V.tensor_scalar(u_i[e, :], src_i[e, :], P - 1, 5, ALU.bitwise_and, ALU.logical_shift_left))
            c.link(V.tensor_tensor(t_i[e, :], t_i[e, :], u_i[e, :], ALU.bitwise_or))
            V.tensor_scalar(m.code_h[e, 1, :], t_i[e, :], HALF, None, ALU.subtract)
            c.link(V.tensor_scalar(u_i[e, :], ew_i, 5, 2047, ALU.logical_shift_right, ALU.bitwise_and))
            c.link(V.tensor_copy(m.code_h[e, 2, :], u_i[e, :]))
            count_part(1)
            place_part(1)
            for part in range(SUP):
                dve.wait_ge(s["bucket_psum"], part + 1)
                c.link(V.tensor_copy(m.bucket_i[0:1, part, :, 0:GB],
                                     b_bucket[part][0:1, 0:NI * GB].rearrange("p (i u) -> p i u", u=GB)))


def edge_stage(nc, m):
    with ExitStack() as ctx:
        ph = Phase(nc, ctx, "edge")
        a = Arena(m.W1, NE * DC * FF, m.small_words)
        mixed = a.cut([DC, D])
        kvT, t1, t2, vsum = a.cut([DC, P]), a.cut([DC, P]), a.cut([DC, P]), a.cut([DC])
        eps_kv, bias = a.cut([1]), a.cut([D])
        squares, kv = a.cut([2 * D]), a.cut([2 * D])
        ssum, root, rs = a.cut([8]), a.cut([8]), a.cut([8])
        xt, weff = ph.sb("xn_tile", [D]), ph.sb("mixed_weight", [DC, D])
        target, pair = ph.sb("slot_target", [SUP, NC], I32), ph.sb("slot_place_weight", [SUP, NC, 2])
        code, bits = ph.sb("slot_code", [3, NC], I32), ph.sb("slot_bits", [2, NC], I32)
        columns, row_1 = ph.sb("onehot_col", [2, NC, HB], BF16), ph.sb("onehot_row", [P, HB], BF16)
        row_c, row_w = ph.sb("row_code", [2, 3, P, HB], FP16), ph.sb("row_weight", [2, P, HB], BF16)
        spread, fetched = ph.sb("spread", [GB, P]), ph.sb("fetched", [GB, D])
        index, now = ph.sb("fetch_index", [GB], I32), ph.sb("now_place_weight", [GB, 2])
        names = ("placed shown closed table link mix_added w1_in xt_ready kv_psum squared "
                 "reduced kv_rooted kv_ready kv_used kv_folded mixed_psum mixed_ready weff_psum weff_ready again mix_psum "
                 "eps_ready act_link bias_link bias_added")
        s = {n: ph.sem(n) for n in names.split()}
        staged, paired, landed = ph.sems("staged", GB), ph.sems("paired", GB), ph.sems("landed", GB)
        spreads, used, added = ph.sems("spread_ready", GB), ph.sems("used", GB), ph.sems("added", GB)
        def steps(i):
            return REST if isinstance(i, int) and i == NI - 1 else GB

        def count(part, i, u):
            return part * (NI if u < REST else NI - 1) + i + 1

        def columns_of(eng, part, body):
            body(part, 0)
            with eng.Fori(1, NI - 1) as i:
                body(part, i)
            body(part, NI - 1)

        place_of = [m.bank[j // 2][:, (j % 2) * 256:(j % 2) * 256 + NC] for j in range(4)]
        b_kv, b_acc, b_ks, b_add = m.bank[3], m.bank[4], m.bank[5], m.bank[3:8]
        MIX = 4
        b_mix = b_add[MIX]
        block = ctx.enter_context(nc.Block())

        @block.sync
        def _(sp):
            sp.wait_ge(s["weff_ready"], 1)
            sp.wait_ge(s["bias_added"], 1)
            for e in range(NE):
                sp.dma_start(m.w1_sb[:, e, :, :], m.w1[e].rearrange("(c p) f -> p c f", p=P)).then_inc(s["w1_in"], 16)
            sp.wait_ge(s["w1_in"], 16 * NE)

        @block.gpsimd
        def _(pool):
            pool.wait_ge(m.w_loaded, m.w_total)
            nc.gpsimd.tensor_tensor(bias[:, :], m.biases[:, 0, :], m.biases[:, 1, :], ALU.add).then_inc(s["bias_link"], 1)
            pool.wait_ge(s["bias_link"], 1)
            nc.gpsimd.tensor_tensor(bias[:, :], bias[:, :], m.biases[:, 2, :], ALU.add).then_inc(s["bias_link"], 1)
            pool.wait_ge(s["bias_link"], 2)
            nc.gpsimd.tensor_tensor(m.Y[:, :, :], m.Y[:, :, :], bias[:, :].unsqueeze(1).to_broadcast([P, NT, D]),
                                    ALU.add).then_inc(s["bias_added"], 1)
            def fetch(part, i):
                for u in range(steps(i)):
                    pool.wait_ge(staged[u], count(part, i, u))
                    pool.nop(nofuse=True)
                    nc.gpsimd.indirect_dma_start(fetched[:, u, :], None, m.h_table,
                                                 bass.IndirectOffsetOnAxis(ap=index[:, u:u + 1], axis=0)).then_inc(landed[u], 16)

            for part in range(SUP):
                columns_of(pool, part, fetch)

        @block.scalar
        def _(act):
            A = nc.scalar
            c = Chain(act, s["act_link"])

            def take_root(i):
                act.wait_ge(s["reduced"], i + 1)
                A.activation(root[:, :], ssum[:, :], ACT.Sqrt, bias=eps_kv[:, :]).then_inc(s["kv_rooted"], 1)

            def keys(i):
                wait(act, s["kv_psum"], i)
                A.copy(xt[:, :].unsqueeze(1), m.xnT[:, bass.ds(i, 1), :]).then_inc(s["xt_ready"], 1)
                act.wait_ge(s["kv_psum"], i + 1)
                A.activation(squares[:, :], b_kv[:, :], ACT.Square).then_inc(s["squared"], 1)
                take_root(i)

            act.wait_ge(s["eps_ready"], 1)
            rounds(act, NT, keys)

            def stage(part, i):
                for u in range(steps(i)):
                    wait(act, used[u], count(part, i, u) - 1)
                    A.copy(index[:, u:u + 1], target[:, part, bass.ds(i * GB + u, 1)]).then_inc(staged[u], 1)
                    if u in BY_ACT:
                        row = spread[:, u, :]
                        c.link(A.activation(row, m.iota[:, 0:P], ACT.Square, scale=-1.0,
                                            bias=pair[:, part, bass.ds(i * GB + u, 1), 0]))
                        c.link(A.activation(row, row, ACT.Relu, scale=-1.0, bias=m.ones[:, 0:1]))
                        A.activation(row, row, ACT.Copy,
                                     scale=pair[:, part, bass.ds(i * GB + u, 1), 1]).then_inc(spreads[u], 1)
                    else:
                        A.copy(now[:, u:u + 1, :], pair[:, part, bass.ds(i * GB + u, 1), :]).then_inc(paired[u], 1)

            def again(i):
                wait(act, s["mix_psum"], i)
                A.copy(xt[:, :].unsqueeze(1), m.xnT[:, bass.ds(i, 1), :]).then_inc(s["again"], 1)

            act.wait_ge(s["table"], 1)
            stage(0, 0)
            act.wait_ge(s["mixed_psum"], 1)
            A.activation(mixed[:, :, :], m.bank[6][:, :].rearrange("p (c d) -> p c d", c=DC), ACT.Copy,
                         scale=1.0 / N).then_inc(s["mixed_ready"], 1)
            c.loop(1, NI - 1, 2 * len(BY_ACT), lambda i: stage(0, i))
            stage(0, NI - 1)

            def second(i):
                stage(1, i)
                again(i)

            act.wait_ge(s["table"], 2)
            second(0)
            c.loop(1, NI - 1, 2 * len(BY_ACT), second)
            second(NI - 1)

        @block.tensor
        def _(pe):
            T = nc.tensor

            def zero(start, stop):
                for b in range(2):
                    last = T.matmul(m.bank[b][:, :], m.zero_h[:, 0:P], m.zero_h[:, :], start=start, stop=stop)
                return last

            def place_column(part, i, h, n):
                if n == 0:
                    pe.wait_ge(s["shown"], (part * NI + i) * 2 + h + 1)
                for j in range(4):
                    row = row_c[0:EP, h, j, :, n] if j < 3 else row_w[0:EP, h, :, n]
                    last = T.matmul(place_of[j], row, columns[0:EP, h, :, n], start=False, stop=False)
                if n == HB - 1:
                    last.then_inc(s["placed"], 1)

            def place_batch(part, i, h):
                for n in range(HB):
                    place_column(part, i, h, n)

            def keys(i):
                pe.wait_ge(s["xt_ready"], i + 1)
                wait(pe, s["kv_ready"], i)
                for c in range(DC):
                    last = T.matmul(b_kv[:, :], xt[:, c * P:(c + 1) * P], m.wkv[:, c, :], start=(c == 0), stop=(c == DC - 1))
                last.then_inc(s["kv_psum"], 1)

            def accumulate(i, rows=P):
                pe.wait_ge(s["kv_ready"], i + 1)
                done = rows != P
                slot = kv[0:rows, :]
                for c in range(DC):
                    v = slot[:, D + c * P:D + (c + 1) * P]
                    T.matmul(b_acc[:, c * P:(c + 1) * P], v, slot[:, c * P:(c + 1) * P], start=False, stop=False)
                    T.matmul(b_acc[:, D + c:D + c + 1], v, m.ones[0:rows, 0:1], start=False,
                             stop=done and c == DC - 1)
                T.matmul(b_ks[:, 0:D], m.ones[0:rows, :], slot[:, 0:D], start=False, stop=done).then_inc(s["kv_used"], 1)

            def mix(i):
                pe.wait_ge(s["again"], i + 1)
                if steps(i) > MIX:
                    pe.wait_ge(added[MIX], count(1, i, MIX))
                else:
                    pe.wait_ge(s["mix_added"], i)
                for c in range(DC):
                    last = T.matmul(b_mix[:, 0:D], xt[:, c * P:(c + 1) * P], weff[:, c, :], start=(c == 0), stop=(c == DC - 1))
                last.then_inc(s["mix_psum"], 1)

            def spread_column(part, i, u):
                v = count(part, i, u)
                pe.wait_ge(landed[u], v * 16)
                pe.wait_ge(spreads[u], v)
                back = last_use(u, 5, GB)
                if u == MIX and part == 1 and not (isinstance(i, int) and i == 0):
                    pe.wait_ge(s["mix_added"], i)
                elif u >= back:
                    pe.wait_ge(added[u - back], count(part, i, u - back))
                elif part == 1 and isinstance(i, int) and i == 0 and u < REST:
                    pe.wait_ge(added[u], NI)
                else:
                    wait(pe, added[u - back + GB], count(part, i, u - back + GB) - 1)
                T.matmul(b_add[u % 5][:, 0:D], spread[:, u, :], fetched[:, u, :], start=True,
                         stop=True).then_inc(used[u], 1)

            zero(True, False)
            T.matmul(b_acc[:, :], m.zero_h[:, 0:P], m.zero_h[:, :], start=True, stop=False)
            T.matmul(b_ks[:, :], m.zero_h[:, 0:P], m.zero_h[:, :], start=True, stop=False)

            def first(i):
                keys(i)
                place_batch(0, i, 0)
                if not (isinstance(i, int) and i == 0):
                    accumulate(i - 1)
                place_batch(0, i, 1)

            rounds(pe, NI, first)
            zero(False, True).then_inc(s["closed"], 1)
            accumulate(NT - 1, TAIL)
            pe.wait_ge(s["kv_folded"], 1)
            for c in range(DC):
                last = T.matmul(m.bank[6][:, c * D:(c + 1) * D], kvT[:, c, :], m.woT[:, c, :], start=True, stop=True)
            last.then_inc(s["mixed_psum"], 1)
            pe.wait_ge(s["table"], 1)
            zero(True, False)
            place_batch(1, 0, 0)
            pe.wait_ge(s["mixed_ready"], 1)

            def body(part, i):
                last = isinstance(i, int) and i == NI - 1
                if part == 0 and last:
                    place_batch(1, i, 1)
                    zero(False, True).then_inc(s["closed"], 1)
                for u in range(steps(i)):
                    spread_column(part, i, u)
                    if part == 0 and not last and u < HB:
                        place_column(1, i, 1, u)
                    elif part == 0 and not last and u >= GB - HB:
                        place_column(1, i + 1, 0, u - (GB - HB))
                if part == 1:
                    mix(i)

            body(0, 0)
            pe.wait_ge(added[MIX], 1)
            for o in range(DC):
                for c in range(DC):
                    last = T.matmul(m.bank[7][:, o * D:(o + 1) * D], m.wq_sb[:, c, o * P:(o + 1) * P], mixed[:, c, :],
                                    start=(c == 0), stop=(c == DC - 1))
            last.then_inc(s["weff_psum"], 1)
            pe.wait_ge(s["weff_ready"], 1)
            with pe.Fori(1, NI - 1) as i:
                body(0, i)
            body(0, NI - 1)
            columns_of(pe, 1, body)

        @block.vector
        def _(dve):
            V = nc.vector
            c = Chain(dve, s["link"])
            e = slice(0, EP)
            V.memset(eps_kv[:, :], HEAD * EPS).then_inc(s["eps_ready"], 1)

            def show_places(part, i, h):
                t = part * TC + i * SB + h * HB
                no = (part * NI + i) * 2 + h
                wait(dve, s["placed"], no - 1)
                V.tensor_tensor(columns[e, h, :, :], m.iota_t[e, :, :],
                                m.col_of[e, bass.ds(t, HB)].unsqueeze(1).to_broadcast([EP, NC, HB]), ALU.is_equal)
                wait(dve, s["shown"], no)
                c.link(V.tensor_tensor(row_1[e, :, :], m.iota_t[e, 0:P, :],
                                       m.row_of[e, bass.ds(t, HB)].unsqueeze(1).to_broadcast([EP, P, HB]), ALU.is_equal))

            def show_codes(part, i, h):
                t = part * TC + i * SB + h * HB
                V.tensor_tensor(row_c[e, h, :, :, :], row_1[e, :, :].unsqueeze(1).to_broadcast([EP, 3, P, HB]),
                                m.code_h[e, :, bass.ds(t, HB)].unsqueeze(2).to_broadcast([EP, 3, P, HB]), ALU.mult)

            def show_weights(part, i, h):
                t = part * TC + i * SB + h * HB
                V.tensor_tensor(row_w[e, h, :, :], row_1[e, :, :], m.top_h[e, bass.ds(t, HB)].unsqueeze(1).to_broadcast([EP, P, HB]),
                                ALU.mult).then_inc(s["shown"], 1)

            def read_table(part):
                dve.wait_ge(s["closed"], part + 1)
                V.tensor_scalar(target[:, part, :], place_of[0], HALF, None, ALU.add)
                V.tensor_scalar(code[:, 0, :], place_of[1], HALF, None, ALU.add)
                V.tensor_copy(code[:, 1, :], place_of[2])
                c.link(V.tensor_copy(code[:, 2, :].bitcast(F32), place_of[3]))
                V.tensor_scalar(bits[:, 0, :], code[:, 1, :], 5, None, ALU.logical_shift_left)
                V.tensor_scalar(bits[:, 1, :], code[:, 0, :], 31, None, ALU.bitwise_and)
                c.link(V.tensor_scalar(code[:, 0, :], code[:, 0, :], 5, None, ALU.logical_shift_right))
                V.tensor_copy(pair[:, part, :, 0], code[:, 0, :])
                c.link(V.tensor_tensor(bits[:, 0, :], bits[:, 0, :], bits[:, 1, :], ALU.bitwise_or))
                V.tensor_tensor(pair[:, part, :, 1].bitcast(I32), bits[:, 0, :], code[:, 2, :],
                                ALU.bitwise_or).then_inc(s["table"], 1)
                dve.wait_ge(s["table"], part + 1)

            def reduce_kv(i):
                dve.wait_ge(s["squared"], i + 1)
                wait(dve, s["kv_rooted"], i)
                V.tensor_reduce(ssum[:, :], squares[:, :].rearrange("p (h d) -> p h d", d=HEAD), AX_X,
                                ALU.add).then_inc(s["reduced"], 1)

            def scale_kv(i):
                dve.wait_ge(s["kv_rooted"], i + 1)
                c.link(V.reciprocal(rs[:, :], root[:, :]))
                wait(dve, s["kv_used"], i)
                V.scalar_tensor_tensor(kv[:, :].rearrange("p (h d) -> p h d", d=HEAD),
                                       b_kv[:, :].rearrange("p (h d) -> p h d", d=HEAD), float(HEAD) ** 0.5,
                                       rs[:, :].unsqueeze(2).to_broadcast([P, 8, HEAD]),
                                       ALU.mult, ALU.mult).then_inc(s["kv_ready"], 1)

            def first(i):
                show_places(0, i, 0)
                if not (isinstance(i, int) and i == 0):
                    scale_kv(i - 1)
                show_codes(0, i, 0)
                show_weights(0, i, 0)
                show_places(0, i, 1)
                show_codes(0, i, 1)
                show_weights(0, i, 1)
                reduce_kv(i)

            c.rounds(NI, 3, first)
            scale_kv(NT - 1)
            read_table(0)

            dve.wait_ge(s["kv_used"], NT)
            dve.wait_ge(m.w_loaded, m.w_total)
            heads = lambda v: v.rearrange("p (h d) -> p h d", d=HEAD)
            kg2, kb2 = (v[:, :].unsqueeze(1).to_broadcast([P, 2, HEAD]) for v in (m.kg_sb, m.kb_sb))
            vg, vb = m.vg_sb, m.vb_sb
            c.link(V.tensor_copy(vsum[:, :], b_acc[:, D:D + DC]))
            for h in range(DC):
                c.link(V.tensor_tensor(heads(t1[:, h, :]), heads(b_acc[:, h * P:(h + 1) * P]), kg2, ALU.mult))
                c.link(V.scalar_tensor_tensor(heads(t1[:, h, :]), kb2, vsum[:, h:h + 1], heads(t1[:, h, :]), ALU.mult, ALU.add))
                c.link(V.tensor_tensor(heads(t2[:, h, :]), heads(b_ks[:, h * P:(h + 1) * P]), kg2, ALU.mult))
                c.link(V.scalar_tensor_tensor(heads(t2[:, h, :]), kb2, float(N), heads(t2[:, h, :]), ALU.mult, ALU.add))
                c.link(V.tensor_scalar(t2[:, h, :], t2[:, h, :], vb[:, :], None, ALU.mult))
                c.link(V.scalar_tensor_tensor(t1[:, h, :], t1[:, h, :], vg[:, :], t2[:, h, :], ALU.mult, ALU.add))
                last = V.tensor_tensor(kvT[:, h, :], t1[:, h, :], m.mask, ALU.mult)
            last.then_inc(s["kv_folded"], 1)
            for h in range(2):
                for show in (show_places, show_codes, show_weights):
                    show(1, 0, h)
            dve.wait_ge(s["bias_added"], 1)

            buckets = [dve.alloc_register(f"bucket{u}") for u in range(GB)]

            def spread_weights(part, i, u):
                dve.wait_ge(paired[u], count(part, i, u))
                V.tensor_scalar(spread[:, u, :], m.iota[:, 0:P], now[:, u, 0:1], now[:, u, 1:2],
                                ALU.is_equal, ALU.mult).then_inc(spreads[u], 1)

            def bucket_of(u):
                return dve.snap(buckets[u], min_val=0, max_val=NT - 1)

            def add(part, i, u, bucket):
                dve.wait_ge(used[u], count(part, i, u))
                if u:
                    dve.wait_ge(added[u - 1], count(part, i, u - 1))
                elif not (isinstance(i, int) and i == 0):
                    dve.wait_ge(*((s["mix_added"], i) if part == 1 else (added[GB - 1], i)))
                elif part == 1:
                    dve.wait_ge(added[REST - 1], NI)
                tile = m.Y[:, bass.ds(bucket, 1), :]
                V.tensor_tensor(tile, tile, b_add[u % 5][:, 0:D].unsqueeze(1), ALU.add).then_inc(added[u], 1)

            def add_mix(i):
                dve.wait_ge(s["mix_psum"], i + 1)
                dve.wait_ge(added[steps(i) - 1], count(1, i, steps(i) - 1))
                tile = m.Y[:, bass.ds(i, 1), :]
                V.tensor_tensor(tile, tile, b_mix[:, 0:D].unsqueeze(1), ALU.add).then_inc(s["mix_added"], 1)

            def body(part, i):
                last = isinstance(i, int) and i == NI - 1
                for u in range(steps(i)):
                    if u == LAG:
                        dve.load(buckets, m.bucket_i[0:1, part, bass.ds(i, 1), 0:GB].rearrange("p a u -> p (a u)"))
                    bucket = bucket_of((u - LAG) % GB)
                    if u not in BY_ACT:
                        spread_weights(part, i, u)
                    if part == 0 and u in SHOW and not last:
                        h, n = SHOW[u]
                        (show_places, show_codes, show_weights)[n](1, i + 1, h)
                    if u >= LAG:
                        add(part, i, u - LAG, bucket)
                    elif not (isinstance(i, int) and i == 0):
                        add(part, i - 1, u - LAG + GB, bucket)
                        if part == 1 and u == LAG - 1:
                            add_mix(i - 1)
                    if part == 0 and last and u == 0:
                        read_table(1)

            def finish(part):
                for u in range(REST - LAG, REST):
                    add(part, NI - 1, u, bucket_of(u))

            body(0, 0)
            dve.wait_ge(s["weff_psum"], 1)
            V.tensor_tensor(weff[:, :, :], m.bank[7][:, :].rearrange("p (c d) -> p c d", c=DC), m.wr_sb[:, :, :],
                            ALU.add).then_inc(s["weff_ready"], 1)
            c.loop(1, NI - 1, 2, lambda i: body(0, i))
            body(0, NI - 1)
            finish(0)
            columns_of(dve, 1, body)
            finish(1)
            add_mix(NI - 1)
            dve.wait_ge(s["mix_added"], NI)


def route_stage(nc, m):
    with ExitStack() as ctx:
        ph = Phase(nc, ctx, "route")
        gate, gate_b = ph.sb("gate_w", [DC, NE]), ph.sb("gate_b", [NE])
        st6, mv, rstd, eps = ph.sb("rt_stats", [TB, 6]), ph.sb("rt_mean_var", [TB, 2]), ph.sb("rt_rstd", [NT]), ph.sb("rt_eps", [1])
        root = ph.sb("rt_root", [TB])
        shift_x, zs, zT = ph.sb("rt_shift", [NT]), ph.sb("z_slots", [3, D]), ph.sb("zT_slots", [2, D])
        logit, top, top_at = ph.sb("logits", [TB, NE]), ph.sb("top8", [TB, 8]), ph.sb("top8_at", [TB, 8], U32)
        top_f, chosen = ph.sb("top_f", [TB, 2]), ph.sb("chosen", [NT, 2, NE])
        both, seen = ph.sb("both_onehots", [TB, NE], BF16), ph.sb("seen", [NE], BF16)
        tri_h, ones_h = ph.sb("tri_bf16", [P], BF16), ph.sb("ones_bf16", [P], BF16)
        new, pos, pick = ph.sb("newly_seen", [NE]), ph.sb("positions", [TB, NE]), ph.sb("picked", [TB, 2, NE])
        row_i = ph.sb("scatter_row", [NT, 2], I32)
        b1_rows, zeros = ph.sb("b1_rows", [P]), ph.sb("zeros", [D])
        n_i, n_j, n_f, tiles = ph.sb("n_i", [NE], I32), ph.sb("n_j", [NE], I32), ph.sb("n_f", [NE]), ph.sb("tiles", [NE])
        tile_end, shift = ph.sb("tile_end", [NE]), ph.sb("region_shift", [NE])
        over, ex_f, row_f, valid = ph.sb("over", [MT, NE]), ph.sb("expert_f", [MT]), ph.sb("row_f", [MT]), ph.sb("valid", [MT])
        pad_i = ph.sb("pad_row", [NE], I32)
        fid, ex2 = ph.sb("fetch_f", [NT, 2]), ph.sb("exp_gap", [NT])
        picked2 = over[:, 0:2 * NT, :]
        names = ("params w2_in var_ready rooted link cleared norm_ready z_ready zT_psum zT_ready z_kept logit_psum logit_read "
                 "both_ready rank_psum seen_ready rows_ready scattered b1_psum counts_ready counts pads_ready pads gap_ready gap_exp")
        s = {n: ph.sem(n) for n in names.split()}
        b_t, b_l, b_r, b_b, b_n = m.bank[0:2], m.bank[2], m.bank[3], m.bank[6], m.bank[7]
        block = ctx.enter_context(nc.Block())

        @block.sync
        def _(sp):
            sp.dma_start(gate[:, :, :], m.gate_w.rearrange("(c p) e -> p c e", p=P)).then_inc(s["params"], 16)
            sp.dma_start(gate_b[:, :], m.gate_b.unsqueeze(0).to_broadcast([P, NE])).then_inc(s["params"], 16)
            sp.dma_start(b1_rows[0:NE * FC, :], m.b1.rearrange("e (c f) -> (e c) f", f=P)).then_inc(s["params"], 16)
            sp.dma_start(m.b2_rows[0:NE, :], m.b2).then_inc(s["params"], 16)
            sp.dma_start(m.gamma_b[:, :], m.gamma.unsqueeze(0).to_broadcast([P, D])).then_inc(s["params"], 16)
            sp.dma_start(m.beta_b[:, :], m.beta.unsqueeze(0).to_broadcast([P, D])).then_inc(s["params"], 16)
            for e in range(NE):
                sp.dma_start(m.w2_sb[:, e, :, :], m.w2[e].rearrange("(c p) d -> p c d", p=P)).then_inc(s["w2_in"], 16)
            sp.wait_ge(s["cleared"], 1)
            sp.dma_start(m.routed[DUMMY:DUMMY + P, :], zeros[:, :]).then_inc(s["pads"], 16)
            sp.wait_ge(s["pads_ready"], 1)
            for e in range(NE):
                row = sp.value_load(pad_i[0:1, e:e + 1], min_val=0, max_val=DUMMY - P)
                sp.dma_start(m.routed[bass.ds(row, P), :], zeros[:, :]).then_inc(s["pads"], 16)
            sp.wait_ge(s["pads"], 16 * (NE + 1))
            sp.wait_ge(s["params"], 16 * 6)
            sp.wait_ge(s["w2_in"], 16 * NE)

        @block.gpsimd
        def _(pool):
            for t in range(NT):
                if t % TB == 0:
                    pool.wait_ge(s["rows_ready"], t // TB + 1)
                pool.wait_ge(s["z_kept"], t + 1)
                for r in range(2):
                    nc.gpsimd.indirect_dma_start(m.routed, bass.IndirectOffsetOnAxis(ap=row_i[:, t, r:r + 1], axis=0),
                                                 m.Z[:, t, :], None).then_inc(s["scattered"], 16)
            pool.wait_ge(s["scattered"], 32 * NT)

        @block.scalar
        def _(act):
            A = nc.scalar

            def take_root(i):
                act.wait_ge(s["var_ready"], i + 2)
                A.activation(root[:, :], mv[:, :, 1], ACT.Sqrt, bias=eps[:, :]).then_inc(s["rooted"], 1)

            def normalise(i, k):
                t = i * TB + k
                wait(act, s["zT_psum"], t - last_use(k, 3, TB) + 1)
                wait(act, s["z_kept"], t - last_use(k, 3, TB) + 1)
                A.activation(zs[:, k % 3:k % 3 + 1, :], m.Y[:, bass.ds(t, 1), :], ACT.Identity, bias=shift_x[:, bass.ds(t, 1)],
                             scale=rstd[:, bass.ds(t, 1)]).then_inc(s["z_ready"], 1)
                act.wait_ge(s["z_ready"], t + 1)
                A.copy(m.Z[:, bass.ds(t, 1), :], zs[:, k % 3:k % 3 + 1, :]).then_inc(s["z_kept"], 1)

            def copy_t(i, k):
                t = i * TB + k
                act.wait_ge(s["zT_psum"], t + 1)
                wait(act, s["logit_psum"], t - last_use(k, 2, TB) + 1)
                A.copy(zT[:, k % 2, :], b_t[k % 2][:, 0:D]).then_inc(s["zT_ready"], 1)

            def body(i):
                act.wait_ge(s["norm_ready"], i + 1)
                for k in range(TB):
                    normalise(i, k)
                    if before := earlier(i, k, 1):
                        copy_t(*before)
                    if k == 1 and not (isinstance(i, int) and i == TI - 1):
                        take_root(i + 1)

            take_root(0)
            body(0)
            with act.Fori(1, TI - 1) as i:
                body(i)
            body(TI - 1)
            copy_t(TI - 1, TB - 1)
            act.wait_ge(s["b1_psum"], 1)
            A.copy(m.b1_cols[:, :], b_b[:, 0:NE * FC]).then_inc(s["z_kept"], 1)
            act.wait_ge(s["gap_ready"], 1)
            A.activation(ex2[:, :], m.share[:, :, 1], ACT.Exp).then_inc(s["gap_exp"], 1)

        @block.tensor
        def _(pe):
            T = nc.tensor
            pe.wait_ge(s["params"], 16 * 6)
            T.transpose(b_b[:, 0:NE * FC], b1_rows[0:NE * FC, :], m.ident[0:NE * FC, 0:NE * FC]).then_inc(s["b1_psum"], 1)

            def turn(i, k):
                t = i * TB + k
                pe.wait_ge(s["z_ready"], t + 1)
                wait(pe, s["zT_ready"], t - last_use(k, 2, TB) + 1)
                for c in range(DC):
                    last = T.transpose(b_t[k % 2][:, c * P:(c + 1) * P], zs[:, k % 3, c * P:(c + 1) * P], m.ident)
                last.then_inc(s["zT_psum"], 1)

            def logits(i, k):
                t = i * TB + k
                pe.wait_ge(s["zT_ready"], t + 1)
                if k == 0:
                    wait(pe, s["logit_read"], i)
                for c in range(DC):
                    last = T.matmul(b_l[:, k * NE:(k + 1) * NE], zT[:, k % 2, c * P:(c + 1) * P], gate[:, c, :],
                                    start=(c == 0), stop=(c == DC - 1))
                last.then_inc(s["logit_psum"], 1)

            def rank(i):
                pe.wait_ge(s["both_ready"], i + 1)
                pe.wait_ge(s["seen_ready"], i + 1)
                T.matmul(b_r[:, 0:TB * NE], tri_h[:, :], both[:, :, :], start=True, stop=False)
                for k in range(TB - 1):
                    T.matmul(b_r[:, (k + 1) * NE:TB * NE], ones_h[:, :], both[:, k:k + 1, :].to_broadcast([P, TB - 1 - k, NE]),
                             start=False, stop=False)
                T.matmul(b_r[:, 0:TB * NE], ones_h[:, :], seen[:, :].unsqueeze(1).to_broadcast([P, TB, NE]), start=False,
                         stop=True).then_inc(s["rank_psum"], 1)

            def body(i):
                for k in range(TB):
                    turn(i, k)
                    if k:
                        logits(i, k - 1)
                    if k == 3 and not (isinstance(i, int) and i == 0):
                        rank(i - 1)
                logits(i, TB - 1)

            rounds(pe, TI, body)
            rank(TI - 1)
            pe.wait_ge(s["seen_ready"], TI + 1)
            T.matmul(b_n[:, 0:NE], ones_h[:, :], seen[:, :], start=True, stop=True).then_inc(s["counts"], 1)

        @block.vector
        def _(dve):
            V = nc.vector
            c = Chain(dve, s["link"])
            V.memset(zeros[:, :], 0.0).then_inc(s["cleared"], 1)
            V.memset(eps[:, :], EPS).then_inc(s["var_ready"], 1)
            V.tensor_copy(tri_h[:, :], m.tri)
            V.tensor_copy(ones_h[:, :], m.ones)
            V.memset(seen[:, :], 0.0).then_inc(s["seen_ready"], 1)

            def variances(i):
                for k in range(TB):
                    last = V.bn_stats(st6[:, k, :], m.Y[:, bass.ds(i * TB + k, 1), :].rearrange("p a d -> p (a d)"))
                c.link(last, apart=True)
                for k in range(TB):
                    last = V.bn_aggr(mv[:, k, :], st6[:, k, :])
                last.then_inc(s["var_ready"], 1)

            def factors(i):
                dve.wait_ge(s["rooted"], i + 1)
                c.link(V.reciprocal(root[:, :], root[:, :]))
                V.tensor_copy(rstd[:, bass.ds(i * TB, TB)], root[:, :])
                V.scalar_tensor_tensor(shift_x[:, bass.ds(i * TB, TB)], mv[:, :, 0], -1.0, root[:, :], ALU.mult,
                                       ALU.mult).then_inc(s["norm_ready"], 1)

            variances(0)
            factors(0)
            variances(1)
            factors(1)
            dve.wait_ge(s["params"], 16 * 6)

            def choose(i):
                at = bass.ds(i * TB, TB)
                dve.wait_ge(s["logit_psum"], i * TB + TB)
                V.tensor_tensor(logit[:, :, :], b_l[:, 0:TB * NE].rearrange("p (t e) -> p t e", e=NE),
                                gate_b[:, :].unsqueeze(1).to_broadcast([P, TB, NE]), ALU.add).then_inc(s["logit_read"], 1)
                dve.wait_ge(s["logit_read"], i + 1)
                dve.nop(nofuse=True)
                for k in range(TB):
                    last = V.max(top[:, k, :], logit[:, k, :])
                c.link(last, apart=True)
                for k in range(TB):
                    last = V.max_index(top_at[:, k, :], top[:, k, :], logit[:, k, :])
                c.link(last)
                V.tensor_scalar(m.share[:, at, :], top[:, :, 0:2], 1.0, None, ALU.mult)
                c.link(V.tensor_copy(top_f[:, :, :], top_at[:, :, 0:2]))
                pair = chosen[:, at, :, :]
                c.link(V.tensor_tensor(pair, m.iota[:, 0:NE].unsqueeze(1).unsqueeze(1).to_broadcast([P, TB, 2, NE]),
                                       top_f[:, :, :].unsqueeze(3).to_broadcast([P, TB, 2, NE]), ALU.is_equal))
                flat = pair.rearrange("p t r e -> p t (r e)")
                c.link(V.tensor_tensor(flat, flat, m.C[:, bass.ds(i * TB + K_VAL, TB)].unsqueeze(2).to_broadcast([P, TB, 2 * NE]),
                                       ALU.mult))
                V.tensor_tensor(both[:, :, :], pair[:, :, 0, :], pair[:, :, 1, :], ALU.add).then_inc(s["both_ready"], 1)

            def place(i):
                at = bass.ds(i * TB, TB)
                dve.wait_ge(s["rank_psum"], i + 1)
                dve.wait_ge(s["both_ready"], i + 1)
                c.link(V.tensor_reduce(new[:, :], both[:, :, :].rearrange("p t e -> p e t"), AX_X, ALU.add))
                c.link(V.tensor_tensor(pos[:, :, :], b_r[:, 0:TB * NE].rearrange("p (t e) -> p t e", e=NE),
                                       m.C[:, K_CAP:K_CAP + NE].unsqueeze(1).to_broadcast([P, TB, NE]), ALU.add))
                V.tensor_tensor(seen[:, :], seen[:, :], new[:, :], ALU.add).then_inc(s["seen_ready"], 1)
                c.link(V.tensor_tensor(pick[:, :, :, :], chosen[:, at, :, :],
                                       pos[:, :, :].unsqueeze(2).to_broadcast([P, TB, 2, NE]), ALU.mult))
                row = m.row_f[:, at, :]
                c.link(V.tensor_reduce(row, pick[:, :, :, :], AX_X, ALU.add))
                V.tensor_tensor(row_i[:, at, :], row,
                                m.C[:, bass.ds(i * 2 * TB + K_TR, 2 * TB)].rearrange("p (t r) -> p t r", r=2),
                                ALU.add).then_inc(s["rows_ready"], 1)

            def body(i):
                more = not (isinstance(i, int) and i >= TI - 2)
                if more:
                    variances(i + 2)
                choose(i)
                if more:
                    factors(i + 2)
                place(i)

            body(0)
            c.loop(1, TI - 2, 11, body)
            body(TI - 2)
            body(TI - 1)

            dve.wait_ge(s["counts"], 1)
            c.link(V.tensor_tensor(n_f[:, :], b_n[:, 0:NE], m.C[:, K_CAP:K_CAP + NE], ALU.add))
            V.tensor_copy(pad_i[:, :], n_f[:, :]).then_inc(s["pads_ready"], 1)
            c.link(V.tensor_scalar(n_i[:, :], b_n[:, 0:NE], float(P - 1), None, ALU.add))
            c.link(V.tensor_scalar(n_j[:, :], n_i[:, :], 7, None, ALU.logical_shift_right))
            c.link(V.tensor_copy(tiles[:, :], n_j[:, :]))
            c.link(V.tensor_tensor_scan(tile_end[:, :], tiles[:, :], tiles[:, :], 0.0, ALU.add, ALU.max))
            c.link(V.tensor_tensor(shift[:, :], tile_end[:, :], tiles[:, :], ALU.subtract))
            c.link(V.scalar_tensor_tensor(shift[:, :], shift[:, :], -float(P), m.C[:, K_CAP:K_CAP + NE], ALU.mult, ALU.add))
            o = slice(0, 1)
            tile_no = m.iota[o, 0:MT]
            c.link(V.tensor_tensor(over[o, :, :], tile_end[o, :].unsqueeze(1).to_broadcast([1, MT, NE]),
                                   tile_no.unsqueeze(2).to_broadcast([1, MT, NE]), ALU.is_le))
            c.link(V.tensor_reduce(ex_f[o, :], over[o, :, :], AX_X, ALU.add))
            c.link(V.tensor_scalar(valid[o, :], ex_f[o, :], float(NE), None, ALU.is_lt))
            c.link(V.tensor_scalar(ex_f[o, :], ex_f[o, :], float(NE - 1), None, ALU.min))
            c.link(V.tensor_copy(m.expert_i[o, :], ex_f[o, :]))
            c.link(V.tensor_tensor(over[o, :, :], ex_f[o, :].unsqueeze(2).to_broadcast([1, MT, NE]),
                                   m.iota[o, 0:NE].unsqueeze(1).to_broadcast([1, MT, NE]), ALU.is_equal))
            c.link(V.tensor_tensor(over[o, :, :], over[o, :, :], shift[o, :].unsqueeze(1).to_broadcast([1, MT, NE]), ALU.mult))
            c.link(V.tensor_reduce(row_f[o, :], over[o, :, :], AX_X, ALU.add))
            c.link(V.scalar_tensor_tensor(row_f[o, :], tile_no, float(P), row_f[o, :], ALU.mult, ALU.add))
            c.link(V.scalar_tensor_tensor(row_f[o, :], row_f[o, :], float(DUMMY), valid[o, :], ALU.subtract, ALU.mult))
            c.link(V.tensor_scalar(m.tile_row_i[o, :], row_f[o, :], float(DUMMY), None, ALU.add))
            c.link(V.tensor_tensor(picked2,
                                   chosen[:, :, :, :].rearrange("p t r e -> p (t r) e"),
                                   shift[:, :].unsqueeze(1).to_broadcast([P, 2 * NT, NE]), ALU.mult))
            c.link(V.tensor_reduce(fid[:, :, :].rearrange("p t r -> p (t r)"),
                                   picked2, AX_X, ALU.add))
            c.link(V.tensor_tensor(fid[:, :, :], m.row_f[:, :, :], fid[:, :, :], ALU.subtract))
            c.link(V.tensor_tensor(m.fetch_i[:, :, :], fid[:, :, :],
                                   m.C[:, K_VAL:K_VAL + NT].unsqueeze(2).to_broadcast([P, NT, 2]), ALU.mult))
            V.tensor_tensor(m.share[:, :, 1], m.share[:, :, 1], m.share[:, :, 0], ALU.subtract).then_inc(s["gap_ready"], 1)
            dve.wait_ge(s["gap_exp"], 1)
            c.link(V.tensor_scalar(m.share[:, :, 0], ex2[:, :], 1.0, None, ALU.add))
            c.link(V.reciprocal(m.share[:, :, 0], m.share[:, :, 0]))
            c.link(V.tensor_tensor(m.share[:, :, 1], ex2[:, :], m.share[:, :, 0], ALU.mult))
            c.link(V.tensor_tensor(chosen[:, :, :, :], chosen[:, :, :, :],
                                   m.share[:, :, :].unsqueeze(3).to_broadcast([P, NT, 2, NE]), ALU.mult))
            c.link(V.tensor_tensor(m.mix[:, :, :], chosen[:, :, 0, :], chosen[:, :, 1, :], ALU.add))


def expert_stage(nc, m):
    UN = 4
    with ExitStack() as ctx:
        ph = Phase(nc, ctx, "expert")
        z, zT, hT, y = ph.sb("tile_z", [2, D]), ph.sb("tile_zT", [2, D]), ph.sb("tile_hT", [2, FF]), ph.sb("tile_y", [2, D])
        w1_now = ph.sb("w1_now", [2, DC, FF])
        names = "zT_psum zT_ready w1_staged hT_psum hT_ready y_psum y_ready beta_added"
        s = {n: ph.sem(n) for n in names.split()}
        loaded, stored = ph.sems("z_loaded", 2), ph.sems("y_stored", 2)
        b_zT, b_hT, b_y = m.bank[0:2], m.bank[4:6], m.bank[6:8]
        block = ctx.enter_context(nc.Block())
        turns = MT // UN

        def step(body):
            def run(eng):
                for k in range(UN):
                    body(0, k)
                with eng.Fori(1, turns - 1) as i:
                    for k in range(UN):
                        body(i, k)
                for k in range(UN):
                    body(turns - 1, k)
            return run

        def following(i, k, lead):
            if k + lead < UN:
                return i, k + lead
            return None if isinstance(i, int) and i == turns - 1 else (i + 1, k + lead - UN)

        @block.sync
        def _(sp):
            def load(i, k):
                j = i * UN + k
                row = sp.value_load(m.tile_row_i[0:1, bass.ds(j, 1)], min_val=0, max_val=DUMMY)
                wait(sp, s["zT_psum"], j - 1)
                sp.dma_start(z[:, k % 2, :], m.routed[bass.ds(row, P), :]).then_inc(loaded[k % 2], 16)

            step(load)(sp)

        @block.scalar
        def _(act):
            def stage_w1(i, k):
                j = i * UN + k
                expert = act.value_load(m.expert_i[0:1, bass.ds(j, 1)], min_val=0, max_val=NE - 1)
                wait(act, s["hT_psum"], j - 1)
                nc.scalar.copy(w1_now[:, k % 2:k % 2 + 1, :, :].rearrange("p a c f -> p a (c f)"),
                               m.w1_sb[:, bass.ds(expert, 1), :, :].rearrange("p a c f -> p a (c f)")).then_inc(s["w1_staged"], 1)

            stage_w1(0, 0)
            stage_w1(0, 1)

            def relu(i, k):
                j = i * UN + k
                expert = act.value_load(m.expert_i[0:1, bass.ds(j, 1)], min_val=0, max_val=NE - 1)
                act.wait_ge(s["hT_psum"], j + 1)
                wait(act, s["y_psum"], j - 1)
                for f in range(FC):
                    last = nc.scalar.activation(hT[:, k % 2, f * P:(f + 1) * P], b_hT[k % 2][:, f * P:(f + 1) * P],
                                                ACT.Relu, bias=m.b1_cols[:, bass.ds(expert * FC + f, 1)])
                last.then_inc(s["hT_ready"], 1)

            def store(i, k):
                j = i * UN + k
                act.wait_ge(s["y_ready"], j + 1)
                act.dma_start(m.expert_out[bass.ds(j * P, P), :], y[:, k % 2, :]).then_inc(stored[k % 2], 16)

            def body(i, k):
                relu(i, k)
                if k:
                    store(i, k - 1)
                elif not (isinstance(i, int) and i == 0):
                    store(i - 1, UN - 1)
                if after := following(i, k, 2):
                    stage_w1(*after)

            step(body)(act)
            store(turns - 1, UN - 1)
            for k in range(2):
                act.wait_ge(stored[k], 16 * MT // 2)

        @block.gpsimd
        def _(pool):
            nc.gpsimd.tensor_tensor(m.Y[:, :, :], m.Y[:, :, :], m.beta_b[:, :].unsqueeze(1).to_broadcast([P, NT, D]),
                                    ALU.add).then_inc(s["beta_added"], 1)
            pool.wait_ge(s["beta_added"], 1)

        @block.tensor
        def _(pe):
            T = nc.tensor

            def turn(i, k):
                j = i * UN + k
                b = k % 2
                pe.wait_ge(loaded[b], (i * (UN // 2) + k // 2) * 16 + 16)
                wait(pe, s["zT_ready"], j - 1)
                for c in range(DC):
                    last = T.transpose(b_zT[b][:, c * P:(c + 1) * P], z[:, b, c * P:(c + 1) * P], m.ident)
                last.then_inc(s["zT_psum"], 1)

            def hidden(i, k):
                j = i * UN + k
                b = k % 2
                pe.wait_ge(s["zT_ready"], j + 1)
                pe.wait_ge(s["w1_staged"], j + 1)
                wait(pe, s["hT_ready"], j - 1)
                for f in range(FC):
                    for c in range(DC):
                        last = T.matmul(b_hT[b][:, f * P:(f + 1) * P], w1_now[:, b, c, f * P:(f + 1) * P],
                                        zT[:, b, c * P:(c + 1) * P], start=(c == 0), stop=(c == DC - 1))
                last.then_inc(s["hT_psum"], 1)

            def body(i, k):
                j = i * UN + k
                b = k % 2
                if after := following(i, k, 1):
                    hidden(*after)
                if after := following(i, k, 2):
                    turn(*after)
                expert = pe.value_load(m.expert_i[0:1, bass.ds(j, 1)], min_val=0, max_val=NE - 1)
                pe.wait_ge(s["hT_ready"], j + 1)
                wait(pe, s["y_ready"], j - 1)
                for f in range(FC):
                    last = T.matmul(b_y[b][:, 0:D], hT[:, b, f * P:(f + 1) * P],
                                    m.w2_sb[:, bass.ds(expert, 1), f, :].rearrange("p a f -> p (a f)"),
                                    start=(f == 0), stop=(f == FC - 1))
                last.then_inc(s["y_psum"], 1)

            turn(0, 0)
            turn(0, 1)
            hidden(0, 0)
            step(body)(pe)

        @block.vector
        def _(dve):
            V = nc.vector

            def enter(i, k):
                j = i * UN + k
                b = k % 2
                dve.wait_ge(s["zT_psum"], j + 1)
                wait(dve, s["hT_psum"], j - 1)
                V.tensor_copy(zT[:, b, :], b_zT[b][:, 0:D]).then_inc(s["zT_ready"], 1)

            def body(i, k):
                j = i * UN + k
                if after := following(i, k, 2):
                    enter(*after)
                dve.wait_ge(s["y_psum"], j + 1)
                wait(dve, stored[k % 2], (i * (UN // 2) + k // 2) * 16)
                V.tensor_copy(y[:, k % 2, :], b_y[k % 2][:, 0:D]).then_inc(s["y_ready"], 1)

            enter(0, 0)
            enter(0, 1)
            step(body)(dve)


def combine_stage(nc, m):
    with ExitStack() as ctx:
        ph = Phase(nc, ctx, "combine")
        a = Arena(m.W1, NE * DC * FF)
        got, y, o = a.cut([TB, 2, D]), a.cut([TB, D]), a.cut([TB, D])
        mix_now, mixT, diagonal = a.cut([2, NE]), a.cut([2, P]), a.cut([2, 2 * P])
        st6, mv, root, eps = ph.sb("cb_stats", [TB, 6]), ph.sb("cb_mean_var", [TB, 2]), ph.sb("cb_root", [TB, 1]), ph.sb("cb_eps", [1])
        s = {n: ph.sem(n) for n in "link eps_ready var_ready rooted centred result tail_out mix_staged mixT_psum mixT_ready diagonal_ready sum_psum".split()}
        landed, stored = ph.sems("landed", TB), ph.sems("stored", TB)
        b_mT, b_sum = m.bank[0:2], m.bank[3:8]
        block = ctx.enter_context(nc.Block())

        @block.sync
        def _(sp):
            def store(i, k):
                t = i * TB + k
                sp.wait_ge(s["result"], t + 1)
                sp.dma_start(m.out[bass.ds(t * P, P), :], o[:, k, :]).then_inc(stored[k], 16)

            for k in range(TB):
                store(0, k)
            with sp.Fori(1, TI - 1) as i:
                for k in range(TB):
                    store(i, k)
            for k in range(TB - 1):
                store(TI - 1, k)
            sp.wait_ge(s["result"], NT)
            sp.dma_start(m.out[N - TAIL:N, :], o[0:TAIL, TB - 1, :]).then_inc(s["tail_out"], 16)
            for k in range(TB):
                sp.wait_ge(stored[k], 16 * (TI - (k == TB - 1)))
            sp.wait_ge(s["tail_out"], 16)

        @block.gpsimd
        def _(pool):
            for t in range(NT):
                k = t % TB
                wait(pool, s["sum_psum"], t - TB + 1)
                for r in range(2):
                    nc.gpsimd.indirect_dma_start(got[:, k, r, :], None, m.expert_out,
                                                 bass.IndirectOffsetOnAxis(ap=m.fetch_i[:, t, r:r + 1], axis=0)).then_inc(landed[k], 16)

        @block.scalar
        def _(act):
            A = nc.scalar

            def stage_mix(i, k):
                t = i * TB + k
                wait(act, s["mixT_psum"], t - last_use(k, 2, TB) + 1)
                A.copy(mix_now[:, k % 2:k % 2 + 1, :], m.mix[:, bass.ds(t, 1), :]).then_inc(s["mix_staged"], 1)

            def copy_mix(i, k):
                t = i * TB + k
                act.wait_ge(s["mixT_psum"], t + 1)
                wait(act, s["sum_psum"], t - last_use(k, 2, TB) + 1)
                A.copy(mixT[0:NE, k % 2, :], b_mT[k % 2][0:NE, 0:P]).then_inc(s["mixT_ready"], 1)
                for r in range(2):
                    last = A.activation(diagonal[:, k % 2, r * P:(r + 1) * P], m.ident, ACT.Copy,
                                        scale=m.share[:, bass.ds(t, 1), r:r + 1].rearrange("p a b -> p (a b)"))
                last.then_inc(s["diagonal_ready"], 1)

            def take_root(i, k):
                act.wait_ge(s["var_ready"], i * TB + k + 1)
                A.activation(root[:, k, :], mv[:, k, 1:2], ACT.Sqrt, bias=eps[:, :]).then_inc(s["rooted"], 1)

            def body(i):
                for k in range(TB):
                    stage_mix(i, k)
                    if before := earlier(i, k, 1):
                        copy_mix(*before)
                    if before := earlier(i, k, 3):
                        take_root(*before)

            act.wait_ge(s["eps_ready"], 1)
            rounds(act, TI, body)
            copy_mix(TI - 1, TB - 1)
            for k in range(TB - 3, TB):
                take_root(TI - 1, k)

        @block.tensor
        def _(pe):
            T = nc.tensor

            def turn_mix(i, k):
                t = i * TB + k
                pe.wait_ge(s["mix_staged"], t + 1)
                wait(pe, s["mixT_ready"], t - last_use(k, 2, TB) + 1)
                T.transpose(b_mT[k % 2][0:NE, 0:P], mix_now[:, k % 2, :], m.ident).then_inc(s["mixT_psum"], 1)

            def add_up(i, k):
                t = i * TB + k
                pe.wait_ge(s["mixT_ready"], t + 1)
                wait(pe, s["centred"], t - TB + 1)
                T.matmul(b_sum[k][:, 0:D], m.ident, m.Z[:, bass.ds(t, 1), :].rearrange("p a d -> p (a d)"), start=True, stop=False)
                T.matmul(b_sum[k][:, 0:D], mixT[0:NE, k % 2, :], m.b2_rows[0:NE, :], start=False, stop=False)
                pe.wait_ge(s["diagonal_ready"], t + 1)
                pe.wait_ge(landed[k], i * 32 + 32)
                for r in range(2):
                    last = T.matmul(b_sum[k][:, 0:D], diagonal[:, k % 2, r * P:(r + 1) * P], got[:, k, r, :], start=False, stop=(r == 1))
                last.then_inc(s["sum_psum"], 1)

            def body(i):
                for k in range(TB):
                    turn_mix(i, k)
                    if before := earlier(i, k, 1):
                        add_up(*before)

            rounds(pe, TI, body)
            add_up(TI - 1, TB - 1)

        @block.vector
        def _(dve):
            V = nc.vector
            c = Chain(dve, s["link"])
            V.memset(eps[:, :], EPS).then_inc(s["eps_ready"], 1)

            def stats(i, k):
                dve.wait_ge(s["sum_psum"], i * TB + k + 1)
                c.link(V.bn_stats(st6[:, k, :], b_sum[k][:, 0:D]), apart=True)
                V.bn_aggr(mv[:, k, :], st6[:, k, :]).then_inc(s["var_ready"], 1)

            def finish(i, k):
                t = i * TB + k
                dve.wait_ge(s["rooted"], t + 1)
                c.link(V.reciprocal(root[:, k, :], root[:, k, :]))
                V.scalar_tensor_tensor(y[:, k, :], b_sum[k][:, 0:D], mv[:, k, 0:1], m.gamma_b[:, :], ALU.subtract,
                                       ALU.mult).then_inc(s["centred"], 1)
                dve.wait_ge(s["centred"], t + 1)
                wait(dve, stored[k], i * 16)
                V.scalar_tensor_tensor(o[:, k:k + 1, :], y[:, k:k + 1, :], root[:, k, :], m.Y[:, bass.ds(t, 1), :],
                                       ALU.mult, ALU.add).then_inc(s["result"], 1)

            def body(i):
                for k in range(TB):
                    stats(i, k)
                    if before := earlier(i, k, 3):
                        finish(*before)

            c.rounds(TI, 2 * TB, body)
            for k in range(TB - 3, TB):
                finish(TI - 1, k)


class Memory:
    pass


def build(nc, x, src, dst, ew, wl, bl, wr, br, wq, wk, wv, wo, bo, kg, kb, vg, vb,
          gate_w, gate_b, w1, b1, w2, b2, gamma, beta, consts, out):
    m = Memory()
    m.x, m.src, m.dst, m.ew, m.consts, m.out = x, src, dst, ew, consts, out
    m.wl, m.bl, m.wr, m.br = wl, bl, wr, br
    m.wq, m.wk, m.wv, m.wo, m.bo = wq, wk, wv, wo, bo
    m.kg, m.kb, m.vg, m.vb = kg, kb, vg, vb
    m.gate_w, m.gate_b, m.w1, m.b1, m.w2, m.b2, m.gamma, m.beta = gate_w, gate_b, w1, b1, w2, b2, gamma, beta
    m.h_table = nc.dram_tensor("h_table", (NT * P, D), F32, kind="Internal").ap()
    m.routed = nc.dram_tensor("routed_z", (ZROWS, D), F32, kind="Internal").ap()
    m.expert_out = nc.dram_tensor("expert_out", (MT * P, D), F32, kind="Internal").ap()
    with ExitStack() as ctx:
        ph = Phase(nc, ctx, "whole")
        m.bank = [ctx.enter_context(nc.psum_tensor(f"bank{i}", [P, 512], F32)) for i in range(8)]
        m.C = ph.sb("constants", [K_END])
        m.ident, m.tri, m.ones = m.C[:, K_ID:K_ID + P], m.C[:, K_TRI:K_TRI + P], m.C[:, K_ONE:K_ONE + P]
        m.center, m.mask, m.iota = m.C[:, K_CEN:K_CEN + P], m.C[:, K_MSK:K_MSK + P], m.C[:, K_IOTA:K_IOTA + 256]
        m.Y = ph.sb("nodes", [NT, D])
        m.W1 = ph.sb("w1_all", [NE * DC * FF])
        m.W2 = ph.sb("w2_all", [NE * FC * D])
        m.w1_sb = m.W1[:, :].rearrange("p (e c f) -> p e c f", e=NE, c=DC)
        m.w2_sb = m.W2[:, :].rearrange("p (e c d) -> p e c d", e=NE, c=FC)
        a = Arena(m.W2, NE * FC * D)
        m.xnT = a.cut([NT, D])
        m.xnT_words = a.at
        a = Arena(m.W1, NE * DC * FF)
        m.wq_sb, m.wk_sb, m.wv_sb, m.wo_sb, m.wr_sb = (a.cut([DC, D]) for _ in range(5))
        m.kg_sb, m.kb_sb, m.vg_sb, m.vb_sb = a.cut([HEAD]), a.cut([HEAD]), a.cut([1]), a.cut([1])
        m.biases = a.cut([3, D])
        m.wkv, m.woT = a.cut([DC, 2 * D]), a.cut([DC, D])
        m.small_words = a.at
        m.w_loaded, m.w_total = ph.sem("small_weights"), 16 * 14
        with ExitStack() as edge_ctx:
            edges = Phase(nc, edge_ctx, "edges")
            m.row_of, m.col_of = edges.sb("edge_slot_row", [EC], BF16), edges.sb("edge_slot_col", [EC], BF16)
            m.code_h, m.top_h = edges.sb("edge_code", [3, EC], FP16), edges.sb("edge_weight_top", [EC], BF16)
            m.bucket_i = edges.sb("column_bucket", [SUP, NI, GBP], I32)
            m.zero_h = edges.sb("zero_bf16", [512], BF16)
            m.iota_t = edges.sb("iota_batch", [NC, HB], BF16)
            prepare_stage(nc, m)
            edge_stage(nc, m)
        late = Phase(nc, ctx, "late")
        m.Z = late.sb("normed_nodes", [NT, D])
        m.mix, m.share = late.sb("expert_shares", [NT, NE]), late.sb("share", [NT, 2])
        m.row_f, m.fetch_i = late.sb("routed_row", [NT, 2]), late.sb("fetch_row", [NT, 2], I32)
        m.expert_i, m.tile_row_i = late.sb("tile_expert", [MT], I32), late.sb("tile_row", [MT], I32)
        m.b1_cols, m.b2_rows = late.sb("b1_columns", [NE * FC]), late.sb("b2_rows", [D])
        m.gamma_b, m.beta_b = late.sb("gamma", [D]), late.sb("beta", [D])
        route_stage(nc, m)
        expert_stage(nc, m)
        combine_stage(nc, m)


_INS = ["x", "src", "dst", "edge_weight", "L0_gnn_weight_l", "L0_gnn_bias_l", "L0_gnn_weight_r", "L0_gnn_bias_r",
        "L0_mix_wq", "L0_mix_wk", "L0_mix_wv", "L0_mix_wo", "L0_mix_bo", "L0_mix_ln_k_g", "L0_mix_ln_k_b",
        "L0_mix_ln_v_g", "L0_mix_ln_v_b", "L0_ffn_gate_w", "L0_ffn_gate_b", "L0_ffn_w1", "L0_ffn_b1", "L0_ffn_w2",
        "L0_ffn_b2", "L0_ffn_gamma", "L0_ffn_beta"]


def kernel(**inputs):
    import concourse.bacc as _bacc
    from concourse.bass_utils import run_bass_kernel_spmd as _run

    nc = _bacc.Bacc("TRN2", target_bir_lowering=False, num_devices=1)
    arrays, args = {}, []
    feed = [(name, np.ascontiguousarray(inputs[name])) for name in _INS] + [("consts", constant_table())]
    for name, a in feed:
        arrays[f"in_{name}_dram"] = a
        args.append(nc.dram_tensor(f"in_{name}_dram", a.shape, mybir.dt.from_np(a.dtype), kind="ExternalInput").ap())
    args.append(nc.dram_tensor("out_0_dram", (N, D), F32, kind="ExternalOutput").ap())
    build(nc, *args)
    r = _run(nc, [arrays], core_ids=[0])
    return r.results[0]["out_0_dram"]
```
